# Optimizing a Trainium2 kernel written in Bass

```python
import numpy as np
import jax
import jax.numpy as jnp

def _softmax(x, axis=-1):
    return jax.nn.softmax(x, axis=axis)

def _gelu(x):
    return jax.nn.gelu(x, approximate=True)

def _silu(x):
    return jax.nn.silu(x)

def _sigmoid(x):
    return jax.nn.sigmoid(x)

def _layernorm(x, axis=-1, eps=1e-05):
    m = jnp.mean(x, axis=axis, keepdims=True)
    v = jnp.var(x, axis=axis, keepdims=True)
    return (x - m) / jnp.sqrt(v + eps)

def _scatter_add(tgt, idx, src, axis=0):
    return tgt.at[idx].add(src)

def _segment_sum(src, seg, n):
    return jax.ops.segment_sum(src, seg, n)
kernel_name = 'mk_adj_ffn_d2_adj_r2_0f39eb'

def setup_inputs(seed: int=0):
    np.random.seed(seed)
    _w = jnp.asarray

    def _rec_inputs():
        import jax
        import jax.numpy as jnp
        _gk = jax.random.key(seed)
        x = -0.0002928 + 1 * jax.random.normal(jax.random.fold_in(_gk, 1), (64, 128, 128), jnp.float32)
        _a = jax.random.bernoulli(jax.random.fold_in(_gk, 2), 0.03125, (64, 128, 128))
        _a = jnp.logical_or(_a, jnp.swapaxes(_a, -1, -2))
        _a = jnp.logical_or(_a, jnp.eye(128, dtype=bool))
        adj = _a.astype(jnp.int32)
        return (x, adj)
    x, adj = _rec_inputs()

    def _L0_gnn_setup():
        import jax, jax.numpy as jnp
        import numpy as np
        ALPHA = 0.2
        NEG_INF = -9000000000000000.0
        key = jax.random.key(seed)
        k1, k2, k3, k4 = jax.random.split(key, 4)
        B, N, D = (8, 1024, 128)
        h = jax.random.normal(k1, (B, N, D), dtype=jnp.float32)
        adj = jax.random.randint(k2, (B, N, N), 0, 2, dtype=jnp.int32)
        W = jax.random.normal(k3, (D, D), dtype=jnp.float32) * (1.0 / np.sqrt(D))
        a = jax.random.normal(k4, (2 * D, 1), dtype=jnp.float32) * 0.05
        return {'h': h, 'adj': adj, 'W': W, 'a': a}
    _L0_gnn_all = _L0_gnn_setup()
    _L0_gnn_in = {k: v for k, v in _L0_gnn_all.items() if k in ('W', 'a')}
    del _L0_gnn_all

    def _L0_ffn_setup():
        import jax, jax.numpy as jnp
        import numpy as np
        C = 128
        HID = 512
        E = 8
        TEMP = 1.0
        key = jax.random.key(seed)
        ks = jax.random.split(key, 7)
        x = jax.random.normal(ks[0], (8, 8192, C), dtype=jnp.float32)
        W1 = jax.random.normal(ks[1], (C, HID), dtype=jnp.float32) * 0.02
        b1 = jnp.zeros((HID,), dtype=jnp.float32)
        Wg = jax.random.normal(ks[2], (HID, E), dtype=jnp.float32) * 0.02
        bg = jnp.zeros((E,), dtype=jnp.float32)
        Wd = jax.random.normal(ks[3], (E, HID, C), dtype=jnp.float32) * 0.02
        bd = jnp.zeros((E, C), dtype=jnp.float32)
        return {'x': x, 'W1': W1, 'b1': b1, 'Wg': Wg, 'bg': bg, 'Wd': Wd, 'bd': bd}
    _L0_ffn_all = _L0_ffn_setup()
    _L0_ffn_in = {k: v for k, v in _L0_ffn_all.items() if k in ('W1', 'b1', 'Wg', 'bg', 'Wd', 'bd')}
    del _L0_ffn_all

    def _L1_gnn_setup():
        import jax, jax.numpy as jnp
        import numpy as np
        B, S, D = (64, 256, 128)

        def _leaky(x):
            return jnp.where(x >= 0, x, 0.2 * x)
        key = jax.random.key(seed)
        k = jax.random.split(key, 6)
        stdv = 1.0 / np.sqrt(D)
        return {'hidden': jax.random.normal(k[0], (B, S, D), dtype=jnp.float32), 'adj': jax.random.randint(k[1], (B, S, S), 0, 5, dtype=jnp.int32), 'a0': jax.random.uniform(k[2], (D, 1), jnp.float32, -stdv, stdv), 'a1': jax.random.uniform(k[3], (D, 1), jnp.float32, -stdv, stdv), 'a2': jax.random.uniform(k[4], (D, 1), jnp.float32, -stdv, stdv), 'a3': jax.random.uniform(k[5], (D, 1), jnp.float32, -stdv, stdv), 'bias': jnp.zeros((D,), dtype=jnp.float32)}
    _L1_gnn_all = _L1_gnn_setup()
    _L1_gnn_in = {k: v for k, v in _L1_gnn_all.items() if k in ('a0', 'a1', 'a2', 'a3', 'bias')}
    del _L1_gnn_all

    def _L1_ffn_setup():
        import jax, jax.numpy as jnp
        import numpy as np
        D_MODEL = 128
        D_STATE = 64
        D_CONV = 4
        EXPAND = 2
        HEADDIM = 64
        D_INNER = EXPAND * D_MODEL
        NHEADS = D_INNER // HEADDIM
        CONV_DIM = D_INNER + 2 * D_STATE
        D_IN_PROJ = 2 * D_INNER + 2 * D_STATE + NHEADS
        CHUNK = 128
        EPS = 1e-05

        def segsum(a):
            T = a.shape[-1]
            cs = jnp.cumsum(a, axis=-1)
            ss = cs[..., :, None] - cs[..., None, :]
            mask = jnp.tril(jnp.ones((T, T), dtype=bool))
            return jnp.where(mask, ss, -jnp.inf)

        def mamba2_block(x, W_in, conv_w, conv_b, dt_bias, A_log, D, norm_w, W_out, W_lin, b_lin):
            Bsz, L, _ = x.shape
            zxbcdt = x @ W_in
            z, xBC, dt = jnp.split(zxbcdt, [D_INNER, D_INNER + CONV_DIM], axis=-1)
            xp = jnp.pad(xBC, ((0, 0), (D_CONV - 1, 0), (0, 0)))
            conv = conv_b + sum((xp[:, k:k + L, :] * conv_w[:, k] for k in range(D_CONV)))
            xBC = jax.nn.silu(conv)
            xh, Bmat, Cmat = jnp.split(xBC, [D_INNER, D_INNER + D_STATE], axis=-1)
            dt = jax.nn.softplus(dt + dt_bias)
            A = -jnp.exp(A_log)
            nc = L // CHUNK
            xh = xh.reshape(Bsz, nc, CHUNK, NHEADS, HEADDIM)
            Bc = Bmat.reshape(Bsz, nc, CHUNK, D_STATE)
            Cc = Cmat.reshape(Bsz, nc, CHUNK, D_STATE)
            dtc = dt.reshape(Bsz, nc, CHUNK, NHEADS)
            dA = jnp.einsum('bclh,h->bhcl', dtc, A)
            A_cum = jnp.cumsum(dA, axis=-1)
            Lmat = jnp.exp(segsum(dA))
            xdt = xh * dtc[..., None]
            Y_diag = jnp.einsum('bcln,bcsn,bhcls,bcshp->bclhp', Cc, Bc, Lmat, xdt)
            decay_states = jnp.exp(A_cum[..., -1:] - A_cum)
            states = jnp.einsum('bcln,bhcl,bclhp->bchpn', Bc, decay_states, xdt)
            chunk_decay = jnp.exp(A_cum[..., -1])

            def step(h, inp):
                s, d = inp
                return (h * d[..., None, None] + s, h)
            _, prevs = jax.lax.scan(step, jnp.zeros_like(states[:, 0]), (jnp.moveaxis(states, 1, 0), jnp.moveaxis(chunk_decay, 2, 0)))
            prevs = jnp.moveaxis(prevs, 0, 1)
            Y_off = jnp.einsum('bcln,bchpn,bhcl->bclhp', Cc, prevs, jnp.exp(A_cum))
            Y = (Y_diag + Y_off + xh * D[:, None]).reshape(Bsz, L, D_INNER)
            Y = Y * jax.nn.silu(z)
            Y = Y * jax.lax.rsqrt(jnp.mean(Y * Y, axis=-1, keepdims=True) + EPS) * norm_w
            out = Y @ W_out
            return out @ W_lin + b_lin
        key = jax.random.key(seed)
        ks = jax.random.split(key, 12)
        B, L = (8, 2048)

        def gauss(k, shape, scale):
            return jax.random.normal(k, shape, dtype=jnp.float32) * scale
        return {'x': gauss(ks[0], (B, L, D_MODEL), 1.0), 'W_in': gauss(ks[1], (D_MODEL, D_IN_PROJ), D_MODEL ** (-0.5)), 'conv_w': gauss(ks[2], (CONV_DIM, D_CONV), 0.3), 'conv_b': gauss(ks[3], (CONV_DIM,), 0.1), 'dt_bias': jax.random.uniform(ks[4], (NHEADS,), minval=-4.0, maxval=-1.0), 'A_log': jnp.log(jax.random.uniform(ks[5], (NHEADS,), minval=1.0, maxval=16.0)), 'D': jnp.ones((NHEADS,), jnp.float32), 'norm_w': jnp.ones((D_INNER,), jnp.float32), 'W_out': gauss(ks[6], (D_INNER, D_MODEL), D_INNER ** (-0.5)), 'W_lin': gauss(ks[7], (D_MODEL, D_MODEL), D_MODEL ** (-0.5)), 'b_lin': jnp.zeros((D_MODEL,), jnp.float32)}
    _L1_ffn_all = _L1_ffn_setup()
    _L1_ffn_in = {k: v for k, v in _L1_ffn_all.items() if k in ('W_in', 'conv_w', 'conv_b', 'dt_bias', 'A_log', 'D', 'norm_w', 'W_out', 'W_lin', 'b_lin')}
    del _L1_ffn_all
    return {'x': x, 'adj': adj, 'L0_gnn_W': _L0_gnn_in['W'], 'L0_gnn_a': _L0_gnn_in['a'], 'L0_ffn_W1': _L0_ffn_in['W1'], 'L0_ffn_b1': _L0_ffn_in['b1'], 'L0_ffn_Wg': _L0_ffn_in['Wg'], 'L0_ffn_bg': _L0_ffn_in['bg'], 'L0_ffn_Wd': _L0_ffn_in['Wd'], 'L0_ffn_bd': _L0_ffn_in['bd'], 'L1_gnn_a0': _L1_gnn_in['a0'], 'L1_gnn_a1': _L1_gnn_in['a1'], 'L1_gnn_a2': _L1_gnn_in['a2'], 'L1_gnn_a3': _L1_gnn_in['a3'], 'L1_gnn_bias': _L1_gnn_in['bias'], 'L1_ffn_W_in': _L1_ffn_in['W_in'], 'L1_ffn_conv_w': _L1_ffn_in['conv_w'], 'L1_ffn_conv_b': _L1_ffn_in['conv_b'], 'L1_ffn_dt_bias': _L1_ffn_in['dt_bias'], 'L1_ffn_A_log': _L1_ffn_in['A_log'], 'L1_ffn_D': _L1_ffn_in['D'], 'L1_ffn_norm_w': _L1_ffn_in['norm_w'], 'L1_ffn_W_out': _L1_ffn_in['W_out'], 'L1_ffn_W_lin': _L1_ffn_in['W_lin'], 'L1_ffn_b_lin': _L1_ffn_in['b_lin']}

def reference(x, adj, L0_gnn_W, L0_gnn_a, L0_ffn_W1, L0_ffn_b1, L0_ffn_Wg, L0_ffn_bg, L0_ffn_Wd, L0_ffn_bd, L1_gnn_a0, L1_gnn_a1, L1_gnn_a2, L1_gnn_a3, L1_gnn_bias, L1_ffn_W_in, L1_ffn_conv_w, L1_ffn_conv_b, L1_ffn_dt_bias, L1_ffn_A_log, L1_ffn_D, L1_ffn_norm_w, L1_ffn_W_out, L1_ffn_W_lin, L1_ffn_b_lin):
    import jax
    import jax.numpy as jnp

    def _L0_gnn_ref(h, adj, W, a):
        import jax, jax.numpy as jnp
        import numpy as np
        ALPHA = 0.2
        NEG_INF = -9000000000000000.0
        Wh = jnp.einsum('bnd,od->bno', h, W)
        D = Wh.shape[-1]
        a1, a2 = (a[:D, 0], a[D:, 0])
        s1 = Wh @ a1
        s2 = Wh @ a2
        e = jax.nn.leaky_relu(s1[:, :, None] + s2[:, None, :], negative_slope=ALPHA)
        e = jnp.where(adj > 0, e, NEG_INF)
        attention = jax.nn.softmax(e, axis=-1)
        h_prime = jnp.einsum('bij,bjd->bid', attention, Wh)
        return h_prime

    def _L0_ffn_ref(x, W1, b1, Wg, bg, Wd, bd):
        import jax, jax.numpy as jnp
        import numpy as np
        C = 128
        HID = 512
        E = 8
        TEMP = 1.0
        orig_shape = x.shape
        xf = x.reshape(-1, orig_shape[-1])
        H = jax.nn.gelu(xf @ W1 + b1, approximate=False)
        probs = jax.nn.softmax((H @ Wg + bg) / TEMP, axis=-1)
        assign = jnp.argmax(probs, axis=-1)
        out = jnp.zeros_like(xf)
        for e in range(Wd.shape[0]):
            y = H @ Wd[e] + bd[e]
            sel = (assign == e)[:, None]
            out = out + jnp.where(sel, probs[:, e:e + 1] * y, 0.0)
        return out.reshape(orig_shape)

    def _L1_gnn_ref(hidden, adj, a0, a1, a2, a3, bias):
        import jax, jax.numpy as jnp
        import numpy as np
        B, S, D = (64, 256, 128)

        def _leaky(x):
            return jnp.where(x >= 0, x, 0.2 * x)
        h = hidden

        def e_of(a):
            return _leaky(jnp.einsum('bid,bjd->bij', h * a[:, 0], h))
        e0, e1, e2, e3 = (e_of(a0), e_of(a1), e_of(a2), e_of(a3))
        neg_inf = jnp.float32(-jnp.finfo(e0.dtype).max)
        alpha = jnp.where(adj == 1, e0, neg_inf)
        alpha = jnp.where(adj == 2, e1, alpha)
        alpha = jnp.where(adj == 3, e2, alpha)
        alpha = jnp.where(adj == 4, e3, alpha)
        alpha = jax.nn.sigmoid(alpha)
        return jnp.einsum('bij,bjd->bid', alpha, h) + bias

    def _L1_ffn_ref(x, W_in, conv_w, conv_b, dt_bias, A_log, D, norm_w, W_out, W_lin, b_lin):
        import jax, jax.numpy as jnp
        import numpy as np
        D_MODEL = 128
        D_STATE = 64
        D_CONV = 4
        EXPAND = 2
        HEADDIM = 64
        D_INNER = EXPAND * D_MODEL
        NHEADS = D_INNER // HEADDIM
        CONV_DIM = D_INNER + 2 * D_STATE
        D_IN_PROJ = 2 * D_INNER + 2 * D_STATE + NHEADS
        CHUNK = 128
        EPS = 1e-05

        def segsum(a):
            T = a.shape[-1]
            cs = jnp.cumsum(a, axis=-1)
            ss = cs[..., :, None] - cs[..., None, :]
            mask = jnp.tril(jnp.ones((T, T), dtype=bool))
            return jnp.where(mask, ss, -jnp.inf)

        def mamba2_block(x, W_in, conv_w, conv_b, dt_bias, A_log, D, norm_w, W_out, W_lin, b_lin):
            Bsz, L, _ = x.shape
            zxbcdt = x @ W_in
            z, xBC, dt = jnp.split(zxbcdt, [D_INNER, D_INNER + CONV_DIM], axis=-1)
            xp = jnp.pad(xBC, ((0, 0), (D_CONV - 1, 0), (0, 0)))
            conv = conv_b + sum((xp[:, k:k + L, :] * conv_w[:, k] for k in range(D_CONV)))
            xBC = jax.nn.silu(conv)
            xh, Bmat, Cmat = jnp.split(xBC, [D_INNER, D_INNER + D_STATE], axis=-1)
            dt = jax.nn.softplus(dt + dt_bias)
            A = -jnp.exp(A_log)
            nc = L // CHUNK
            xh = xh.reshape(Bsz, nc, CHUNK, NHEADS, HEADDIM)
            Bc = Bmat.reshape(Bsz, nc, CHUNK, D_STATE)
            Cc = Cmat.reshape(Bsz, nc, CHUNK, D_STATE)
            dtc = dt.reshape(Bsz, nc, CHUNK, NHEADS)
            dA = jnp.einsum('bclh,h->bhcl', dtc, A)
            A_cum = jnp.cumsum(dA, axis=-1)
            Lmat = jnp.exp(segsum(dA))
            xdt = xh * dtc[..., None]
            Y_diag = jnp.einsum('bcln,bcsn,bhcls,bcshp->bclhp', Cc, Bc, Lmat, xdt)
            decay_states = jnp.exp(A_cum[..., -1:] - A_cum)
            states = jnp.einsum('bcln,bhcl,bclhp->bchpn', Bc, decay_states, xdt)
            chunk_decay = jnp.exp(A_cum[..., -1])

            def step(h, inp):
                s, d = inp
                return (h * d[..., None, None] + s, h)
            _, prevs = jax.lax.scan(step, jnp.zeros_like(states[:, 0]), (jnp.moveaxis(states, 1, 0), jnp.moveaxis(chunk_decay, 2, 0)))
            prevs = jnp.moveaxis(prevs, 0, 1)
            Y_off = jnp.einsum('bcln,bchpn,bhcl->bclhp', Cc, prevs, jnp.exp(A_cum))
            Y = (Y_diag + Y_off + xh * D[:, None]).reshape(Bsz, L, D_INNER)
            Y = Y * jax.nn.silu(z)
            Y = Y * jax.lax.rsqrt(jnp.mean(Y * Y, axis=-1, keepdims=True) + EPS) * norm_w
            out = Y @ W_out
            return out @ W_lin + b_lin
        return mamba2_block(x, W_in, conv_w, conv_b, dt_bias, A_log, D, norm_w, W_out, W_lin, b_lin)
    x = x + _L0_gnn_ref(_layernorm(x, axis=-1), adj, L0_gnn_W, L0_gnn_a)
    x = x + _L0_ffn_ref(_layernorm(x, axis=-1), L0_ffn_W1, L0_ffn_b1, L0_ffn_Wg, L0_ffn_bg, L0_ffn_Wd, L0_ffn_bd)
    x = x + _L1_gnn_ref(_layernorm(x, axis=-1), adj, L1_gnn_a0, L1_gnn_a1, L1_gnn_a2, L1_gnn_a3, L1_gnn_bias)
    x = x + _L1_ffn_ref(_layernorm(x, axis=-1), L1_ffn_W_in, L1_ffn_conv_w, L1_ffn_conv_b, L1_ffn_dt_bias, L1_ffn_A_log, L1_ffn_D, L1_ffn_norm_w, L1_ffn_W_out, L1_ffn_W_lin, L1_ffn_b_lin)
    return x

_drawn_inputs = setup_inputs


def setup_inputs(seed=0):
    import zlib

    import numpy as np

    out = dict(_drawn_inputs(seed))
    spreads = {'L0_ffn_b1': (0.0, 0.797),
     'L0_ffn_bg': (0.0, 0.1),
     'L0_ffn_bd': (0.0, 0.1),
     'L1_gnn_bias': (0.0, 0.1),
     'L1_ffn_D': (1.0, 0.2),
     'L1_ffn_norm_w': (1.0, 0.2),
     'L1_ffn_b_lin': (0.0, 0.267)}
    factors = {'L0_ffn_W1': 5.047,
     'L0_ffn_Wg': 3.912,
     'L0_ffn_Wd': 5.132,
     'L1_ffn_dt_bias': 23.0,
     'L1_ffn_A_log': 8.0}
    for name, (base, spread) in spreads.items():
        noise = np.random.default_rng([zlib.crc32(name.encode()), seed]).standard_normal(out[name].shape)
        drawn = base * np.exp(spread * noise) if base else spread * noise
        out[name] = jnp.asarray(drawn.astype(out[name].dtype))
    for name, factor in factors.items():
        out[name] = (out[name] * factor).astype(out[name].dtype)
    return out
```

```python
from contextlib import ExitStack

import concourse.bass as bass
from concourse import mybir

F32 = mybir.dt.float32
I32 = mybir.dt.int32
ALU = mybir.AluOpType
ACT = mybir.ActivationFunctionType
AX = mybir.AxisListType.X

P = 128
D = 128
GT = 4
W = GT * P
EPS = 1e-5
NEG = -9e15
BIG = 3e38


class Space:

    def __init__(self, nc, ctx, tag):
        self.nc, self.ctx, self.tag, self.sems = nc, ctx, tag, []
        ctx.callback(self.end)

    def end(self):
        if self.sems:
            self.nc.clear_and_free_semaphores(self.sems)
            self.nc.all_engine_barrier()

    def sb(self, name, shape, dt=F32):
        return self.ctx.enter_context(self.nc.sbuf_tensor(f"{self.tag}_{name}", list(shape), dt))

    def bank(self, name, shape):
        return self.ctx.enter_context(self.nc.psum_tensor(f"{self.tag}_{name}", list(shape), F32))

    def sem(self, name):
        self.sems.append(self.nc.alloc_semaphore(name=f"{self.tag}_{name}"))
        return self.sems[-1]


def passed(eng, sem, q, n=1):
    if isinstance(q, int) and q < 0:
        return
    eng.wait_ge(sem, q * n + n)


def within(eng, sem, q, n, k):
    eng.wait_ge(sem, q * n + k)


def pair(q, b):
    return (q - b) * 8 + 16


def scattered(q, b):
    return ((q - b) * 8 + 16) * GT


def pipeline(eng, groups, lags, body):
    head = (lags + 3) // 2 * 2
    tail = groups // 2 * 2

    def peeled(s):
        body(s, s % 2, lambda lag: 0 <= s - lag < groups)

    for s in range(head):
        peeled(s)
    with eng.Fori(head // 2, tail // 2) as i:
        for u in range(2):
            body(i * 2 + u, u, lambda lag: True)
    for s in range(tail, groups + lags):
        peeled(s)


def gate(pool, tick, zero, s, sem_gate):
    passed(pool, sem_gate, s - 1)
    pool.tensor_tensor(tick[:, :], zero[:, 0:1], zero[:, 0:1], ALU.add).then_inc(sem_gate, 1)


def gather_view(dram):
    return dram.rearrange("(g t) p d -> g p t d", t=GT)


def norm_stats(dve, x, st, mv, tick, s, sem_st, sem_mv):
    for t in range(GT):
        dve.bn_stats(st[:, t, :], x[:, t, :]).then_inc(sem_st, 1)
    passed(dve, sem_st, s, GT)
    dve.memset(tick[:, 0:1], 0.0)
    for t in range(GT):
        dve.bn_aggr(mv[:, t, :], st[:, t, :]).then_inc(sem_mv, 1)


def norm_rstd(pool, mv, ve, rstd, eps, half, s, sem_mv, sem_ve, sem_rstd, sem_h):
    passed(pool, sem_rstd, s - 1)
    passed(pool, sem_mv, s, GT)
    pool.tensor_tensor(ve[:, :], mv[:, :, 1], eps[:, :], ALU.add).then_inc(sem_ve, 1)
    passed(pool, sem_ve, s)
    passed(pool, sem_h, s - 2, GT)
    pool.tensor_tensor(rstd[:, :], ve[:, :], half[:, :], ALU.pow).then_inc(sem_rstd, 1)


def norm_apply(dve, x, mv, rstd, h, s, sem_rstd, sem_h):
    passed(dve, sem_rstd, s)
    for t in range(GT):
        dve.tensor_scalar(h[:, t, :], x[:, t, :], mv[:, t, 0:1], rstd[:, t:t + 1],
                          ALU.subtract, ALU.mult).then_inc(sem_h, 1)


def make_identity(nc, pool, ident, sem):
    pool.memset(ident[:, :], 0.0).then_inc(sem, 1)
    pool.wait_ge(sem, 1)
    pool.affine_select(out=ident[:, :], in_=ident[:, :], compare_op=ALU.not_equal, fill=1.0, base=0,
                       pattern=[[-1, P]], channel_multiplier=1).then_inc(sem, 1)


def additive_attention(nc, x, adj, w, a, x1):
    B = x.shape[0]
    G = B // GT
    xg, adjg, x1g = gather_view(x), gather_view(adj), gather_view(x1)
    with ExitStack() as ctx:
        m = Space(nc, ctx, "aa")
        sb, bank, sem = m.sb, m.bank, m.sem
        ident = sb("ident", [P, P])
        ones = sb("ones", [P, P])
        half, eps, zero = sb("half", [P, GT]), sb("eps", [P, GT]), sb("zero", [P, GT])
        tick, ptick = sb("tick", [P, 8]), sb("ptick", [P, 1])
        wn = sb("wn", [P, D])
        wt = sb("wt", [P, D])
        ab = sb("ab", [P, 2, P])
        acol = sb("acol", [P, 2])
        wab = sb("wab", [P, 2, P])
        xt = [sb(f"x{b}", [P, GT, D]) for b in range(2)]
        xr = [sb(f"xr{b}", [P, GT, D]) for b in range(2)]
        aj = [sb(f"adj{b}", [P, GT, P], I32) for b in range(2)]
        st = sb("st", [P, GT, 6])
        mv = [sb(f"mv{b}", [P, GT, 2]) for b in range(2)]
        ve = sb("ve", [P, GT])
        rstd = [sb(f"rstd{b}", [P, GT]) for b in range(2)]
        h = [sb(f"h{b}", [P, GT, D]) for b in range(2)]
        hT = [sb(f"hT{b}", [P, GT, P]) for b in range(2)]
        wh = [sb(f"wh{b}", [P, GT, D]) for b in range(2)]
        msk = [sb(f"msk{b}", [P, GT, P]) for b in range(2)]
        e = sb("e", [P, GT, P])
        em = [sb(f"em{b}", [P, GT, P]) for b in range(2)]
        mx = sb("mx", [P, GT])
        nmx = [sb(f"nmx{b}", [P, GT]) for b in range(2)]
        prob = [sb(f"prob{b}", [P, GT, P]) for b in range(2)]
        probT = [sb(f"probT{b}", [P, GT, P]) for b in range(2)]
        rden = [sb(f"rden{b}", [P, GT]) for b in range(2)]
        xo = [sb(f"xo{b}", [P, GT, D]) for b in range(2)]
        T_ps, PT_ps, E_ps, Wh_ps, U_ps = (bank(n, [P, GT, P]) for n in ("T", "PT", "E", "Wh", "U"))
        den_ps = bank("den", [P, 512])

        s_gate = sem("gate")
        s_w, s_const, s_wt, s_wtc, s_ab = sem("w"), sem("const"), sem("wt"), sem("wtc"), sem("ab")
        s_x = [sem(f"x{b}") for b in range(2)]
        s_xr = [sem(f"xr{b}") for b in range(2)]
        s_adj = [sem(f"adj{b}") for b in range(2)]
        s_out = [sem(f"out{b}") for b in range(2)]
        s_st, s_mv, s_ve, s_rstd, s_h = sem("st"), sem("mv"), sem("ve"), sem("rstd"), sem("h")
        s_T, s_hT, s_E, s_e, s_msk, s_em, s_mx, s_nmx, s_prob = (
            sem(n) for n in ("T", "hT", "E", "e", "msk", "em", "mx", "nmx", "prob"))
        s_Wh, s_wh, s_PT, s_probT, s_den, s_U, s_rden, s_xo = (
            sem(n) for n in ("Wh", "wh", "PT", "probT", "den", "U", "rden", "xo"))
        block = ctx.enter_context(nc.Block())

        @block.sync
        def _(sp):
            sp.dma_start(wn[:, :], w).then_inc(s_w, 16)
            sp.dma_start(acol[:, :], a.rearrange("(k p) z -> p (k z)", p=P),
                         allow_slow_non_contiguous=True).then_inc(s_w, 16)

            def body(s, b, live):
                if live(0):
                    passed(sp, s_h, s - 2, GT)
                    sp.dma_start(xt[b][:, :, :], xg[s]).then_inc(s_x[b], 16)
                    passed(sp, s_msk, s - 2)
                    sp.dma_start(aj[b][:, :, :], adjg[s]).then_inc(s_adj[b], 16)
                if live(1):
                    passed(sp, s_xo, s - 3, GT)
                    sp.dma_start(xr[1 - b][:, :, :], xg[s - 1]).then_inc(s_xr[1 - b], 16)
                if live(2):
                    passed(sp, s_xo, s - 2, GT)
                    sp.dma_start(x1g[s - 2], xo[b][:, :, :]).then_inc(s_out[b], 16)

            pipeline(sp, G, 2, body)
            for b in range(2):
                sp.wait_ge(s_out[b], 16 * (G // 2))

        @block.gpsimd
        def _(pool):
            make_identity(nc, pool, ident, s_const)
            pool.memset(ones[:, :], 1.0).then_inc(s_const, 1)
            pool.memset(half[:, :], -0.5).then_inc(s_const, 1)
            pool.memset(eps[:, :], EPS).then_inc(s_const, 1)
            pool.memset(zero[:, :], 0.0).then_inc(s_const, 1)
            pool.wait_ge(s_const, 6)

            def body(s, b, live):
                if live(0):
                    norm_rstd(pool, mv[b], ve, rstd[b], eps, half, s, s_mv, s_ve, s_rstd, s_h)
                    pool.wait_ge(s_adj[b], pair(s, b))
                    passed(pool, s_e, s - 2)
                    gate(pool, ptick, zero, s, s_gate)
                    pool.tensor_scalar(msk[b][:, :, :], aj[b][:, :, :], 0.0, None, ALU.is_le).then_inc(s_msk, 1)

            pipeline(pool, G, 2, body)

        @block.scalar
        def _(act):
            def body(s, b, live):
                c = 1 - b
                if live(1):
                    passed(act, s_T, s - 1)
                    act.activation(hT[c][:, :, :], T_ps[:, :, :], ACT.Copy).then_inc(s_hT, 1)
                if live(2):
                    passed(act, s_PT, s - 2)
                    act.activation(probT[b][:, :, :], PT_ps[:, :, :], ACT.Copy).then_inc(s_probT, 1)
                if live(1):
                    passed(act, s_Wh, s - 1)
                    passed(act, s_U, s - 3)
                    act.activation(wh[c][:, :, :], Wh_ps[:, :, :], ACT.Copy).then_inc(s_wh, 1)
                    passed(act, s_nmx, s - 1)
                    passed(act, s_PT, s - 3)
                    for t in range(GT):
                        act.activation(prob[c][:, t, :], em[c][:, t, :], ACT.Exp,
                                       bias=nmx[c][:, t:t + 1]).then_inc(s_prob, 1)

            pipeline(act, G, 2, body)

        @block.vector
        def _(dve):
            dve.wait_ge(s_w, 32)
            dve.wait_ge(s_const, 3)
            for k in range(2):
                dve.tensor_scalar(ab[:, k, :], ones[:, :], acol[:, k:k + 1], None, ALU.mult).then_inc(s_ab, 1)
            dve.wait_ge(s_wt, 1)
            dve.tensor_copy(wt[:, :], T_ps[:, 0, :]).then_inc(s_wtc, 1)
            dve.wait_ge(s_wt, 2)
            dve.tensor_copy(wab[:, :, :], E_ps[:, 0:2, :]).then_inc(s_wtc, 1)

            def body(s, b, live):
                c = 1 - b
                if live(0):
                    dve.wait_ge(s_x[b], pair(s, b))
                    passed(dve, s_mv, s - 1, GT)
                    norm_stats(dve, xt[b], st, mv[b], tick, s, s_st, s_mv)
                if live(1):
                    passed(dve, s_E, s - 1)
                    passed(dve, s_msk, s - 1)
                    dve.scalar_tensor_tensor(out=e[:, :, :], in0=msk[c][:, :, :], scalar=NEG,
                                             in1=E_ps[:, :, :], op0=ALU.mult, op1=ALU.add).then_inc(s_e, 1)
                    passed(dve, s_e, s - 1)
                    passed(dve, s_prob, s - 3, GT)
                    dve.scalar_tensor_tensor(out=em[c][:, :, :], in0=e[:, :, :], scalar=0.2,
                                             in1=e[:, :, :], op0=ALU.mult, op1=ALU.max).then_inc(s_em, 1)
                    passed(dve, s_em, s - 1)
                    dve.tensor_reduce(mx[:, :], em[c][:, :, :], AX, ALU.max).then_inc(s_mx, 1)
                    passed(dve, s_mx, s - 1)
                    dve.tensor_scalar(nmx[c][:, :], mx[:, :], -1.0, None, ALU.mult).then_inc(s_nmx, 1)
                if live(0):
                    passed(dve, s_T, s - 2)
                    norm_apply(dve, xt[b], mv[b], rstd[b], h[b], s, s_rstd, s_h)
                if live(2):
                    passed(dve, s_den, s - 2)
                    dve.reciprocal(rden[b][:, :], den_ps[:, 0:GT]).then_inc(s_rden, 1)
                    passed(dve, s_rden, s - 2)
                    passed(dve, s_U, s - 2)
                    dve.wait_ge(s_xr[b], pair(s - 2, b))
                    if not (isinstance(s, int) and s < 4):
                        dve.wait_ge(s_out[b], pair(s - 4, b))
                    for t in range(GT):
                        dve.scalar_tensor_tensor(out=xo[b][:, t, :], in0=U_ps[:, t, :],
                                                 scalar=rden[b][:, t:t + 1], in1=xr[b][:, t, :],
                                                 op0=ALU.mult, op1=ALU.add).then_inc(s_xo, 1)

            pipeline(dve, G, 2, body)

        @block.tensor
        def _(pe):
            pe.wait_ge(s_w, 32)
            pe.wait_ge(s_const, 2)
            pe.transpose(T_ps[:, 0, :], wn[:, :], ident[:, :]).then_inc(s_wt, 1)
            pe.wait_ge(s_ab, 2)
            pe.matmul(E_ps[:, 0:2, :], wn[:, :], ab[:, :, :], start=True, stop=True).then_inc(s_wt, 1)
            pe.wait_ge(s_wtc, 2)

            def body(s, b, live):
                c = 1 - b
                if live(1):
                    passed(pe, s_h, s - 1, GT)
                    passed(pe, s_hT, s - 2)
                    for t in range(GT):
                        mm = pe.transpose(T_ps[:, t, :], h[c][:, t, :], ident[:, :])
                    mm.then_inc(s_T, 1)
                if live(2):
                    passed(pe, s_prob, s - 2, GT)
                    passed(pe, s_probT, s - 3)
                    for t in range(GT):
                        mm = pe.transpose(PT_ps[:, t, :], prob[b][:, t, :], ident[:, :])
                    mm.then_inc(s_PT, 1)
                if live(1):
                    passed(pe, s_hT, s - 1)
                    passed(pe, s_e, s - 2)
                    pe.matmul(E_ps[:, :, :], wab[:, 1, :], hT[c][:, :, :], start=True, stop=False)
                    for t in range(GT):
                        mm = pe.matmul(E_ps[:, t, :], hT[c][:, t, :], wab[:, 0, :], start=False, stop=(t == GT - 1))
                    mm.then_inc(s_E, 1)
                    passed(pe, s_wh, s - 2)
                    for t in range(GT):
                        mm = pe.matmul(Wh_ps[:, t, :], hT[c][:, t, :], wt[:, :], start=True, stop=True)
                    mm.then_inc(s_Wh, 1)
                if live(2):
                    passed(pe, s_probT, s - 2)
                    passed(pe, s_rden, s - 3)
                    for t in range(GT):
                        mm = pe.matmul(den_ps[:, t:t + 1], probT[b][:, t, :], ones[:, 0:1], start=True, stop=True)
                    mm.then_inc(s_den, 1)
                    passed(pe, s_xo, s - 3, GT)
                    for t in range(GT):
                        mm = pe.matmul(U_ps[:, t, :], probT[b][:, t, :], wh[b][:, t, :], start=True, stop=True)
                    mm.then_inc(s_U, 1)

            pipeline(pe, G, 2, body)

class Routing:

    def __init__(self, nc, ctx, graphs, experts):
        m = Space(nc, ctx, "rt")
        self.tiles = graphs + experts
        self.tiles += -self.tiles % (2 * GT)
        self.ptop = m.sb("ptop", [P, graphs])
        self.row = m.sb("row", [P, graphs], I32)
        self.expert = m.sb("expert", [P, self.tiles], I32)


def gates(nc, x1, w1, b1, wg, bg, rt, h_rows):
    B = x1.shape[0]
    G = B // GT
    E = bg.shape[0]
    C = w1.shape[1] // P
    xg, hg = gather_view(x1), h_rows.rearrange("(g t p) d -> g p t d", t=GT, p=P)
    with ExitStack() as ctx:
        m = Space(nc, ctx, "ga")
        sb, bank, sem = m.sb, m.bank, m.sem
        ident, ones = sb("ident", [P, P]), sb("ones", [P, P])
        before = sb("before", [P, P])
        half, eps = sb("half", [P, GT]), sb("eps", [P, GT])
        tick = sb("tick", [P, 8])
        w1s, b1s = sb("w1s", [P, C * P]), sb("b1s", [P, C])
        wgs, bgs = sb("wgs", [P, C, E]), sb("bgs", [P, E])
        xt = [sb(f"x{b}", [P, GT, D]) for b in range(2)]
        st, ve = sb("st", [P, GT, 6]), sb("ve", [P, GT])
        mv = [sb(f"mv{b}", [P, GT, 2]) for b in range(2)]
        rstd = [sb(f"rstd{b}", [P, GT]) for b in range(2)]
        h = [sb(f"h{b}", [P, GT, D]) for b in range(2)]
        hT = [sb(f"hT{b}", [P, GT, P]) for b in range(2)]
        HT = [sb(f"HT{b}", [P, C, GT, P]) for b in range(2)]
        lg = sb("lg", [P, B, E])
        iota_e, iota_j = sb("iota_e", [P, B, E]), sb("iota_j", [P, rt.tiles, E])
        top, ex, first, oh = (sb(n, [P, B, E]) for n in ("top", "ex", "first", "oh"))
        mx, den, idx, pos = (sb(n, [P, B]) for n in ("mx", "den", "idx", "pos"))
        inc, off = sb("inc", [P, B, E]), sb("off", [P, B, E])
        cnt_i, pad_i = sb("cnt_i", [P, E], I32), sb("pad_i", [P, E], I32)
        pad, end, start = sb("pad", [P, E]), sb("end", [P, E]), sb("start", [P, E])
        full, tex = sb("full", [P, rt.tiles, E]), sb("tex", [P, rt.tiles])
        T_ps = bank("T", [P, GT, P])
        G_ps = [bank(f"G{c}", [P, GT, P]) for c in range(C)]
        L_ps = bank("L", [P, B, E])

        s_w, s_const = sem("w"), sem("const")
        s_x, s_hd = [sem(f"x{b}") for b in range(2)], [sem(f"hd{b}") for b in range(2)]
        s_st, s_mv, s_ve, s_rstd, s_h = sem("st"), sem("mv"), sem("ve"), sem("rstd"), sem("h")
        s_T, s_hT, s_G, s_HT, s_L, s_lg = (sem(n) for n in ("T", "hT", "G", "HT", "L", "lg"))
        s_r, s_max, s_ex, s_cnt, s_oh = sem("r"), sem("max"), sem("ex"), sem("cnt"), sem("oh")
        block = ctx.enter_context(nc.Block())

        @block.sync
        def _(sp):
            sp.dma_start(w1s[:, :], w1).then_inc(s_w, 16)
            for c in range(C):
                sp.dma_start(b1s[:, c:c + 1], b1[c * P:(c + 1) * P].rearrange("(p z) -> p z", z=1)).then_inc(s_w, 16)
            sp.dma_start(wgs[:, :, :], wg.rearrange("(c p) e -> p c e", p=P)).then_inc(s_w, 16)
            sp.dma_start(bgs[:, :], bg.partition_broadcast(P)).then_inc(s_w, 16)

            def body(s, b, live):
                if live(0):
                    passed(sp, s_h, s - 2, GT)
                    sp.dma_start(xt[b][:, :, :], xg[s]).then_inc(s_x[b], 16)
                if live(1):
                    passed(sp, s_h, s - 1, GT)
                    sp.dma_start(hg[s - 1], h[1 - b][:, :, :]).then_inc(s_hd[1 - b], 16)

            pipeline(sp, G, 2, body)
            for b in range(2):
                sp.wait_ge(s_hd[b], 16 * (G // 2))

        @block.gpsimd
        def _(pool):
            make_identity(nc, pool, ident, s_const)
            pool.memset(half[:, :], -0.5).then_inc(s_const, 1)
            pool.memset(eps[:, :], EPS).then_inc(s_const, 1)
            pool.memset(ones[:, :], 1.0).then_inc(s_const, 1)
            pool.wait_ge(s_const, 5)
            pool.affine_select(out=before[:, :], in_=ones[:, :], compare_op=ALU.is_gt, fill=0.0, base=0,
                               pattern=[[1, P]], channel_multiplier=-1).then_inc(s_const, 1)
            pool.iota(iota_e[:, :, :], pattern=[[0, B], [1, E]], base=0, channel_multiplier=0,
                      allow_small_or_imprecise_dtypes=True).then_inc(s_const, 1)
            pool.iota(iota_j[:, :, :], pattern=[[P, rt.tiles], [0, E]], base=0, channel_multiplier=0,
                      allow_small_or_imprecise_dtypes=True).then_inc(s_const, 1)
            pool.wait_ge(s_const, 8)

            def body(s, b, live):
                if live(0):
                    norm_rstd(pool, mv[b], ve, rstd[b], eps, half, s, s_mv, s_ve, s_rstd, s_h)

            pipeline(pool, G, 2, body)

        @block.scalar
        def _(act):
            act.wait_ge(s_w, 16 * (C + 3))

            def body(s, b, live):
                c = 1 - b
                if live(1):
                    passed(act, s_T, s - 1)
                    passed(act, s_G, s - 3, C)
                    act.activation(hT[c][:, :, :], T_ps[:, :, :], ACT.Copy).then_inc(s_hT, 1)
                    passed(act, s_L, s - 3)
                    for k in range(C):
                        within(act, s_G, s - 1, C, k + 1)
                        act.activation(HT[c][:, k, :, :], G_ps[k][:, :, :], ACT.Gelu,
                                       bias=b1s[:, k:k + 1]).then_inc(s_HT, 1)

            pipeline(act, G, 2, body)
            act.wait_ge(s_max, 1)
            act.activation(ex[:, :, :], top[:, :, :], ACT.Exp).then_inc(s_ex, 1)

        @block.vector
        def _(dve):
            dve.wait_ge(s_w, 16 * (C + 3))
            dve.wait_ge(s_const, 8)

            def body(s, b, live):
                if live(0):
                    dve.wait_ge(s_x[b], pair(s, b))
                    passed(dve, s_mv, s - 1, GT)
                    norm_stats(dve, xt[b], st, mv[b], tick, s, s_st, s_mv)
                if live(2):
                    passed(dve, s_L, s - 2)
                    dve.tensor_tensor(lg[:, bass.ts(s - 2, GT), :], L_ps[:, 0:GT, :],
                                      bgs[:, :].unsqueeze(1).to_broadcast([P, GT, E]), ALU.add).then_inc(s_lg, 1)
                if live(0):
                    passed(dve, s_T, s - 2)
                    if not (isinstance(s, int) and s < 2):
                        dve.wait_ge(s_hd[b], pair(s - 2, b))
                    norm_apply(dve, xt[b], mv[b], rstd[b], h[b], s, s_rstd, s_h)

            pipeline(dve, G, 2, body)

            n = [0]

            def then(ins):
                n[0] += 1
                ins.then_inc(s_r, 1)
                dve.wait_ge(s_r, n[0])

            dve.wait_ge(s_lg, G)
            then(dve.tensor_reduce(mx[:, :], lg[:, :, :], AX, ALU.max))
            mx_e = mx[:, :].unsqueeze(2).to_broadcast([P, B, E])
            dve.tensor_tensor(top[:, :, :], lg[:, :, :], mx_e, ALU.subtract).then_inc(s_max, 1)
            then(dve.tensor_tensor(oh[:, :, :], lg[:, :, :], mx_e, ALU.is_equal))
            then(dve.scalar_tensor_tensor(out=first[:, :, :], in0=oh[:, :, :], scalar=-float(E),
                                          in1=iota_e[:, :, :], op0=ALU.mult, op1=ALU.add))
            then(dve.tensor_reduce(idx[:, :], first[:, :, :], AX, ALU.min))
            dve.tensor_tensor(oh[:, :, :], first[:, :, :], idx[:, :].unsqueeze(2).to_broadcast([P, B, E]),
                              ALU.is_equal).then_inc(s_oh, 1)
            dve.wait_ge(s_ex, 1)
            then(dve.tensor_reduce(den[:, :], ex[:, :, :], AX, ALU.add))
            then(dve.reciprocal(rt.ptop[:, :], den[:, :]))
            dve.wait_ge(s_cnt, 2)
            for k in range(E):
                sc = dve.tensor_tensor_scan(inc[:, :, k], ones[:, 0:B], G_ps[0][:, :, :].rearrange(
                    "p t (u e) -> p (t u) e", e=E)[:, :, k], 0.0, ALU.mult, ALU.add)
            then(sc)
            then(dve.tensor_tensor(off[:, :, :], inc[:, :, :], G_ps[0][:, :, :].rearrange(
                "p t (u e) -> p (t u) e", e=E), ALU.subtract))
            then(dve.tensor_tensor(off[:, :, :], off[:, :, :], G_ps[1][:, :, :].rearrange(
                "p t (u e) -> p (t u) e", e=E), ALU.add))
            then(dve.tensor_scalar(cnt_i[:, :], inc[:, B - 1, :], float(P - 1), None, ALU.add))
            shift = P.bit_length() - 1
            then(dve.tensor_scalar(pad_i[:, :], cnt_i[:, :], shift, shift, ALU.arith_shift_right,
                                   ALU.arith_shift_left))
            then(dve.tensor_copy(pad[:, :], pad_i[:, :]))
            then(dve.tensor_tensor_scan(end[:, :], ones[:, 0:E], pad[:, :], 0.0, ALU.mult, ALU.add))
            then(dve.tensor_tensor(start[:, :], end[:, :], pad[:, :], ALU.subtract))
            then(dve.tensor_tensor(off[:, :, :], off[:, :, :], start[:, :].unsqueeze(1).to_broadcast([P, B, E]),
                                   ALU.add))
            then(dve.tensor_tensor(off[:, :, :], off[:, :, :], oh[:, :, :], ALU.mult))
            then(dve.tensor_reduce(pos[:, :], off[:, :, :], AX, ALU.add))
            then(dve.tensor_copy(rt.row[:, :], pos[:, :]))
            then(dve.tensor_tensor(full[:, :, :], end[:, :].unsqueeze(1).to_broadcast([P, rt.tiles, E]),
                                   iota_j[:, :, :], ALU.is_le))
            then(dve.tensor_reduce(tex[:, :], full[:, :, :], AX, ALU.add))
            then(dve.tensor_scalar(rt.expert[:, :], tex[:, :], float(E - 1), None, ALU.min))

        @block.tensor
        def _(pe):
            pe.wait_ge(s_w, 16 * (C + 3))
            pe.wait_ge(s_const, 6)

            def body(s, b, live):
                c = 1 - b
                if live(1):
                    passed(pe, s_h, s - 1, GT)
                    passed(pe, s_hT, s - 2)
                    for t in range(GT):
                        mm = pe.transpose(T_ps[:, t, :], h[c][:, t, :], ident[:, :])
                    mm.then_inc(s_T, 1)
                if live(2):
                    passed(pe, s_HT, s - 2, C)
                    passed(pe, s_lg, s - 3)
                    for t in range(GT):
                        for k in range(C):
                            mm = pe.matmul(L_ps[:, t, :], HT[b][:, k, t, :], wgs[:, k, :],
                                           start=(k == 0), stop=(k == C - 1))
                    mm.then_inc(s_L, 1)
                if live(1):
                    passed(pe, s_hT, s - 1)
                    for k in range(C):
                        if not (isinstance(s, int) and s < 2):
                            within(pe, s_HT, s - 2, C, k + 1)
                        pe.matmul(G_ps[k][:, :, :], w1s[:, k * P:(k + 1) * P], hT[c][:, :, :],
                                  start=True, stop=True).then_inc(s_G, 1)

            pipeline(pe, G, 2, body)
            pe.wait_ge(s_oh, 1)
            oh2 = oh[:, :, :].rearrange("p t e -> p (t e)")
            flat = [g[:, :, :].rearrange("p t d -> p (t d)") for g in G_ps]
            pe.matmul(flat[0], ones[:, :], oh2, start=True, stop=True).then_inc(s_cnt, 1)
            pe.matmul(flat[1], before[:, :], oh2, start=True, stop=True).then_inc(s_cnt, 1)


def dispatch(nc, rt, h_rows, sorted_rows):
    G = h_rows.shape[0] // (GT * P)
    hg = h_rows.rearrange("(g t p) d -> g p t d", t=GT, p=P)
    clear = sorted_rows.rearrange("(g t p) d -> g p t d", t=GT, p=P)
    with ExitStack() as ctx:
        m = Space(nc, ctx, "di")
        sb, sem = m.sb, m.sem
        zeros = sb("zeros", [P, GT, D])
        ht = [sb(f"h{b}", [P, GT, D]) for b in range(2)]
        row = [sb(f"row{b}", [P, GT], I32) for b in range(2)]
        zero, ptick = sb("zero", [P, 1]), sb("ptick", [P, 1])
        s_gate, s_z, s_clear, s_row = sem("gate"), sem("z"), sem("clear"), sem("row")
        s_h, s_sc = [sem(f"h{b}") for b in range(2)], [sem(f"sc{b}") for b in range(2)]
        block = ctx.enter_context(nc.Block())

        @block.sync
        def _(sp):
            sp.wait_ge(s_z, 2)
            for g in range(rt.tiles // GT):
                sp.dma_start(clear[g], zeros[:, :, :]).then_inc(s_clear, 16)

            def body(s, b, live):
                if not (isinstance(s, int) and s < 2):
                    sp.wait_ge(s_sc[b], scattered(s - 2, b))
                sp.dma_start(ht[b][:, :, :], hg[s]).then_inc(s_h[b], 16)

            pipeline(sp, G, 0, body)

        @block.gpsimd
        def _(pool):
            pool.memset(zero[:, :], 0.0).then_inc(s_z, 1)
            pool.memset(zeros[:, :, :], 0.0).then_inc(s_z, 1)
            pool.wait_ge(s_z, 2)
            pool.wait_ge(s_clear, 16 * (rt.tiles // GT))

            def body(s, b, live):
                pool.wait_ge(s_row, s + 1)
                pool.wait_ge(s_h[b], pair(s, b))
                gate(pool, ptick, zero, s, s_gate)
                for t in range(GT):
                    pool.indirect_dma_start(sorted_rows, bass.IndirectOffsetOnAxis(row[b][:, t:t + 1], 0),
                                            ht[b][:, t, :], None).then_inc(s_sc[b], 16)

            pipeline(pool, G, 0, body)
            for b in range(2):
                pool.wait_ge(s_sc[b], scattered(G - 2 + b, b))

        @block.vector
        def _(dve):
            def body(s, b, live):
                if not (isinstance(s, int) and s < 2):
                    dve.wait_ge(s_sc[b], scattered(s - 2, b))
                dve.tensor_copy(row[b][:, :], rt.row[:, bass.ts(s, GT)]).then_inc(s_row, 1)

            pipeline(dve, G, 0, body)


def experts(nc, w1, b1, wd, bd, rt, sorted_rows, y_rows):
    G = rt.tiles // GT
    E = bd.shape[0]
    C = w1.shape[1] // P
    hg = sorted_rows.rearrange("(g t p) d -> g p t d", t=GT, p=P)
    yg = y_rows.rearrange("(g t p) d -> g p t d", t=GT, p=P)
    with ExitStack() as ctx:
        m = Space(nc, ctx, "ex")
        sb, bank, sem = m.sb, m.bank, m.sem
        ident, ones = sb("ident", [P, P]), sb("ones", [1, P])
        w1s, b1s = sb("w1s", [P, C * P]), sb("b1s", [P, C])
        wds, bds = sb("wds", [P, C, E * D]), sb("bds", [1, E * D])
        h = [sb(f"h{b}", [P, GT, D]) for b in range(2)]
        hT = [sb(f"hT{b}", [P, GT, P]) for b in range(2)]
        HT = [sb(f"HT{b}", [P, C, GT, P]) for b in range(2)]
        y = [sb(f"y{b}", [P, GT, D]) for b in range(2)]
        T_ps, Y_ps = bank("T", [P, GT, P]), bank("Y", [P, GT, D])
        G_ps = [bank(f"G{c}", [P, GT, P]) for c in range(C)]
        s_w, s_const = sem("w"), sem("const")
        s_hl, s_out = [sem(f"hl{b}") for b in range(2)], [sem(f"out{b}") for b in range(2)]
        s_T, s_hT, s_G, s_HT, s_Y, s_y = (sem(n) for n in ("T", "hT", "G", "HT", "Y", "y"))
        N_W = 2 + 2 * C
        block = ctx.enter_context(nc.Block())

        @block.sync
        def _(sp):
            def body(s, b, live):
                if live(0):
                    passed(sp, s_T, s - 2)
                    sp.dma_start(h[b][:, :, :], hg[s]).then_inc(s_hl[b], 16)
                if live(1):
                    passed(sp, s_y, s - 1)
                    sp.dma_start(yg[s - 1], y[1 - b][:, :, :]).then_inc(s_out[1 - b], 16)

            pipeline(sp, G, 1, body)
            for b in range(2):
                sp.wait_ge(s_out[b], 16 * (G // 2))

        @block.gpsimd
        def _(pool):
            make_identity(nc, pool, ident, s_const)
            pool.memset(ones[:, :], 1.0).then_inc(s_const, 1)

        @block.scalar
        def _(act):
            act.dma_start(w1s[:, :], w1).then_inc(s_w, 16)
            for c in range(C):
                act.dma_start(b1s[:, c:c + 1], b1[c * P:(c + 1) * P].rearrange("(p z) -> p z", z=1)).then_inc(s_w, 16)
                act.dma_start(wds[:, c, :].rearrange("p (e d) -> p e d", e=E),
                              wd[:, c * P:(c + 1) * P, :].rearrange("e p d -> p e d")).then_inc(s_w, 16)
            act.dma_start(bds[:, :], bd.rearrange("(z e) d -> z (e d)", z=1)).then_inc(s_w, 16)
            act.wait_ge(s_w, 16 * N_W)

            def body(s, b, live):
                if live(0):
                    passed(act, s_Y, s - 2)
                    for k in range(C):
                        within(act, s_G, s, C, k + 1)
                        act.activation(HT[b][:, k, :, :], G_ps[k][:, :, :], ACT.Gelu,
                                       bias=b1s[:, k:k + 1]).then_inc(s_HT, 1)

            pipeline(act, G, 1, body)

        @block.vector
        def _(dve):
            def body(s, b, live):
                if live(0):
                    passed(dve, s_T, s)
                    passed(dve, s_G, s - 2, C)
                    dve.tensor_copy(hT[b][:, :, :], T_ps[:, :, :]).then_inc(s_hT, 1)
                if live(1):
                    passed(dve, s_Y, s - 1)
                    if not (isinstance(s, int) and s < 3):
                        dve.wait_ge(s_out[1 - b], pair(s - 3, 1 - b))
                    dve.tensor_copy(y[1 - b][:, :, :], Y_ps[:, :, :]).then_inc(s_y, 1)

            pipeline(dve, G, 1, body)

        @block.tensor
        def _(pe):
            pe.wait_ge(s_w, 16 * N_W)
            pe.wait_ge(s_const, 3)

            def body(s, b, live):
                c = 1 - b
                if live(0):
                    pe.wait_ge(s_hl[b], pair(s, b))
                    passed(pe, s_hT, s - 1)
                    for t in range(GT):
                        mm = pe.transpose(T_ps[:, t, :], h[b][:, t, :], ident[:, :])
                    mm.then_inc(s_T, 1)
                if live(1):
                    passed(pe, s_HT, s - 1, C)
                    passed(pe, s_y, s - 2)
                    for t in range(GT):
                        e = pe.value_load(rt.expert[0:1, bass.ts((s - 1) * GT + t, 1)], min_val=0, max_val=E - 1)
                        for k in range(C):
                            pe.matmul(Y_ps[:, t, :], HT[c][:, k, t, :], wds[:, k, bass.ts(e, D)],
                                      start=(k == 0), stop=False)
                        mm = pe.matmul(Y_ps[:, t, :], ones[:, :], bds[:, bass.ts(e, D)], start=False, stop=True)
                    mm.then_inc(s_Y, 1)
                if live(0):
                    passed(pe, s_hT, s)
                    for k in range(C):
                        if not (isinstance(s, int) and s < 1):
                            within(pe, s_HT, s - 1, C, k + 1)
                        pe.matmul(G_ps[k][:, :, :], w1s[:, k * P:(k + 1) * P], hT[b][:, :, :],
                                  start=True, stop=True).then_inc(s_G, 1)

            pipeline(pe, G, 1, body)


def combine(nc, x1, rt, y_rows, x2):
    G = x1.shape[0] // GT
    xg, x2g = gather_view(x1), gather_view(x2)
    with ExitStack() as ctx:
        m = Space(nc, ctx, "co")
        sb, sem = m.sb, m.sem
        xt, yt, xo = ([sb(f"{n}{b}", [P, GT, D]) for b in range(2)] for n in ("x", "y", "xo"))
        row = [sb(f"row{b}", [P, GT], I32) for b in range(2)]
        pt = [sb(f"pt{b}", [P, GT]) for b in range(2)]
        zero, ptick = sb("zero", [P, 1]), sb("ptick", [P, 1])
        s_gate, s_z, s_row, s_pt, s_xo = sem("gate"), sem("z"), sem("row"), sem("pt"), sem("xo")
        s_x, s_y, s_out = ([sem(f"{n}{b}") for b in range(2)] for n in ("x", "y", "out"))
        block = ctx.enter_context(nc.Block())

        @block.sync
        def _(sp):
            def body(s, b, live):
                if live(0):
                    passed(sp, s_xo, s - 2, GT)
                    sp.dma_start(xt[b][:, :, :], xg[s]).then_inc(s_x[b], 16)
                if live(1):
                    passed(sp, s_xo, s - 1, GT)
                    sp.dma_start(x2g[s - 1], xo[1 - b][:, :, :]).then_inc(s_out[1 - b], 16)

            pipeline(sp, G, 1, body)
            for b in range(2):
                sp.wait_ge(s_out[b], 16 * (G // 2))

        @block.gpsimd
        def _(pool):
            pool.memset(zero[:, :], 0.0).then_inc(s_z, 1)
            pool.wait_ge(s_z, 1)

            def body(s, b, live):
                if live(0):
                    passed(pool, s_row, s)
                    passed(pool, s_xo, s - 2, GT)
                    gate(pool, ptick, zero, s, s_gate)
                    for t in range(GT):
                        pool.indirect_dma_start(yt[b][:, t, :], None, y_rows,
                                                bass.IndirectOffsetOnAxis(row[b][:, t:t + 1], 0)).then_inc(s_y[b], 16)

            pipeline(pool, G, 1, body)

        @block.vector
        def _(dve):
            def body(s, b, live):
                c = 1 - b
                if live(0):
                    if not (isinstance(s, int) and s < 2):
                        dve.wait_ge(s_y[b], scattered(s - 2, b))
                    dve.tensor_copy(row[b][:, :], rt.row[:, bass.ts(s, GT)]).then_inc(s_row, 1)
                    passed(dve, s_xo, s - 2, GT)
                    dve.tensor_copy(pt[b][:, :], rt.ptop[:, bass.ts(s, GT)]).then_inc(s_pt, 1)
                if live(1):
                    passed(dve, s_pt, s - 1)
                    dve.wait_ge(s_x[c], pair(s - 1, c))
                    dve.wait_ge(s_y[c], scattered(s - 1, c))
                    if not (isinstance(s, int) and s < 3):
                        dve.wait_ge(s_out[c], pair(s - 3, c))
                    for t in range(GT):
                        dve.scalar_tensor_tensor(out=xo[c][:, t, :], in0=yt[c][:, t, :], scalar=pt[c][:, t:t + 1],
                                                 in1=xt[c][:, t, :], op0=ALU.mult, op1=ALU.add).then_inc(s_xo, 1)

            pipeline(dve, G, 1, body)



def typed_attention(nc, x, adj, a_all, bias, x3):
    B = x.shape[0]
    G = B // GT
    K = len(a_all)
    xg, adjg, x3g = gather_view(x), gather_view(adj), gather_view(x3)
    with ExitStack() as ctx:
        m = Space(nc, ctx, "ta")
        sb, bank, sem = m.sb, m.bank, m.sem
        ident = sb("ident", [P, P])
        half, eps, zero = sb("half", [P, GT]), sb("eps", [P, GT]), sb("zero", [P, GT])
        tick, ptick = sb("tick", [P, 8]), sb("ptick", [P, 1])
        acol = sb("acol", [P, K])
        brow = sb("brow", [P, D])
        xt = [sb(f"x{b}", [P, GT, D]) for b in range(2)]
        xr = [sb(f"xr{b}", [P, GT, D]) for b in range(2)]
        xb = [sb(f"xb{b}", [P, GT, D]) for b in range(2)]
        aj = [sb(f"adj{b}", [P, GT, P], I32) for b in range(2)]
        st = sb("st", [P, GT, 6])
        mv = [sb(f"mv{b}", [P, GT, 2]) for b in range(2)]
        ve = sb("ve", [P, GT])
        rstd = [sb(f"rstd{b}", [P, GT]) for b in range(2)]
        h = [sb(f"h{b}", [P, GT, D]) for b in range(2)]
        hT = [sb(f"hT{b}", [P, GT, P]) for b in range(2)]
        hTa = [sb(f"hTa{b}", [P, K, GT, P]) for b in range(2)]
        is_k = [sb(f"is_k{b}", [P, K, GT, P], I32) for b in range(2)]
        sel = [sb(f"sel{b}", [P, GT, P]) for b in range(2)]
        lk = [sb(f"lk{b}", [P, GT, P]) for b in range(2)]
        al = [sb(f"al{b}", [P, GT, P]) for b in range(2)]
        alT = [sb(f"alT{b}", [P, GT, P]) for b in range(2)]
        xo = [sb(f"xo{b}", [P, GT, D]) for b in range(2)]
        T_ps, AT_ps, U_ps = (bank(n, [P, GT, P]) for n in ("T", "AT", "U"))
        E_ps = bank("E", [P, GT, K, P])

        s_w, s_const, s_gate = sem("w"), sem("const"), sem("gate")
        s_x = [sem(f"x{b}") for b in range(2)]
        s_xr = [sem(f"xr{b}") for b in range(2)]
        s_adj = [sem(f"adj{b}") for b in range(2)]
        s_out = [sem(f"out{b}") for b in range(2)]
        s_st, s_mv, s_ve, s_rstd, s_h = sem("st"), sem("mv"), sem("ve"), sem("rstd"), sem("h")
        s_T, s_hT, s_hTa, s_isk, s_fill, s_E, s_sel, s_lk, s_al, s_AT, s_alT, s_U, s_xb, s_xo = (
            sem(n) for n in ("T", "hT", "hTa", "isk", "fill", "E", "sel", "lk", "al", "AT", "alT", "U", "xb", "xo"))
        block = ctx.enter_context(nc.Block())

        @block.sync
        def _(sp):
            for k in range(K):
                sp.dma_start(acol[:, k:k + 1], a_all[k]).then_inc(s_w, 16)
            sp.dma_start(brow[:, :], bias.partition_broadcast(P)).then_inc(s_w, 16)

            def body(s, b, live):
                if live(0):
                    passed(sp, s_h, s - 2, GT)
                    sp.dma_start(xt[b][:, :, :], xg[s]).then_inc(s_x[b], 16)
                    passed(sp, s_isk, s - 2, K)
                    sp.dma_start(aj[b][:, :, :], adjg[s]).then_inc(s_adj[b], 16)
                if live(1):
                    passed(sp, s_xb, s - 3)
                    sp.dma_start(xr[1 - b][:, :, :], xg[s - 1]).then_inc(s_xr[1 - b], 16)
                if live(2):
                    passed(sp, s_xo, s - 2)
                    sp.dma_start(x3g[s - 2], xo[b][:, :, :]).then_inc(s_out[b], 16)

            pipeline(sp, G, 2, body)
            for b in range(2):
                sp.wait_ge(s_out[b], 16 * (G // 2))

        @block.gpsimd
        def _(pool):
            make_identity(nc, pool, ident, s_const)
            pool.memset(half[:, :], -0.5).then_inc(s_const, 1)
            pool.memset(eps[:, :], EPS).then_inc(s_const, 1)
            pool.memset(zero[:, :], 0.0).then_inc(s_const, 1)
            pool.wait_ge(s_const, 5)
            pool.wait_ge(s_w, 16 * (K + 1))

            def body(s, b, live):
                c = 1 - b
                if live(0):
                    norm_rstd(pool, mv[b], ve, rstd[b], eps, half, s, s_mv, s_ve, s_rstd, s_h)
                    pool.wait_ge(s_adj[b], pair(s, b))
                    passed(pool, s_sel, s - 2, K)
                    passed(pool, s_lk, s - 2)
                    gate(pool, ptick, zero, s, s_gate)
                    for k in range(K):
                        pool.tensor_scalar(is_k[b][:, k, :, :], aj[b][:, :, :], float(k + 1), None,
                                           ALU.is_equal).then_inc(s_isk, 1)
                    pool.memset(sel[b][:, :, :], -BIG).then_inc(s_fill, 1)
                if live(1):
                    pool.wait_ge(s_xr[c], pair(s - 1, c))
                    passed(pool, s_xo, s - 3)
                    pool.tensor_tensor(xb[c][:, :, :], xr[c][:, :, :],
                                       brow[:, :].unsqueeze(1).to_broadcast([P, GT, D]), ALU.add).then_inc(s_xb, 1)

            pipeline(pool, G, 2, body)

        @block.scalar
        def _(act):
            act.wait_ge(s_w, 16 * (K + 1))

            def body(s, b, live):
                c = 1 - b
                if live(1):
                    passed(act, s_T, s - 1)
                    passed(act, s_E, s - 3)
                    act.activation(hT[c][:, :, :], T_ps[:, :, :], ACT.Copy).then_inc(s_hT, 1)
                    passed(act, s_hT, s - 1)
                    for k in range(K):
                        act.activation(hTa[c][:, k, :, :], hT[c][:, :, :], ACT.Copy,
                                       scale=acol[:, k:k + 1]).then_inc(s_hTa, 1)
                if live(2):
                    passed(act, s_AT, s - 2)
                    act.activation(alT[b][:, :, :], AT_ps[:, :, :], ACT.Copy).then_inc(s_alT, 1)
                if live(1):
                    passed(act, s_lk, s - 1)
                    passed(act, s_AT, s - 3)
                    act.activation(al[c][:, :, :], lk[c][:, :, :], ACT.Sigmoid).then_inc(s_al, 1)

            pipeline(act, G, 2, body)

        @block.vector
        def _(dve):
            def body(s, b, live):
                c = 1 - b
                if live(0):
                    dve.wait_ge(s_x[b], pair(s, b))
                    passed(dve, s_mv, s - 1, GT)
                    norm_stats(dve, xt[b], st, mv[b], tick, s, s_st, s_mv)
                if live(1):
                    passed(dve, s_isk, s - 1, K)
                    passed(dve, s_fill, s - 1)
                    passed(dve, s_E, s - 1)
                    for k in range(K):
                        if k:
                            within(dve, s_sel, s - 1, K, k)
                        dve.memset(tick[:, k + 1:k + 2], 0.0)
                        dve.copy_predicated(sel[c][:, :, :], is_k[c][:, k, :, :],
                                            E_ps[:, :, k, :]).then_inc(s_sel, 1)
                    passed(dve, s_sel, s - 1, K)
                    passed(dve, s_al, s - 3)
                    dve.scalar_tensor_tensor(out=lk[c][:, :, :], in0=sel[c][:, :, :], scalar=0.2,
                                             in1=sel[c][:, :, :], op0=ALU.mult, op1=ALU.max).then_inc(s_lk, 1)
                if live(0):
                    passed(dve, s_U, s - 2)
                    norm_apply(dve, xt[b], mv[b], rstd[b], h[b], s, s_rstd, s_h)
                if live(2):
                    passed(dve, s_U, s - 2)
                    passed(dve, s_xb, s - 2)
                    if not (isinstance(s, int) and s < 4):
                        dve.wait_ge(s_out[b], pair(s - 4, b))
                    dve.tensor_tensor(xo[b][:, :, :], U_ps[:, :, :], xb[b][:, :, :], ALU.add).then_inc(s_xo, 1)

            pipeline(dve, G, 2, body)

        @block.tensor
        def _(pe):
            pe.wait_ge(s_const, 2)

            def body(s, b, live):
                c = 1 - b
                if live(1):
                    passed(pe, s_h, s - 1, GT)
                    passed(pe, s_hT, s - 2)
                    for t in range(GT):
                        mm = pe.transpose(T_ps[:, t, :], h[c][:, t, :], ident[:, :])
                    mm.then_inc(s_T, 1)
                if live(2):
                    passed(pe, s_al, s - 2)
                    passed(pe, s_alT, s - 3)
                    for t in range(GT):
                        mm = pe.transpose(AT_ps[:, t, :], al[b][:, t, :], ident[:, :])
                    mm.then_inc(s_AT, 1)
                    passed(pe, s_alT, s - 2)
                    passed(pe, s_xo, s - 3)
                    for t in range(GT):
                        mm = pe.matmul(U_ps[:, t, :], alT[b][:, t, :], h[b][:, t, :], start=True, stop=True)
                    mm.then_inc(s_U, 1)
                if live(1):
                    passed(pe, s_hTa, s - 1, K)
                    passed(pe, s_sel, s - 2, K)
                    for t in range(GT):
                        mm = pe.matmul(E_ps[:, t, :, :], hT[c][:, t, :], hTa[c][:, :, t, :], start=True, stop=True)
                    mm.then_inc(s_E, 1)

            pipeline(pe, G, 2, body)


def mamba_block(nc, x, w_in, conv_w, conv_b, dt_bias, a_log, d_skip, norm_w, w_out, w_lin, b_lin, x4):
    B = x.shape[0]
    G = B // GT
    H = dt_bias.shape[0]
    DI = norm_w.shape[0]
    C = DI // P
    HC = H // C
    HD = DI // H
    NS = (conv_b.shape[0] - DI) // 2
    TAPS = conv_w.shape[1]
    DT0 = DI + conv_b.shape[0]
    xg, x4g = gather_view(x), gather_view(x4)
    with ExitStack() as ctx:
        m = Space(nc, ctx, "mb")
        sb, bank, sem = m.sb, m.bank, m.sem
        ident, ones = sb("ident", [P, P]), sb("ones", [P, P])
        upto = sb("upto", [P, P])
        above = sb("above", [P, P])
        half, eps, zero = sb("half", [P, GT]), sb("eps", [P, GT]), sb("zero", [P, GT])
        tick, ptick = sb("tick", [P, 8]), sb("ptick", [P, 1])
        win = sb("win", [P, w_in.shape[1]])
        cw, cb = sb("cw", [P, C + 1, TAPS]), sb("cb", [P, C + 1])
        dtb, alog, nega = sb("dtb", [P, H]), sb("alog", [P, H]), sb("nega", [P, H])
        dcol, nw = sb("dcol", [P, C]), sb("nw", [P, C])
        wout, woutT, wlin = sb("wout", [P, C, D]), sb("woutT", [P, C, P]), sb("wlin", [P, D])
        wol = sb("wol", [P, C, D])
        brow = sb("brow", [P, D])

        def two(name, shape):
            return [sb(f"{name}{b}", shape) for b in range(2)]

        xt, xr, xb, xo, h = (two(n, [P, GT, D]) for n in ("x", "xr", "xb", "xo", "h"))
        st, ve = sb("st", [P, GT, 6]), sb("ve", [P, GT])
        mv, rstd = two("mv", [P, GT, 2]), two("rstd", [P, GT])
        hT = two("hT", [P, GT, P])
        cv = [two(f"cv{j}_", [P, GT, P]) for j in range(C + 1)]
        xs = [two(f"xs{j}_", [P, GT, P]) for j in range(C)]
        bs, cs = two("bs", [NS, GT, P]), two("cs", [NS, GT, P])
        sz = [two(f"sz{j}_", [P, GT, P]) for j in range(C)]
        dr, dn, dm, du, dd, dq, dz, dz2, dp, dp2 = (
            sb(n, [P, GT, H]) for n in ("dr", "dn", "dm", "du", "dd", "dq", "dz", "dz2", "dp", "dp2"))
        dt, da = two("dt", [P, GT, H]), two("da", [P, GT, H])
        sg = two("sg", [P, GT, H, P])
        ls = two("ls", [P, GT, H, P])
        gm = two("gm", [P, GT, P])
        xdt = two("xdt", [P, GT, H, HD])
        y1 = [sb(f"y1_{j}", [P, GT, P]) for j in range(C)]
        y2 = [two(f"y2_{j}_", [P, GT, P]) for j in range(C)]
        sq = [sb(f"sq{j}", [P, GT, P]) for j in range(C)]
        vs, rr = sb("vs", [P, GT]), sb("rr", [P, GT])

        T_ps = bank("T", [P, GT, P])
        X_ps = [bank(f"X{j}", [P, GT, P]) for j in range(C + 1)]
        Y_ps = [bank(f"Y{j}", [P, GT, P]) for j in range(C)]
        R_ps = [bank(f"R{j}", [P, GT, P]) for j in range(2)]
        dt_ps = T_ps[:, 0, 0:GT * H].rearrange("p (t h) -> p t h", t=GT)

        s_w, s_const, s_prep = sem("w"), sem("const"), sem("prep")
        s_x, s_xr, s_out = ([sem(f"{n}{b}") for b in range(2)] for n in ("x", "xr", "out"))
        s_st, s_mv, s_ve, s_rstd, s_h = sem("st"), sem("mv"), sem("ve"), sem("rstd"), sem("h")
        (s_T, s_hT, s_X, s_cv, s_tap, s_dt, s_dn, s_du, s_dtc, s_da, s_sg, s_Z, s_sz, s_xs, s_seg, s_ls,
         s_G, s_gm, s_xT, s_xdt, s_m, s_Y, s_y1, s_y2, s_sq, s_O, s_SS, s_vs, s_rr, s_xb, s_xo, s_ol, s_dtr) = (
            sem(n) for n in ("T", "hT", "X", "cv", "tap", "dt", "dn", "du", "dtc", "da", "sg", "Z", "sz", "xs",
                             "seg", "ls", "G", "gm", "xT", "xdt", "m", "Y", "y1", "y2", "sq", "O", "SS", "vs",
                             "rr", "xb", "xo", "ol", "dtr"))
        N_W = 5 + (C + 1) * 2 + 2 * C + H
        DTC = 13
        NT = (C + 1) * (TAPS - 1)
        block = ctx.enter_context(nc.Block())

        @block.sync
        def _(sp):
            def col(dst, src):
                sp.dma_start(dst, src.rearrange("(p z) -> p z", z=1)).then_inc(s_w, 16)

            sp.dma_start(win[:, :], w_in).then_inc(s_w, 16)
            for j in range(C + 1):
                sp.dma_start(cw[:, j, :], conv_w[j * P:(j + 1) * P, :]).then_inc(s_w, 16)
                col(cb[:, j:j + 1], conv_b[j * P:(j + 1) * P])
            sp.dma_start(dtb[:, :], dt_bias.partition_broadcast(P)).then_inc(s_w, 16)
            sp.dma_start(alog[:, :], a_log.partition_broadcast(P)).then_inc(s_w, 16)
            for k in range(H):
                sp.dma_start(dcol[k % HC * HD:(k % HC + 1) * HD, k // HC:k // HC + 1],
                             d_skip[k:k + 1].partition_broadcast(HD)).then_inc(s_w, 16)
            for j in range(C):
                col(nw[:, j:j + 1], norm_w[j * P:(j + 1) * P])
                sp.dma_start(wout[:, j, :], w_out[j * P:(j + 1) * P, :]).then_inc(s_w, 16)
            sp.dma_start(wlin[:, :], w_lin).then_inc(s_w, 16)
            sp.dma_start(brow[:, :], b_lin.partition_broadcast(P)).then_inc(s_w, 16)

            def body(s, b, live):
                if live(0):
                    passed(sp, s_h, s - 2, GT)
                    sp.dma_start(xt[b][:, :, :], xg[s]).then_inc(s_x[b], 16)
                if live(3):
                    passed(sp, s_xb, s - 5)
                    sp.dma_start(xr[1 - b][:, :, :], xg[s - 3]).then_inc(s_xr[1 - b], 16)
                if live(4):
                    passed(sp, s_xo, s - 4, GT)
                    sp.dma_start(x4g[s - 4], xo[b][:, :, :]).then_inc(s_out[b], 16)

            pipeline(sp, G, 4, body)
            for b in range(2):
                sp.wait_ge(s_out[b], 16 * (G // 2))

        @block.gpsimd
        def _(pool):
            make_identity(nc, pool, ident, s_const)
            pool.memset(half[:, :], -0.5).then_inc(s_const, 1)
            pool.memset(eps[:, :], EPS).then_inc(s_const, 1)
            pool.memset(ones[:, :], 1.0).then_inc(s_const, 1)
            pool.wait_ge(s_const, 5)
            pool.affine_select(out=upto[:, :], in_=ones[:, :], compare_op=ALU.is_ge, fill=0.0, base=0,
                               pattern=[[1, P]], channel_multiplier=-1).then_inc(s_const, 1)
            pool.affine_select(out=above[:, :], in_=ones[:, :], compare_op=ALU.is_gt, fill=0.0, base=0,
                               pattern=[[-1, P]], channel_multiplier=1).then_inc(s_const, 1)
            pool.wait_ge(s_const, 7)
            pool.wait_ge(s_w, 16 * N_W)

            def body(s, b, live):
                c = 1 - b
                if live(0):
                    norm_rstd(pool, mv[b], ve, rstd[b], eps, half, s, s_mv, s_ve, s_rstd, s_h)
                if live(4):
                    passed(pool, s_vs, s - 4)
                    passed(pool, s_xo, s - 5, GT)
                    pool.tensor_tensor(rr[:, :], vs[:, :], half[:, :], ALU.pow).then_inc(s_rr, 1)
                if live(3):
                    pool.wait_ge(s_xr[c], pair(s - 3, c))
                    passed(pool, s_xo, s - 5, GT)
                    pool.tensor_tensor(xb[c][:, :, :], xr[c][:, :, :],
                                       brow[:, :].unsqueeze(1).to_broadcast([P, GT, D]), ALU.add).then_inc(s_xb, 1)
                if live(1):
                    passed(pool, s_da, s - 1)
                    passed(pool, s_seg, s - 3, GT)
                    pool.tensor_tensor(sg[c][:, :, :, :].rearrange("p t h l -> p (t h) l"),
                                       da[c][:, :, :].rearrange("p t h -> p (t h)").unsqueeze(2)
                                       .to_broadcast([P, GT * H, P]),
                                       upto[:, :].unsqueeze(1).to_broadcast([P, GT * H, P]),
                                       ALU.mult).then_inc(s_sg, 1)

            pipeline(pool, G, 4, body)

        @block.scalar
        def _(act):
            act.wait_ge(s_w, 16 * N_W)
            act.activation(nega[:, :], alog[:, :], ACT.Exp).then_inc(s_prep, 1)

            def body(s, b, live):
                c = 1 - b
                if live(1):
                    passed(act, s_T, s - 1)
                    passed(act, s_Z, s - 3)
                    act.activation(hT[c][:, :, :], T_ps[:, :, :], ACT.Copy).then_inc(s_hT, 1)
                if live(4):
                    passed(act, s_SS, s - 5)
                    for j in range(C):
                        within(act, s_y2, s - 4, C, j + 1)
                        act.activation(sq[j][:, :, :], y2[j][b][:, :, :], ACT.Square).then_inc(s_sq, 1)
                if live(2):
                    passed(act, s_Z, s - 2)
                    passed(act, s_y2, s - 4, C)
                    for j in range(C):
                        act.activation(sz[j][b][:, :, :], Y_ps[j][:, :, :], ACT.Silu).then_inc(s_sz, 1)
                    passed(act, s_tap, s - 2, NT)
                    passed(act, s_y1, s - 4, C)
                    for j in range(C):
                        act.activation(xs[j][b][:, :, :], cv[j][b][:, :, :], ACT.Silu).then_inc(s_xs, 1)
                    act.activation(bs[b][:, :, :], cv[C][b][0:NS, :, :], ACT.Silu).then_inc(s_xs, 1)
                    act.activation(cs[b][:, :, :], cv[C][b][NS:2 * NS, :, :], ACT.Silu).then_inc(s_xs, 1)
                if live(1):
                    passed(act, s_xs, s - 3, C + 2)
                    for j in range(C + 1):
                        within(act, s_X, s - 1, C + 1, j + 1)
                        act.activation(cv[j][c][:, :, :], X_ps[j][:, :, :], ACT.Identity,
                                       bias=cb[:, j:j + 1], scale=cw[:, j, TAPS - 1:TAPS]).then_inc(s_cv, 1)
                    passed(act, s_dn, s - 1)
                    act.activation(du[:, :, :], dn[:, :, :], ACT.Exp).then_inc(s_du, 1)
                if live(2):
                    passed(act, s_Y, s - 4)
                    for t in range(GT):
                        within(act, s_seg, s - 2, GT, t + 1)
                        act.activation(ls[b][:, t, :, :], R_ps[t % 2][:, :, :], ACT.Exp).then_inc(s_ls, 1)

            pipeline(act, G, 4, body)

        @block.vector
        def _(dve):
            dve.wait_ge(s_w, 16 * N_W)
            dve.wait_ge(s_prep, 1)
            dve.tensor_scalar(nega[:, :], nega[:, :], -1.0, None, ALU.mult).then_inc(s_prep, 1)
            dve.wait_ge(s_ol, 1)
            dve.tensor_copy(woutT[:, :, :], T_ps[:, 0:C, :]).then_inc(s_prep, 1)
            dve.wait_ge(s_ol, 2)
            for j in range(C):
                dve.tensor_scalar(wol[:, j, :], R_ps[0][:, j, :], nw[:, j:j + 1], None, ALU.mult).then_inc(s_prep, 1)
            dve.wait_ge(s_prep, 3 + C)
            dve.wait_ge(s_const, 7)

            def body(s, b, live):
                c = 1 - b

                def taps(k):
                    for j in range(C + 1):
                        if k == 1:
                            within(dve, s_cv, s - 1, C + 1, j + 1)
                        else:
                            within(dve, s_tap, s - 1, NT, (k - 2) * (C + 1) + j + 1)
                        dve.scalar_tensor_tensor(out=cv[j][c][:, :, k:P], in0=X_ps[j][:, :, 0:P - k],
                                                 scalar=cw[:, j, TAPS - 1 - k:TAPS - k],
                                                 in1=cv[j][c][:, :, k:P], op0=ALU.mult,
                                                 op1=ALU.add).then_inc(s_tap, 1)

                if live(0):
                    dve.wait_ge(s_x[b], pair(s, b))
                    passed(dve, s_mv, s - 1, GT)
                    norm_stats(dve, xt[b], st, mv[b], tick, s, s_st, s_mv)
                if live(3):
                    passed(dve, s_gm, s - 3)
                    passed(dve, s_ls, s - 3, GT)
                    dve.tensor_tensor(ls[c][:, :, :, :], ls[c][:, :, :, :],
                                      gm[c][:, :, :].unsqueeze(2).to_broadcast([P, GT, H, P]),
                                      ALU.mult).then_inc(s_m, 1)
                if live(1):
                    passed(dve, s_dt, s - 1)
                    dve.tensor_tensor(dr[:, :, :], dt_ps, dtb[:, :].unsqueeze(1).to_broadcast([P, GT, H]),
                                      ALU.add).then_inc(s_dtc, 1)
                    within(dve, s_dtc, s - 1, DTC, 1)
                    dve.scalar_tensor_tensor(out=dn[:, :, :], in0=dr[:, :, :], scalar=-1.0, in1=dr[:, :, :],
                                             op0=ALU.mult, op1=ALU.min).then_inc(s_dn, 1)
                    dve.tensor_scalar(dm[:, :, :], dr[:, :, :], 0.0, None, ALU.max).then_inc(s_dtc, 1)
                    taps(1)
                if live(4):
                    passed(dve, s_SS, s - 4)
                    passed(dve, s_rr, s - 5)
                    dve.tensor_scalar(vs[:, :], R_ps[1][:, 0, 0:GT], 1.0 / DI, EPS, ALU.mult,
                                      ALU.add).then_inc(s_vs, 1)
                if live(1):
                    taps(2)
                if live(4):
                    passed(dve, s_rr, s - 4)
                    passed(dve, s_O, s - 4)
                    passed(dve, s_xb, s - 4)
                    if not (isinstance(s, int) and s < 6):
                        dve.wait_ge(s_out[b], pair(s - 6, b))
                    for t in range(GT):
                        dve.scalar_tensor_tensor(out=xo[b][:, t, :], in0=R_ps[0][:, t, :], scalar=rr[:, t:t + 1],
                                                 in1=xb[b][:, t, :], op0=ALU.mult, op1=ALU.add).then_inc(s_xo, 1)
                if live(1):
                    taps(3)
                    passed(dve, s_du, s - 1)
                    dve.tensor_scalar(dd[:, :, :], du[:, :, :], 2.0, None, ALU.add).then_inc(s_dtc, 1)
                    within(dve, s_dtc, s - 1, DTC, 3)
                    dve.reciprocal(dq[:, :, :], dd[:, :, :]).then_inc(s_dtc, 1)
                    within(dve, s_dtc, s - 1, DTC, 4)
                    dve.tensor_tensor(dz[:, :, :], du[:, :, :], dq[:, :, :], ALU.mult).then_inc(s_dtc, 1)
                    within(dve, s_dtc, s - 1, DTC, 5)
                    dve.tensor_tensor(dz2[:, :, :], dz[:, :, :], dz[:, :, :], ALU.mult).then_inc(s_dtc, 1)
                    within(dve, s_dtc, s - 1, DTC, 6)
                    dve.tensor_scalar(dp[:, :, :], dz2[:, :, :], 1.0 / 13, None, ALU.mult).then_inc(s_dtc, 1)
                    for n, k in enumerate((11, 9, 7, 5, 3)):
                        src, dst = (dp, dp2) if n % 2 == 0 else (dp2, dp)
                        within(dve, s_dtc, s - 1, DTC, 7 + n)
                        dve.scalar_tensor_tensor(out=dst[:, :, :], in0=src[:, :, :], scalar=1.0 / k,
                                                 in1=dz2[:, :, :], op0=ALU.add, op1=ALU.mult).then_inc(s_dtc, 1)
                    within(dve, s_dtc, s - 1, DTC, 12)
                    dve.scalar_tensor_tensor(out=dp[:, :, :], in0=dp2[:, :, :], scalar=1.0, in1=dz[:, :, :],
                                             op0=ALU.add, op1=ALU.mult).then_inc(s_dtc, 1)
                    passed(dve, s_dtc, s - 1, DTC)
                    passed(dve, s_xdt, s - 3, C)
                    dve.scalar_tensor_tensor(out=dt[c][:, :, :], in0=dp[:, :, :], scalar=2.0, in1=dm[:, :, :],
                                             op0=ALU.mult, op1=ALU.add).then_inc(s_dtr, 1)
                    passed(dve, s_dtr, s - 1)
                    passed(dve, s_sg, s - 3)
                    dve.tensor_tensor(da[c][:, :, :], dt[c][:, :, :],
                                      nega[:, :].unsqueeze(1).to_broadcast([P, GT, H]), ALU.mult).then_inc(s_da, 1)
                if live(2):
                    passed(dve, s_G, s - 2)
                    passed(dve, s_m, s - 4)
                    dve.tensor_tensor(gm[b][:, :, :], R_ps[0][:, :, :],
                                      upto[:, :].unsqueeze(1).to_broadcast([P, GT, P]), ALU.mult).then_inc(s_gm, 1)
                    passed(dve, s_Y, s - 4)
                    for j in range(C):
                        within(dve, s_xT, s - 2, C, j + 1)
                        dve.tensor_tensor(xdt[b][:, :, j * HC:(j + 1) * HC, :],
                                          R_ps[1 - j][:, :, :].rearrange("p t (h d) -> p t h d", h=HC),
                                          dt[b][:, :, j * HC:(j + 1) * HC].unsqueeze(3)
                                          .to_broadcast([P, GT, HC, HD]), ALU.mult).then_inc(s_xdt, 1)
                if live(3):
                    passed(dve, s_Y, s - 3)
                    passed(dve, s_y2, s - 4, C)
                    for j in range(C):
                        dve.scalar_tensor_tensor(out=y1[j][:, :, :], in0=xs[j][c][:, :, :], scalar=dcol[:, j:j + 1],
                                                 in1=Y_ps[j][:, :, :], op0=ALU.mult, op1=ALU.add).then_inc(s_y1, 1)
                    passed(dve, s_O, s - 5)
                    passed(dve, s_sq, s - 5, C)
                    for j in range(C):
                        within(dve, s_y1, s - 3, C, j + 1)
                        dve.tensor_tensor(y2[j][c][:, :, :], y1[j][:, :, :], sz[j][c][:, :, :],
                                          ALU.mult).then_inc(s_y2, 1)
                if live(0):
                    passed(dve, s_T, s - 2)
                    norm_apply(dve, xt[b], mv[b], rstd[b], h[b], s, s_rstd, s_h)

            pipeline(dve, G, 4, body)

        @block.tensor
        def _(pe):
            pe.wait_ge(s_w, 16 * N_W)
            pe.wait_ge(s_const, 7)
            for j in range(C):
                mm = pe.transpose(T_ps[:, j, :], wout[:, j, :], ident[:, :])
            mm.then_inc(s_ol, 1)
            pe.wait_ge(s_prep, 3)
            for j in range(C):
                mm = pe.matmul(R_ps[0][:, j, :], woutT[:, j, :], wlin[:, :], start=True, stop=True)
            mm.then_inc(s_ol, 1)
            pe.wait_ge(s_prep, 3 + C)

            def body(s, b, live):
                c = 1 - b
                if live(1):
                    passed(pe, s_h, s - 1, GT)
                    passed(pe, s_dn, s - 2)
                    for t in range(GT):
                        mm = pe.transpose(T_ps[:, t, :], h[c][:, t, :], ident[:, :])
                    mm.then_inc(s_T, 1)
                if live(2):
                    passed(pe, s_y1, s - 4, C)
                    for j in range(C):
                        mm = pe.matmul(Y_ps[j][:, :, :], win[:, j * P:(j + 1) * P], hT[b][:, :, :],
                                       start=True, stop=True)
                    mm.then_inc(s_Z, 1)
                if live(1):
                    passed(pe, s_hT, s - 1)
                    passed(pe, s_tap, s - 2, NT)
                    for j in range(C + 1):
                        pe.matmul(X_ps[j][:, :, :], win[:, DI + j * P:DI + (j + 1) * P], hT[c][:, :, :],
                                  start=True, stop=True).then_inc(s_X, 1)
                    for t in range(GT):
                        mm = pe.matmul(dt_ps[:, t, :], hT[c][:, t, :], win[:, DT0:DT0 + H], start=True, stop=True)
                    mm.then_inc(s_dt, 1)
                if live(4):
                    passed(pe, s_sq, s - 4, C)
                    if live(3):
                        passed(pe, s_xdt, s - 3, C)
                    for t in range(GT):
                        for j in range(C):
                            mm = pe.matmul(R_ps[1][:, 0, t:t + 1], sq[j][:, t, :], ones[:, 0:1],
                                           start=(j == 0), stop=(j == C - 1))
                    mm.then_inc(s_SS, 1)
                    for t in range(GT):
                        for j in range(C):
                            mm = pe.matmul(R_ps[0][:, t, :], y2[j][b][:, t, :], wol[:, j, :],
                                           start=(j == 0), stop=(j == C - 1))
                    mm.then_inc(s_O, 1)
                if live(2):
                    passed(pe, s_sg, s - 2)
                    for t in range(GT):
                        if t >= 2:
                            within(pe, s_ls, s - 2, GT, t - 1)
                        elif t == 0:
                            passed(pe, s_xo, s - 4, GT)
                        else:
                            passed(pe, s_vs, s - 4)
                        if t < 2:
                            passed(pe, s_xdt, s - 3, C)
                        pe.matmul(R_ps[t % 2][:, :, :], above[:, :], sg[b][:, t, :, :],
                                  start=True, stop=True).then_inc(s_seg, 1)
                    passed(pe, s_xs, s - 2, C + 2)
                    within(pe, s_ls, s - 2, GT, GT - 1)
                    for t in range(GT):
                        mm = pe.matmul(R_ps[0][:, t, :], bs[b][:, t, :], cs[b][:, t, :], start=True, stop=True)
                    mm.then_inc(s_G, 1)
                    for j in range(C):
                        if j == 0:
                            passed(pe, s_ls, s - 2, GT)
                        else:
                            passed(pe, s_gm, s - 2)
                        for t in range(GT):
                            mm = pe.transpose(R_ps[1 - j][:, t, :], xs[j][b][:, t, :], ident[:, :])
                        mm.then_inc(s_xT, 1)
                if live(3):
                    passed(pe, s_m, s - 3)
                    passed(pe, s_xdt, s - 3, C)
                    passed(pe, s_y1, s - 4, C)
                    if live(2):
                        passed(pe, s_sz, s - 2, C)
                    for t in range(GT):
                        for k in range(H):
                            mm = pe.matmul(Y_ps[k // HC][k % HC * HD:(k % HC + 1) * HD, t, :], xdt[c][:, t, k, :],
                                           ls[c][:, t, k, :], start=True, stop=True)
                    mm.then_inc(s_Y, 1)

            pipeline(pe, G, 4, body)


_INS = ['x', 'adj', 'L0_gnn_W', 'L0_gnn_a', 'L0_ffn_W1', 'L0_ffn_b1', 'L0_ffn_Wg', 'L0_ffn_bg', 'L0_ffn_Wd', 'L0_ffn_bd',
        'L1_gnn_a0', 'L1_gnn_a1', 'L1_gnn_a2', 'L1_gnn_a3', 'L1_gnn_bias', 'L1_ffn_W_in', 'L1_ffn_conv_w',
        'L1_ffn_conv_b', 'L1_ffn_dt_bias', 'L1_ffn_A_log', 'L1_ffn_D', 'L1_ffn_norm_w', 'L1_ffn_W_out',
        'L1_ffn_W_lin', 'L1_ffn_b_lin']
_OUT = ((64, 128, 128), 'float32')


def build(nc, i, out):
    graphs, n_experts = i['x'].shape[0], i['L0_ffn_bd'].shape[0]

    def scratch(name, shape):
        return nc.dram_tensor(name, list(shape), F32, kind="Internal").ap()

    x1, x2, x3 = (scratch(n, (graphs, P, D)) for n in ("x1", "x2", "x3"))
    additive_attention(nc, i['x'], i['adj'], i['L0_gnn_W'], i['L0_gnn_a'], x1)
    with ExitStack() as ctx:
        rt = Routing(nc, ctx, graphs, n_experts)
        h_rows = scratch("h_rows", (graphs * P, D))
        sorted_rows, y_rows = (scratch(n, (rt.tiles * P, D)) for n in ("sorted_rows", "y_rows"))
        gates(nc, x1, i['L0_ffn_W1'], i['L0_ffn_b1'], i['L0_ffn_Wg'], i['L0_ffn_bg'], rt, h_rows)
        dispatch(nc, rt, h_rows, sorted_rows)
        experts(nc, i['L0_ffn_W1'], i['L0_ffn_b1'], i['L0_ffn_Wd'], i['L0_ffn_bd'], rt, sorted_rows, y_rows)
        combine(nc, x1, rt, y_rows, x2)
    typed_attention(nc, x2, i['adj'], [i[f'L1_gnn_a{k}'] for k in range(4)], i['L1_gnn_bias'], x3)
    mamba_block(nc, x3, *(i[f'L1_ffn_{n}'] for n in ('W_in', 'conv_w', 'conv_b', 'dt_bias', 'A_log', 'D',
                                                           'norm_w', 'W_out', 'W_lin', 'b_lin')), out)


def kernel(**inputs):
    import numpy as _np
    import concourse.bacc as _bacc
    from concourse import mybir as _mybir
    from concourse.bass_utils import run_bass_kernel_spmd as _run

    nc = _bacc.Bacc("TRN2", target_bir_lowering=False, num_devices=1)
    arrays, args = {}, {}
    for name in _INS:
        a = _np.ascontiguousarray(inputs[name])
        arrays[f"in_{name}_dram"] = a
        args[name] = nc.dram_tensor(f"in_{name}_dram", a.shape, _mybir.dt.from_np(a.dtype), kind="ExternalInput").ap()
    shape, dtype = _OUT
    out = nc.dram_tensor("out_0_dram", shape, _mybir.dt.from_np(_np.dtype(dtype)), kind="ExternalOutput").ap()
    build(nc, args, out)
    r = _run(nc, [arrays], core_ids=[0])
    return r.results[0]["out_0_dram"]
```

```python
from contextlib import ExitStack

import concourse.bass as bass
from concourse import mybir

F32 = mybir.dt.float32
I32 = mybir.dt.int32
ALU = mybir.AluOpType
ACT = mybir.ActivationFunctionType
AX = mybir.AxisListType.X

P = 128
D = 128
GT = 4
W = GT * P
EPS = 1e-5
NEG = -9e15
BIG = 3e38


class Space:

    def __init__(self, nc, ctx, tag):
        self.nc, self.ctx, self.tag, self.sems = nc, ctx, tag, []
        ctx.callback(self.end)

    def end(self):
        if self.sems:
            self.nc.clear_and_free_semaphores(self.sems)
            self.nc.all_engine_barrier()

    def sb(self, name, shape, dt=F32):
        return self.ctx.enter_context(self.nc.sbuf_tensor(f"{self.tag}_{name}", list(shape), dt))

    def bank(self, name, shape):
        return self.ctx.enter_context(self.nc.psum_tensor(f"{self.tag}_{name}", list(shape), F32))

    def sem(self, name):
        self.sems.append(self.nc.alloc_semaphore(name=f"{self.tag}_{name}"))
        return self.sems[-1]


def passed(eng, sem, q, n=1):
    if isinstance(q, int) and q < 0:
        return
    eng.wait_ge(sem, q * n + n)


def within(eng, sem, q, n, k):
    eng.wait_ge(sem, q * n + k)


def passed_half(eng, sem, q, n, k):
    if not (isinstance(q, int) and q < 0):
        within(eng, sem, q, n, k)


def pair(q, b):
    return (q - b) * 8 + 16


def pair_gt(q, b):
    return ((q - b) * 8 + 16) * GT


def pipeline(eng, groups, lags, body):
    head = (lags + 3) // 2 * 2
    tail = groups // 2 * 2

    def peeled(s):
        body(s, s % 2, lambda lag: 0 <= s - lag < groups)

    for s in range(head):
        peeled(s)
    with eng.Fori(head // 2, tail // 2) as i:
        for u in range(2):
            body(i * 2 + u, u, lambda lag: True)
    for s in range(tail, groups + lags):
        peeled(s)


def gate(pool, tick, zero, s, sem_gate):
    passed(pool, sem_gate, s - 1)
    pool.tensor_tensor(tick[:, :], zero[:, 0:1], zero[:, 0:1], ALU.add).then_inc(sem_gate, 1)


def gather_view(dram):
    return dram.rearrange("(g t) p d -> g p t d", t=GT)


def norm_stats(dve, x, st, mv, tick, s, sem_st, sem_mv):
    for t in range(GT):
        dve.bn_stats(st[:, t, :], x[:, t, :]).then_inc(sem_st, 1)
    passed(dve, sem_st, s, GT)
    dve.memset(tick[:, 0:1], 0.0)
    for t in range(GT):
        dve.bn_aggr(mv[:, t, :], st[:, t, :]).then_inc(sem_mv, 1)


def norm_rstd(pool, mv, ve, rstd, eps, half, s, sem_mv, sem_ve, sem_rstd, sem_h):
    passed(pool, sem_rstd, s - 1)
    passed(pool, sem_mv, s, GT)
    pool.tensor_tensor(ve[:, :], mv[:, :, 1], eps[:, :], ALU.add).then_inc(sem_ve, 1)
    passed(pool, sem_ve, s)
    passed(pool, sem_h, s - 2, GT)
    pool.tensor_tensor(rstd[:, :], ve[:, :], half[:, :], ALU.pow).then_inc(sem_rstd, 1)


def norm_apply(dve, x, mv, rstd, h, s, sem_rstd, sem_h):
    passed(dve, sem_rstd, s)
    for t in range(GT):
        dve.tensor_scalar(h[:, t, :], x[:, t, :], mv[:, t, 0:1], rstd[:, t:t + 1],
                          ALU.subtract, ALU.mult).then_inc(sem_h, 1)


def make_identity(nc, pool, ident, sem, n=0):
    pool.memset(ident[:, :], 0.0).then_inc(sem, 1)
    pool.wait_ge(sem, n + 1)
    pool.affine_select(out=ident[:, :], in_=ident[:, :], compare_op=ALU.not_equal, fill=1.0, base=0,
                       pattern=[[-1, P]], channel_multiplier=1).then_inc(sem, 1)


def additive_attention(nc, x, adj, w, a, x1):
    B = x.shape[0]
    G = B // GT
    xg, adjg, x1g = gather_view(x), gather_view(adj), gather_view(x1)
    with ExitStack() as ctx:
        m = Space(nc, ctx, "aa")
        sb, bank, sem = m.sb, m.bank, m.sem
        ident = sb("ident", [P, P])
        ones = sb("ones", [P, P])
        half, eps, zero = sb("half", [P, GT]), sb("eps", [P, GT]), sb("zero", [P, GT])
        tick, ptick = sb("tick", [P, 8]), sb("ptick", [P, 1])
        wn = sb("wn", [P, D])
        wt = sb("wt", [P, D])
        ab = sb("ab", [P, 2, P])
        acol = sb("acol", [P, 2])
        wab = sb("wab", [P, 2, P])
        xt = [sb(f"x{b}", [P, GT, D]) for b in range(2)]
        xr = [sb(f"xr{b}", [P, GT, D]) for b in range(2)]
        aj = [sb(f"adj{b}", [P, GT, P], I32) for b in range(2)]
        st = sb("st", [P, GT, 6])
        mv = [sb(f"mv{b}", [P, GT, 2]) for b in range(2)]
        ve = sb("ve", [P, GT])
        rstd = [sb(f"rstd{b}", [P, GT]) for b in range(2)]
        h = [sb(f"h{b}", [P, GT, D]) for b in range(2)]
        hT = [sb(f"hT{b}", [P, GT, P]) for b in range(2)]
        wh = [sb(f"wh{b}", [P, GT, D]) for b in range(2)]
        msk = [sb(f"msk{b}", [P, GT, P]) for b in range(2)]
        e = sb("e", [P, GT, P])
        em = [sb(f"em{b}", [P, GT, P]) for b in range(2)]
        mx = sb("mx", [P, GT])
        nmx = [sb(f"nmx{b}", [P, GT]) for b in range(2)]
        prob = [sb(f"prob{b}", [P, GT, P]) for b in range(2)]
        probT = [sb(f"probT{b}", [P, GT, P]) for b in range(2)]
        rden = [sb(f"rden{b}", [P, GT]) for b in range(2)]
        xo = [sb(f"xo{b}", [P, GT, D]) for b in range(2)]
        T_ps, PT_ps, E_ps, Wh_ps, U_ps = (bank(n, [P, GT, P]) for n in ("T", "PT", "E", "Wh", "U"))
        den_ps = bank("den", [P, 512])

        s_gate = sem("gate")
        s_w, s_const, s_wt, s_wtc, s_ab = sem("w"), sem("const"), sem("wt"), sem("wtc"), sem("ab")
        s_x = [sem(f"x{b}") for b in range(2)]
        s_xr = [sem(f"xr{b}") for b in range(2)]
        s_adj = [sem(f"adj{b}") for b in range(2)]
        s_out = [sem(f"out{b}") for b in range(2)]
        s_st, s_mv, s_ve, s_rstd, s_h = sem("st"), sem("mv"), sem("ve"), sem("rstd"), sem("h")
        s_T, s_hT, s_E, s_e, s_msk, s_em, s_mx, s_nmx, s_prob = (
            sem(n) for n in ("T", "hT", "E", "e", "msk", "em", "mx", "nmx", "prob"))
        s_Wh, s_wh, s_PT, s_probT, s_den, s_U, s_rden, s_xo = (
            sem(n) for n in ("Wh", "wh", "PT", "probT", "den", "U", "rden", "xo"))
        block = ctx.enter_context(nc.Block())

        @block.sync
        def _(sp):
            sp.dma_start(wn[:, :], w).then_inc(s_w, 16)
            sp.dma_start(acol[:, :], a.rearrange("(k p) z -> p (k z)", p=P),
                         allow_slow_non_contiguous=True).then_inc(s_w, 16)

            def body(s, b, live):
                if live(0):
                    passed(sp, s_h, s - 2, GT)
                    sp.dma_start(xt[b][:, :, :], xg[s]).then_inc(s_x[b], 16)
                    passed(sp, s_msk, s - 2)
                    sp.dma_start(aj[b][:, :, :], adjg[s]).then_inc(s_adj[b], 16)
                if live(2):
                    passed(sp, s_xo, s - 4, GT)
                    sp.dma_start(xr[b][:, :, :], xg[s - 2]).then_inc(s_xr[b], 16)
                if live(3):
                    passed(sp, s_xo, s - 3, GT)
                    sp.dma_start(x1g[s - 3], xo[1 - b][:, :, :]).then_inc(s_out[1 - b], 16)

            pipeline(sp, G, 3, body)
            for b in range(2):
                sp.wait_ge(s_out[b], 16 * (G // 2))

        @block.gpsimd
        def _(pool):
            make_identity(nc, pool, ident, s_const)
            pool.memset(ones[:, :], 1.0).then_inc(s_const, 1)
            pool.memset(half[:, :], -0.5).then_inc(s_const, 1)
            pool.memset(eps[:, :], EPS).then_inc(s_const, 1)
            pool.memset(zero[:, :], 0.0).then_inc(s_const, 1)
            pool.wait_ge(s_const, 6)

            def body(s, b, live):
                c = 1 - b
                if live(1):
                    pool.wait_ge(s_adj[c], pair(s - 1, c))
                    passed(pool, s_e, s - 3)
                    gate(pool, ptick, zero, s - 1, s_gate)
                    pool.tensor_scalar(msk[c][:, :, :], aj[c][:, :, :], 0.0, None, ALU.is_le).then_inc(s_msk, 1)
                if live(0):
                    norm_rstd(pool, mv[b], ve, rstd[b], eps, half, s, s_mv, s_ve, s_rstd, s_h)

            pipeline(pool, G, 3, body)

        @block.scalar
        def _(act):
            def body(s, b, live):
                c = 1 - b
                if live(3):
                    passed(act, s_PT, s - 3)
                    passed(act, s_U, s - 5)
                    act.activation(probT[c][:, :, :], PT_ps[:, :, :], ACT.Copy).then_inc(s_probT, 1)
                if live(1):
                    passed(act, s_T, s - 1)
                    passed(act, s_Wh, s - 3)
                    act.activation(hT[c][:, :, :], T_ps[:, :, :], ACT.Copy).then_inc(s_hT, 1)
                if live(2):
                    passed(act, s_Wh, s - 2)
                    passed(act, s_U, s - 4)
                    act.activation(wh[b][:, :, :], Wh_ps[:, :, :], ACT.Copy).then_inc(s_wh, 1)
                    passed(act, s_nmx, s - 2)
                    passed(act, s_PT, s - 4)
                    for t in range(GT):
                        act.activation(prob[b][:, t, :], em[b][:, t, :], ACT.Exp,
                                       bias=nmx[b][:, t:t + 1]).then_inc(s_prob, 1)

            pipeline(act, G, 3, body)

        @block.vector
        def _(dve):
            dve.wait_ge(s_w, 32)
            dve.wait_ge(s_const, 3)
            for k in range(2):
                dve.tensor_scalar(ab[:, k, :], ones[:, :], acol[:, k:k + 1], None, ALU.mult).then_inc(s_ab, 1)
            dve.wait_ge(s_wt, 1)
            dve.tensor_copy(wt[:, :], T_ps[:, 0, :]).then_inc(s_wtc, 1)
            dve.wait_ge(s_wt, 2)
            dve.tensor_copy(wab[:, :, :], E_ps[:, 0:2, :]).then_inc(s_wtc, 1)

            def body(s, b, live):
                c = 1 - b
                if live(1):
                    passed(dve, s_T, s - 3)
                    norm_apply(dve, xt[c], mv[c], rstd[c], h[c], s - 1, s_rstd, s_h)
                if live(2):
                    passed(dve, s_E, s - 2)
                    passed(dve, s_msk, s - 2)
                    dve.scalar_tensor_tensor(out=e[:, :, :], in0=msk[b][:, :, :], scalar=NEG,
                                             in1=E_ps[:, :, :], op0=ALU.mult, op1=ALU.add).then_inc(s_e, 1)
                    passed(dve, s_e, s - 2)
                    passed(dve, s_prob, s - 4, GT)
                    dve.scalar_tensor_tensor(out=em[b][:, :, :], in0=e[:, :, :], scalar=0.2,
                                             in1=e[:, :, :], op0=ALU.mult, op1=ALU.max).then_inc(s_em, 1)
                    passed(dve, s_em, s - 2)
                    dve.tensor_reduce(mx[:, :], em[b][:, :, :], AX, ALU.max).then_inc(s_mx, 1)
                    passed(dve, s_mx, s - 2)
                    dve.tensor_scalar(nmx[b][:, :], mx[:, :], -1.0, None, ALU.mult).then_inc(s_nmx, 1)
                if live(0):
                    dve.wait_ge(s_x[b], pair(s, b))
                    passed(dve, s_mv, s - 1, GT)
                    norm_stats(dve, xt[b], st, mv[b], tick, s, s_st, s_mv)
                if live(3):
                    passed(dve, s_den, s - 3)
                    dve.reciprocal(rden[c][:, :], den_ps[:, 0:GT]).then_inc(s_rden, 1)
                    passed(dve, s_rden, s - 3)
                    passed(dve, s_U, s - 3)
                    dve.wait_ge(s_xr[c], pair(s - 3, c))
                    if not (isinstance(s, int) and s < 5):
                        dve.wait_ge(s_out[c], pair(s - 5, c))
                    for t in range(GT):
                        dve.scalar_tensor_tensor(out=xo[c][:, t, :], in0=U_ps[:, t, :],
                                                 scalar=rden[c][:, t:t + 1], in1=xr[c][:, t, :],
                                                 op0=ALU.mult, op1=ALU.add).then_inc(s_xo, 1)

            pipeline(dve, G, 3, body)

        @block.tensor
        def _(pe):
            pe.wait_ge(s_w, 32)
            pe.wait_ge(s_const, 2)
            pe.transpose(T_ps[:, 0, :], wn[:, :], ident[:, :]).then_inc(s_wt, 1)
            pe.wait_ge(s_ab, 2)
            pe.matmul(E_ps[:, 0:2, :], wn[:, :], ab[:, :, :], start=True, stop=True).then_inc(s_wt, 1)
            pe.wait_ge(s_wtc, 2)

            def body(s, b, live):
                c = 1 - b
                if live(3):
                    passed(pe, s_prob, s - 3, GT)
                    passed(pe, s_probT, s - 4)
                    for t in range(GT):
                        mm = pe.transpose(PT_ps[:, t, :], prob[c][:, t, :], ident[:, :])
                    mm.then_inc(s_PT, 1)
                if live(2):
                    passed(pe, s_hT, s - 2)
                    passed(pe, s_e, s - 3)
                    pe.matmul(E_ps[:, :, :], wab[:, 1, :], hT[b][:, :, :], start=True, stop=False)
                    for t in range(GT):
                        mm = pe.matmul(E_ps[:, t, :], hT[b][:, t, :], wab[:, 0, :], start=False, stop=(t == GT - 1))
                    mm.then_inc(s_E, 1)
                if live(1):
                    passed(pe, s_h, s - 1, GT)
                    passed(pe, s_hT, s - 2)
                    for t in range(GT):
                        mm = pe.transpose(T_ps[:, t, :], h[c][:, t, :], ident[:, :])
                    mm.then_inc(s_T, 1)
                if live(2):
                    passed(pe, s_hT, s - 2)
                    passed(pe, s_wh, s - 3)
                    for t in range(GT):
                        mm = pe.matmul(Wh_ps[:, t, :], hT[b][:, t, :], wt[:, :], start=True, stop=True)
                    mm.then_inc(s_Wh, 1)
                if live(3):
                    passed(pe, s_probT, s - 3)
                    passed(pe, s_rden, s - 4)
                    for t in range(GT):
                        mm = pe.matmul(den_ps[:, t:t + 1], probT[c][:, t, :], ones[:, 0:1], start=True, stop=True)
                    mm.then_inc(s_den, 1)
                    passed(pe, s_wh, s - 3)
                    passed(pe, s_xo, s - 4, GT)
                    for t in range(GT):
                        mm = pe.matmul(U_ps[:, t, :], probT[c][:, t, :], wh[c][:, t, :], start=True, stop=True)
                    mm.then_inc(s_U, 1)

            pipeline(pe, G, 3, body)

class Routing:

    def __init__(self, nc, ctx, graphs, experts):
        m = Space(nc, ctx, "rt")
        self.tiles = graphs + experts
        self.tiles += -self.tiles % (2 * GT)
        self.ptop = m.sb("ptop", [P, graphs])
        self.row = m.sb("row", [P, graphs], I32)
        self.expert = m.sb("expert", [P, self.tiles], I32)
        self.node = m.sb("node", [P, self.tiles], I32)


def gates(nc, x1, w1, b1, wg, bg, rt, h_rows):
    B = x1.shape[0]
    G = B // GT
    E = bg.shape[0]
    C = w1.shape[1] // P
    xg, hg = gather_view(x1), h_rows.rearrange("(g t p) d -> g p t d", t=GT, p=P)
    with ExitStack() as ctx:
        m = Space(nc, ctx, "ga")
        sb, bank, sem = m.sb, m.bank, m.sem
        ident, ones = sb("ident", [P, P]), sb("ones", [P, P])
        before = sb("before", [P, P])
        half, eps = sb("half", [P, GT]), sb("eps", [P, GT])
        tick = sb("tick", [P, 8])
        w1s, b1s = sb("w1s", [P, C * P]), sb("b1s", [P, C])
        wgs, bgs = sb("wgs", [P, C, E]), sb("bgs", [E, 1])
        xt = [sb(f"x{b}", [P, GT, D]) for b in range(2)]
        st, ve = sb("st", [P, GT, 6]), sb("ve", [P, GT])
        mv = [sb(f"mv{b}", [P, GT, 2]) for b in range(2)]
        rstd = [sb(f"rstd{b}", [P, GT]) for b in range(2)]
        h = [sb(f"h{b}", [P, GT, D]) for b in range(2)]
        hT = [sb(f"hT{b}", [P, GT, P]) for b in range(2)]
        HT = [sb(f"HT{b}", [P, C, GT, P]) for b in range(2)]
        lg, lgT = sb("lg", [P, B, E]), sb("lgT", [E, GT, P])
        iota_e, iota_j = sb("iota_e", [P, B, E]), sb("iota_j", [P, rt.tiles, E])
        top, ex, first, oh = (sb(n, [P, B, E]) for n in ("top", "ex", "first", "oh"))
        mx, den, idx, pos = (sb(n, [P, B]) for n in ("mx", "den", "idx", "pos"))
        inc, off = sb("inc", [P, B, E]), sb("off", [P, B, E])
        cnt_i, pad_i = sb("cnt_i", [P, E], I32), sb("pad_i", [P, E], I32)
        pad, end, start = sb("pad", [P, E]), sb("end", [P, E]), sb("start", [P, E])
        full, tex = sb("full", [P, rt.tiles, E]), sb("tex", [P, rt.tiles])
        hi_i, lo_i = sb("hi_i", [P, B], I32), sb("lo_i", [P, B], I32)
        hi, lo, nid = sb("hi", [P, B]), sb("lo", [P, B]), sb("nid", [P, B])
        iota_p, iota_t = sb("iota_p", [P, P]), sb("iota_t", [P, rt.tiles])
        at_row = sb("at_row", [P, B, P])
        at_tile = sb("at_tile", [P, B, rt.tiles])
        T_ps = bank("T", [P, GT, P])
        G_ps = [bank(f"G{c}", [P, GT, P]) for c in range(C)]
        L_ps, N_ps = bank("L", [P, GT, P]), bank("N", [P, GT, E])

        s_w, s_const = sem("w"), sem("const")
        s_x, s_hd = [sem(f"x{b}") for b in range(2)], [sem(f"hd{b}") for b in range(2)]
        s_st, s_mv, s_ve, s_rstd, s_h = sem("st"), sem("mv"), sem("ve"), sem("rstd"), sem("h")
        s_T, s_hT, s_G, s_HT, s_L, s_lgT, s_N, s_lg = (
            sem(n) for n in ("T", "hT", "G", "HT", "L", "lgT", "N", "lg"))
        s_r, s_max, s_ex, s_cnt, s_oh = sem("r"), sem("max"), sem("ex"), sem("cnt"), sem("oh")
        s_hilo, s_atr, s_att, s_att_pool, s_inv = (sem(n) for n in ("hilo", "atr", "att", "att_pool", "inv"))
        CH = 8
        ON_POOL = 5
        block = ctx.enter_context(nc.Block())

        @block.sync
        def _(sp):
            sp.dma_start(w1s[:, :], w1).then_inc(s_w, 16)
            for c in range(C):
                sp.dma_start(b1s[:, c:c + 1], b1[c * P:(c + 1) * P].rearrange("(p z) -> p z", z=1)).then_inc(s_w, 16)
            sp.dma_start(wgs[:, :, :], wg.rearrange("(c p) e -> p c e", p=P)).then_inc(s_w, 16)
            sp.dma_start(bgs[:, :], bg.rearrange("(p z) -> p z", z=1)).then_inc(s_w, 16)

            def body(s, b, live):
                if live(0):
                    passed(sp, s_h, s - 2, GT)
                    sp.dma_start(xt[b][:, :, :], xg[s]).then_inc(s_x[b], 16)
                if live(1):
                    passed(sp, s_h, s - 1, GT)
                    sp.dma_start(hg[s - 1], h[1 - b][:, :, :]).then_inc(s_hd[1 - b], 16)

            pipeline(sp, G, 4, body)
            for b in range(2):
                sp.wait_ge(s_hd[b], 16 * (G // 2))

        @block.gpsimd
        def _(pool):
            make_identity(nc, pool, ident, s_const)
            pool.memset(half[:, :], -0.5).then_inc(s_const, 1)
            pool.memset(eps[:, :], EPS).then_inc(s_const, 1)
            pool.memset(ones[:, :], 1.0).then_inc(s_const, 1)
            pool.wait_ge(s_const, 5)
            pool.affine_select(out=before[:, :], in_=ones[:, :], compare_op=ALU.is_gt, fill=0.0, base=0,
                               pattern=[[1, P]], channel_multiplier=-1).then_inc(s_const, 1)
            pool.iota(iota_e[:, :, :], pattern=[[0, B], [1, E]], base=0, channel_multiplier=0,
                      allow_small_or_imprecise_dtypes=True).then_inc(s_const, 1)
            pool.iota(iota_j[:, :, :], pattern=[[P, rt.tiles], [0, E]], base=0, channel_multiplier=0,
                      allow_small_or_imprecise_dtypes=True).then_inc(s_const, 1)
            pool.iota(iota_p[:, :], pattern=[[1, P]], base=0, channel_multiplier=0,
                      allow_small_or_imprecise_dtypes=True).then_inc(s_const, 1)
            pool.iota(iota_t[:, :], pattern=[[1, rt.tiles]], base=0, channel_multiplier=0,
                      allow_small_or_imprecise_dtypes=True).then_inc(s_const, 1)
            pool.iota(nid[:, :], pattern=[[P, B]], base=0, channel_multiplier=1,
                      allow_small_or_imprecise_dtypes=True).then_inc(s_const, 1)
            pool.wait_ge(s_const, 11)

            def body(s, b, live):
                if live(0):
                    norm_rstd(pool, mv[b], ve, rstd[b], eps, half, s, s_mv, s_ve, s_rstd, s_h)

            pipeline(pool, G, 4, body)
            pool.wait_ge(s_hilo, 2)
            for c in range(B // CH):
                for t in range(c * CH, c * CH + ON_POOL):
                    pool.tensor_scalar(at_tile[:, t, :], iota_t[:, :], hi[:, t:t + 1], nid[:, t:t + 1],
                                       ALU.is_equal, ALU.mult).then_inc(s_att_pool, 1)

        @block.scalar
        def _(act):
            act.wait_ge(s_w, 16 * (C + 3))

            def body(s, b, live):
                c = 1 - b
                if live(1):
                    passed(act, s_T, s - 1)
                    passed(act, s_G, s - 3, C)
                    act.activation(hT[c][:, :, :], T_ps[:, :, :], ACT.Copy).then_inc(s_hT, 1)
                if live(2):
                    passed(act, s_L, s - 4)
                    for k in range(C):
                        within(act, s_G, s - 2, C, k + 1)
                        act.activation(HT[b][:, k, :, :], G_ps[k][:, :, :], ACT.Gelu,
                                       bias=b1s[:, k:k + 1]).then_inc(s_HT, 1)

            pipeline(act, G, 4, body)
            act.wait_ge(s_max, 1)
            act.activation(ex[:, :, :], top[:, :, :], ACT.Exp).then_inc(s_ex, 1)

        @block.vector
        def _(dve):
            dve.wait_ge(s_w, 16 * (C + 3))
            dve.wait_ge(s_const, 11)

            def body(s, b, live):
                c = 1 - b
                if live(1):
                    passed(dve, s_T, s - 3)
                    if not (isinstance(s, int) and s < 3):
                        dve.wait_ge(s_hd[c], pair(s - 3, c))
                    norm_apply(dve, xt[c], mv[c], rstd[c], h[c], s - 1, s_rstd, s_h)
                if live(0):
                    dve.wait_ge(s_x[b], pair(s, b))
                    passed(dve, s_mv, s - 1, GT)
                    norm_stats(dve, xt[b], st, mv[b], tick, s, s_st, s_mv)
                if live(4):
                    passed(dve, s_N, s - 4)
                    dve.tensor_copy(lg[:, bass.ts(s - 4, GT), :], N_ps[:, :, :]).then_inc(s_lg, 1)
                if live(3):
                    passed(dve, s_L, s - 3)
                    passed(dve, s_N, s - 4)
                    dve.tensor_tensor(lgT[:, :, :], L_ps[0:E, :, :],
                                      bgs[:, 0:1].unsqueeze(2).to_broadcast([E, GT, P]), ALU.add).then_inc(s_lgT, 1)

            pipeline(dve, G, 4, body)

            n = [0]

            def then(ins):
                n[0] += 1
                ins.then_inc(s_r, 1)
                dve.wait_ge(s_r, n[0])

            dve.wait_ge(s_lg, G)
            then(dve.tensor_reduce(mx[:, :], lg[:, :, :], AX, ALU.max))
            mx_e = mx[:, :].unsqueeze(2).to_broadcast([P, B, E])
            dve.tensor_tensor(top[:, :, :], lg[:, :, :], mx_e, ALU.subtract).then_inc(s_max, 1)
            then(dve.tensor_tensor(oh[:, :, :], lg[:, :, :], mx_e, ALU.is_equal))
            then(dve.scalar_tensor_tensor(out=first[:, :, :], in0=oh[:, :, :], scalar=-float(E),
                                          in1=iota_e[:, :, :], op0=ALU.mult, op1=ALU.add))
            then(dve.tensor_reduce(idx[:, :], first[:, :, :], AX, ALU.min))
            dve.tensor_tensor(oh[:, :, :], first[:, :, :], idx[:, :].unsqueeze(2).to_broadcast([P, B, E]),
                              ALU.is_equal).then_inc(s_oh, 1)
            dve.wait_ge(s_ex, 1)
            then(dve.tensor_reduce(den[:, :], ex[:, :, :], AX, ALU.add))
            then(dve.reciprocal(rt.ptop[:, :], den[:, :]))
            dve.wait_ge(s_cnt, 2)
            for k in range(E):
                sc = dve.tensor_tensor_scan(inc[:, :, k], ones[:, 0:B], G_ps[0][:, :, :].rearrange(
                    "p t (u e) -> p (t u) e", e=E)[:, :, k], 0.0, ALU.mult, ALU.add)
            then(sc)
            then(dve.tensor_tensor(off[:, :, :], inc[:, :, :], G_ps[0][:, :, :].rearrange(
                "p t (u e) -> p (t u) e", e=E), ALU.subtract))
            then(dve.tensor_tensor(off[:, :, :], off[:, :, :], G_ps[1][:, :, :].rearrange(
                "p t (u e) -> p (t u) e", e=E), ALU.add))
            then(dve.tensor_scalar(cnt_i[:, :], inc[:, B - 1, :], float(P - 1), None, ALU.add))
            shift = P.bit_length() - 1
            then(dve.tensor_scalar(pad_i[:, :], cnt_i[:, :], shift, shift, ALU.arith_shift_right,
                                   ALU.arith_shift_left))
            then(dve.tensor_copy(pad[:, :], pad_i[:, :]))
            then(dve.tensor_tensor_scan(end[:, :], ones[:, 0:E], pad[:, :], 0.0, ALU.mult, ALU.add))
            then(dve.tensor_tensor(start[:, :], end[:, :], pad[:, :], ALU.subtract))
            then(dve.tensor_tensor(off[:, :, :], off[:, :, :], start[:, :].unsqueeze(1).to_broadcast([P, B, E]),
                                   ALU.add))
            then(dve.tensor_tensor(off[:, :, :], off[:, :, :], oh[:, :, :], ALU.mult))
            then(dve.tensor_reduce(pos[:, :], off[:, :, :], AX, ALU.add))
            then(dve.tensor_copy(rt.row[:, :], pos[:, :]))
            then(dve.tensor_scalar(hi_i[:, :], rt.row[:, :], shift, None, ALU.arith_shift_right))
            dve.tensor_copy(hi[:, :], hi_i[:, :]).then_inc(s_hilo, 1)
            then(dve.tensor_scalar(lo_i[:, :], rt.row[:, :], P - 1, None, ALU.bitwise_and))
            dve.tensor_copy(lo[:, :], lo_i[:, :]).then_inc(s_hilo, 1)
            dve.wait_ge(s_hilo, 2)
            for c in range(B // CH):
                g = slice(c * CH, (c + 1) * CH)
                dve.tensor_tensor(at_row[:, g, :], iota_p[:, :].unsqueeze(1).to_broadcast([P, CH, P]),
                                  lo[:, g].unsqueeze(2).to_broadcast([P, CH, P]), ALU.is_equal).then_inc(s_atr, 1)
                for t in range(c * CH + ON_POOL, (c + 1) * CH):
                    dve.tensor_scalar(at_tile[:, t, :], iota_t[:, :], hi[:, t:t + 1], nid[:, t:t + 1],
                                      ALU.is_equal, ALU.mult).then_inc(s_att, 1)
            then(dve.tensor_tensor(full[:, :, :], end[:, :].unsqueeze(1).to_broadcast([P, rt.tiles, E]),
                                   iota_j[:, :, :], ALU.is_le))
            then(dve.tensor_reduce(tex[:, :], full[:, :, :], AX, ALU.add))
            then(dve.tensor_scalar(rt.expert[:, :], tex[:, :], float(E - 1), None, ALU.min))
            dve.wait_ge(s_inv, 1)
            dve.tensor_copy(rt.node[:, :], L_ps[:, 0, 0:rt.tiles])

        @block.tensor
        def _(pe):
            pe.wait_ge(s_w, 16 * (C + 3))
            pe.wait_ge(s_const, 6)

            def body(s, b, live):
                c = 1 - b
                if live(1):
                    passed(pe, s_h, s - 1, GT)
                    passed(pe, s_hT, s - 2)
                    for t in range(GT):
                        mm = pe.transpose(T_ps[:, t, :], h[c][:, t, :], ident[:, :])
                    mm.then_inc(s_T, 1)
                if live(3):
                    passed(pe, s_HT, s - 3, C)
                    passed(pe, s_lgT, s - 4)
                    for k in range(C):
                        mm = pe.matmul(L_ps[0:E, :, :], wgs[:, k, :], HT[c][:, k, :, :], start=(k == 0), stop=(k == C - 1))
                    mm.then_inc(s_L, 1)
                if live(2):
                    passed(pe, s_hT, s - 2)
                    for k in range(C):
                        passed_half(pe, s_HT, s - 3, C, k + 1)
                        pe.matmul(G_ps[k][:, :, :], w1s[:, k * P:(k + 1) * P], hT[b][:, :, :],
                                  start=True, stop=True).then_inc(s_G, 1)
                if live(3):
                    passed(pe, s_lgT, s - 3)
                    passed(pe, s_lg, s - 4)
                    for t in range(GT):
                        mm = pe.matmul(N_ps[:, t, :], lgT[:, t, :], ident[0:E, 0:E], start=True, stop=True)
                    mm.then_inc(s_N, 1)

            pipeline(pe, G, 4, body)
            pe.wait_ge(s_oh, 1)
            oh2 = oh[:, :, :].rearrange("p t e -> p (t e)")
            flat = [g[:, :, :].rearrange("p t d -> p (t d)") for g in G_ps]
            pe.matmul(flat[0], ones[:, :], oh2, start=True, stop=True).then_inc(s_cnt, 1)
            pe.matmul(flat[1], before[:, :], oh2, start=True, stop=True).then_inc(s_cnt, 1)
            for c in range(B // CH):
                pe.wait_ge(s_atr, c + 1)
                pe.wait_ge(s_att, (c + 1) * (CH - ON_POOL))
                pe.wait_ge(s_att_pool, (c + 1) * ON_POOL)
                for t in range(c * CH, (c + 1) * CH):
                    mm = pe.matmul(L_ps[:, 0, 0:rt.tiles], at_row[:, t, :], at_tile[:, t, :],
                                   start=(t == 0), stop=(t == B - 1))
            mm.then_inc(s_inv, 1)


def experts(nc, w1, b1, wd, bd, rt, h_rows, y_rows):
    G = rt.tiles // GT
    E = bd.shape[0]
    C = w1.shape[1] // P
    yg = y_rows.rearrange("(g t p) d -> g p t d", t=GT, p=P)
    with ExitStack() as ctx:
        m = Space(nc, ctx, "ex")
        sb, bank, sem = m.sb, m.bank, m.sem
        ident, ones = sb("ident", [P, P]), sb("ones", [1, P])
        w1s, b1s = sb("w1s", [P, C * P]), sb("b1s", [P, C])
        wds, bds = sb("wds", [P, C, E * D]), sb("bds", [1, E * D])
        h = [sb(f"h{b}", [P, GT, D]) for b in range(2)]
        hT = [sb(f"hT{b}", [P, GT, P]) for b in range(2)]
        HT = [sb(f"HT{b}", [P, C, GT, P]) for b in range(2)]
        y = [sb(f"y{b}", [P, GT, D]) for b in range(2)]
        T_ps, Y_ps = bank("T", [P, GT, P]), bank("Y", [P, GT, D])
        G_ps = [bank(f"G{c}", [P, GT, P]) for c in range(C)]
        node = [sb(f"node{b}", [P, GT], I32) for b in range(2)]
        zero, ptick = sb("zero", [P, 1]), sb("ptick", [P, 1])
        s_w, s_const, s_gate, s_node = sem("w"), sem("const"), sem("gate"), sem("node")
        s_hl, s_out = [sem(f"hl{b}") for b in range(2)], [sem(f"out{b}") for b in range(2)]
        s_T, s_hT, s_G, s_HT, s_Y, s_y = (sem(n) for n in ("T", "hT", "G", "HT", "Y", "y"))
        N_W = 2 + 2 * C
        block = ctx.enter_context(nc.Block())

        @block.sync
        def _(sp):
            def body(s, b, live):
                if live(3):
                    passed(sp, s_y, s - 3)
                    sp.dma_start(yg[s - 3], y[1 - b][:, :, :]).then_inc(s_out[1 - b], 16)

            pipeline(sp, G, 3, body)
            for b in range(2):
                sp.wait_ge(s_out[b], 16 * (G // 2))

        @block.gpsimd
        def _(pool):
            make_identity(nc, pool, ident, s_const)
            pool.memset(ones[:, :], 1.0).then_inc(s_const, 1)
            pool.memset(zero[:, :], 0.0).then_inc(s_const, 1)
            pool.wait_ge(s_const, 4)

            def body(s, b, live):
                if live(0):
                    passed(pool, s_node, s)
                    passed(pool, s_T, s - 2)
                    gate(pool, ptick, zero, s, s_gate)
                    for t in range(GT):
                        pool.indirect_dma_start(h[b][:, t, :], None, h_rows,
                                                bass.IndirectOffsetOnAxis(node[b][:, t:t + 1], 0)).then_inc(s_hl[b], 16)

            pipeline(pool, G, 3, body)

        @block.scalar
        def _(act):
            act.dma_start(w1s[:, :], w1).then_inc(s_w, 16)
            for c in range(C):
                act.dma_start(b1s[:, c:c + 1], b1[c * P:(c + 1) * P].rearrange("(p z) -> p z", z=1)).then_inc(s_w, 16)
                act.dma_start(wds[:, c, :].rearrange("p (e d) -> p e d", e=E),
                              wd[:, c * P:(c + 1) * P, :].rearrange("e p d -> p e d")).then_inc(s_w, 16)
            act.dma_start(bds[:, :], bd.rearrange("(z e) d -> z (e d)", z=1)).then_inc(s_w, 16)
            act.wait_ge(s_w, 16 * N_W)

            def body(s, b, live):
                if live(2):
                    passed(act, s_Y, s - 4)
                    for k in range(C):
                        within(act, s_G, s - 2, C, k + 1)
                        act.activation(HT[b][:, k, :, :], G_ps[k][:, :, :], ACT.Gelu,
                                       bias=b1s[:, k:k + 1]).then_inc(s_HT, 1)

            pipeline(act, G, 3, body)

        @block.vector
        def _(dve):
            def body(s, b, live):
                c = 1 - b
                if live(0):
                    if not (isinstance(s, int) and s < 2):
                        dve.wait_ge(s_hl[b], pair_gt(s - 2, b))
                    dve.tensor_copy(node[b][:, :], rt.node[:, bass.ts(s, GT)]).then_inc(s_node, 1)
                if live(1):
                    passed(dve, s_T, s - 1)
                    passed(dve, s_G, s - 3, C)
                    dve.tensor_copy(hT[c][:, :, :], T_ps[:, :, :]).then_inc(s_hT, 1)
                if live(3):
                    passed(dve, s_Y, s - 3)
                    if not (isinstance(s, int) and s < 5):
                        dve.wait_ge(s_out[c], pair(s - 5, c))
                    dve.tensor_copy(y[c][:, :, :], Y_ps[:, :, :]).then_inc(s_y, 1)

            pipeline(dve, G, 3, body)

        @block.tensor
        def _(pe):
            pe.wait_ge(s_w, 16 * N_W)
            pe.wait_ge(s_const, 3)

            def body(s, b, live):
                c = 1 - b
                if live(3):
                    own = [pe.value_load(rt.expert[0:1, bass.ts((s - 3) * GT + t, 1)], min_val=0, max_val=E - 1)
                           for t in range(GT)]
                if live(1):
                    pe.wait_ge(s_hl[c], pair_gt(s - 1, c))
                    passed(pe, s_hT, s - 2)
                    for t in range(GT):
                        mm = pe.transpose(T_ps[:, t, :], h[c][:, t, :], ident[:, :])
                    mm.then_inc(s_T, 1)
                if live(3):
                    passed(pe, s_HT, s - 3, C)
                    passed(pe, s_y, s - 4)
                    for t in range(GT):
                        for k in range(C):
                            pe.matmul(Y_ps[:, t, :], HT[c][:, k, t, :], wds[:, k, bass.ts(own[t], D)],
                                      start=(k == 0), stop=False)
                        mm = pe.matmul(Y_ps[:, t, :], ones[:, :], bds[:, bass.ts(own[t], D)], start=False, stop=True)
                    mm.then_inc(s_Y, 1)
                if live(2):
                    passed(pe, s_hT, s - 2)
                    for k in range(C):
                        passed_half(pe, s_HT, s - 3, C, k + 1)
                        pe.matmul(G_ps[k][:, :, :], w1s[:, k * P:(k + 1) * P], hT[b][:, :, :],
                                  start=True, stop=True).then_inc(s_G, 1)

            pipeline(pe, G, 3, body)


def typed_attention(nc, x1, rt, y_rows, adj, a_all, bias, x3):
    B = x1.shape[0]
    G = B // GT
    K = len(a_all)
    HG = GT // 2
    xg, adjg, x3g = gather_view(x1), gather_view(adj), gather_view(x3)
    with ExitStack() as ctx:
        m = Space(nc, ctx, "ta")
        sb, bank, sem = m.sb, m.bank, m.sem

        def two(name, shape, dt=F32):
            return [sb(f"{name}{b}", shape, dt) for b in range(2)]

        ident = sb("ident", [P, P])
        half, eps, zero = sb("half", [P, GT]), sb("eps", [P, GT]), sb("zero", [P, GT])
        tick, ptick = sb("tick", [P, 1 + 2 * K]), sb("ptick", [P, 1])
        acol, brow = sb("acol", [P, K]), sb("brow", [P, D])
        row, pt = two("row", [P, GT], I32), two("pt", [P, GT])
        xt, yt, x2, xb, xo = (two(n, [P, GT, D]) for n in ("x", "y", "x2", "xb", "xo"))
        aj = two("adj", [P, GT, P], I32)
        st, ve = sb("st", [P, GT, 6]), sb("ve", [P, GT])
        mv, rstd = two("mv", [P, GT, 2]), two("rstd", [P, GT])
        h, hk = two("h", [P, GT, D]), two("hk", [P, GT, D])
        hT, hTa = two("hT", [P, GT, P]), two("hTa", [P, K, GT, P])
        is_k = two("is_k", [P, K, GT, P], I32)
        sel, lk, al, alT = (two(n, [P, GT, P]) for n in ("sel", "lk", "al", "alT"))
        T_ps, AT_ps, U_ps = (bank(n, [P, GT, P]) for n in ("T", "AT", "U"))
        E_ps = [bank(f"E{i}", [P, HG, K, P]) for i in range(2)]

        s_w, s_const, s_gate = sem("w"), sem("const"), sem("gate")
        s_x, s_y, s_adj, s_hk, s_out = ([sem(f"{n}{b}") for b in range(2)] for n in ("x", "y", "adj", "hk", "out"))
        s_st, s_mv, s_ve, s_rstd, s_h = sem("st"), sem("mv"), sem("ve"), sem("rstd"), sem("h")
        (s_row, s_x2, s_T, s_hT, s_hTa, s_isk, s_fill, s_E, s_sel, s_lk, s_al, s_AT, s_alT, s_U, s_xb, s_xo) = (
            sem(n) for n in ("row", "x2", "T", "hT", "hTa", "isk", "fill", "E", "sel", "lk", "al", "AT", "alT",
                             "U", "xb", "xo"))
        block = ctx.enter_context(nc.Block())

        @block.sync
        def _(sp):
            for k in range(K):
                sp.dma_start(acol[:, k:k + 1], a_all[k]).then_inc(s_w, 16)
            sp.dma_start(brow[:, :], bias.partition_broadcast(P)).then_inc(s_w, 16)

            def body(s, b, live):
                c = 1 - b
                if live(0):
                    passed(sp, s_x2, s - 2, GT)
                    sp.dma_start(xt[b][:, :, :], xg[s]).then_inc(s_x[b], 16)
                if live(1):
                    passed(sp, s_isk, s - 3, K)
                    sp.dma_start(aj[c][:, :, :], adjg[s - 1]).then_inc(s_adj[c], 16)
                if live(4):
                    passed(sp, s_xo, s - 4)
                    sp.dma_start(x3g[s - 4], xo[b][:, :, :]).then_inc(s_out[b], 16)
                if live(2):
                    passed(sp, s_h, s - 2, GT)
                    passed(sp, s_U, s - 4)
                    sp.dma_start(hk[b][:, :, :], h[b][:, :, :]).then_inc(s_hk[b], 16)

            pipeline(sp, G, 4, body)
            for b in range(2):
                sp.wait_ge(s_out[b], 16 * (G // 2))

        @block.gpsimd
        def _(pool):
            pool.memset(zero[:, :], 0.0).then_inc(s_const, 1)
            pool.memset(half[:, :], -0.5).then_inc(s_const, 1)
            pool.memset(eps[:, :], EPS).then_inc(s_const, 1)
            make_identity(nc, pool, ident, s_const, 3)
            pool.wait_ge(s_const, 5)
            pool.wait_ge(s_w, 16 * (K + 1))

            def body(s, b, live):
                c = 1 - b
                if live(0):
                    passed(pool, s_row, s, 2)
                    passed(pool, s_x2, s - 2, GT)
                    gate(pool, ptick, zero, s, s_gate)
                    for t in range(GT):
                        pool.indirect_dma_start(yt[b][:, t, :], None, y_rows,
                                                bass.IndirectOffsetOnAxis(row[b][:, t:t + 1], 0)).then_inc(s_y[b], 16)
                if live(1):
                    norm_rstd(pool, mv[c], ve, rstd[c], eps, half, s - 1, s_mv, s_ve, s_rstd, s_h)
                if live(2):
                    passed(pool, s_x2, s - 2, GT)
                    passed(pool, s_xo, s - 4)
                    passed(pool, s_lk, s - 4)
                    pool.tensor_tensor(xb[b][:, :, :], x2[b][:, :, :],
                                       brow[:, :].unsqueeze(1).to_broadcast([P, GT, D]), ALU.add).then_inc(s_xb, 1)
                    pool.memset(sel[b][:, :, :], -BIG).then_inc(s_fill, 1)

            pipeline(pool, G, 4, body)

        @block.scalar
        def _(act):
            act.wait_ge(s_w, 16 * (K + 1))

            def body(s, b, live):
                c = 1 - b
                if live(2):
                    passed(act, s_T, s - 2)
                    passed(act, s_E, s - 4, 2)
                    act.activation(hT[b][:, :, :], T_ps[:, :, :], ACT.Copy).then_inc(s_hT, 1)
                if live(2):
                    passed(act, s_hT, s - 2)
                    for k in range(K):
                        act.activation(hTa[b][:, k, :, :], hT[b][:, :, :], ACT.Copy,
                                       scale=acol[:, k:k + 1]).then_inc(s_hTa, 1)
                if live(4):
                    passed(act, s_AT, s - 4)
                    act.activation(alT[b][:, :, :], AT_ps[:, :, :], ACT.Copy).then_inc(s_alT, 1)
                if live(3):
                    passed(act, s_lk, s - 3)
                    passed(act, s_AT, s - 5)
                    act.activation(al[c][:, :, :], lk[c][:, :, :], ACT.Sigmoid).then_inc(s_al, 1)

            pipeline(act, G, 4, body)

        @block.vector
        def _(dve):
            def take_routing(s, b):
                if not (isinstance(s, int) and s < 2):
                    dve.wait_ge(s_y[b], pair_gt(s - 2, b))
                passed(dve, s_x2, s - 2, GT)
                dve.tensor_copy(row[b][:, :], rt.row[:, bass.ts(s, GT)]).then_inc(s_row, 1)
                dve.tensor_copy(pt[b][:, :], rt.ptop[:, bass.ts(s, GT)]).then_inc(s_row, 1)

            def body(s, b, live):
                c = 1 - b

                def select(i):
                    within(dve, s_E, s - 3, 2, i + 1)
                    for k in range(K):
                        if k:
                            within(dve, s_sel, s - 3, 2 * K, i * K + k)
                        dve.memset(tick[:, 1 + i * K + k:2 + i * K + k], 0.0)
                        dve.copy_predicated(sel[c][:, i * HG:(i + 1) * HG, :],
                                            is_k[c][:, k, i * HG:(i + 1) * HG, :],
                                            E_ps[i][:, :, k, :]).then_inc(s_sel, 1)

                if live(0):
                    take_routing(s, b)
                if live(2):
                    if not (isinstance(s, int) and s < 4):
                        dve.wait_ge(s_hk[b], pair(s - 4, b))
                    passed(dve, s_T, s - 4)
                    norm_apply(dve, x2[b], mv[b], rstd[b], h[b], s - 2, s_rstd, s_h)
                if live(3):
                    passed(dve, s_isk, s - 3, K)
                    passed(dve, s_fill, s - 3)
                    select(0)
                if live(1):
                    passed(dve, s_row, s - 1, 2)
                    dve.wait_ge(s_x[c], pair(s - 1, c))
                    dve.wait_ge(s_y[c], pair_gt(s - 1, c))
                    passed(dve, s_xb, s - 3)
                    passed(dve, s_h, s - 3, GT)
                    for t in range(GT):
                        dve.scalar_tensor_tensor(out=x2[c][:, t, :], in0=yt[c][:, t, :], scalar=pt[c][:, t:t + 1],
                                                 in1=xt[c][:, t, :], op0=ALU.mult, op1=ALU.add).then_inc(s_x2, 1)
                    passed(dve, s_mv, s - 2, GT)
                    passed(dve, s_x2, s - 1, GT)
                    norm_stats(dve, x2[c], st, mv[c], tick, s - 1, s_st, s_mv)
                if live(3):
                    select(1)
                    passed(dve, s_sel, s - 3, 2 * K)
                    passed(dve, s_al, s - 5)
                    dve.scalar_tensor_tensor(out=lk[c][:, :, :], in0=sel[c][:, :, :], scalar=0.2,
                                             in1=sel[c][:, :, :], op0=ALU.mult, op1=ALU.max).then_inc(s_lk, 1)
                if live(2):
                    dve.wait_ge(s_adj[b], pair(s - 2, b))
                    passed(dve, s_sel, s - 4, 2 * K)
                    for k in range(K):
                        dve.tensor_scalar(is_k[b][:, k, :, :], aj[b][:, :, :], float(k + 1), None,
                                          ALU.is_equal).then_inc(s_isk, 1)
                if live(4):
                    passed(dve, s_U, s - 4)
                    passed(dve, s_xb, s - 4)
                    if not (isinstance(s, int) and s < 6):
                        dve.wait_ge(s_out[b], pair(s - 6, b))
                    dve.tensor_tensor(xo[b][:, :, :], U_ps[:, :, :], xb[b][:, :, :], ALU.add).then_inc(s_xo, 1)

            pipeline(dve, G, 4, body)

        @block.tensor
        def _(pe):
            pe.wait_ge(s_const, 5)

            def body(s, b, live):
                c = 1 - b

                def scores(i):
                    passed_half(pe, s_sel, s - 4, 2 * K, (i + 1) * K)
                    for t in range(i * HG, (i + 1) * HG):
                        mm = pe.matmul(E_ps[i][:, t - i * HG, :, :], hT[c][:, t, :], hTa[c][:, :, t, :],
                                       start=True, stop=True)
                    mm.then_inc(s_E, 1)

                if live(3):
                    passed(pe, s_hTa, s - 3, K)
                    scores(0)
                if live(2):
                    passed(pe, s_h, s - 2, GT)
                    passed(pe, s_hT, s - 3)
                    for t in range(GT):
                        mm = pe.transpose(T_ps[:, t, :], h[b][:, t, :], ident[:, :])
                    mm.then_inc(s_T, 1)
                if live(3):
                    scores(1)
                if live(4):
                    passed(pe, s_al, s - 4)
                    passed(pe, s_alT, s - 5)
                    for t in range(GT):
                        mm = pe.transpose(AT_ps[:, t, :], al[b][:, t, :], ident[:, :])
                    mm.then_inc(s_AT, 1)
                    passed(pe, s_alT, s - 4)
                    pe.wait_ge(s_hk[b], pair(s - 4, b))
                    passed(pe, s_xo, s - 5)
                    for t in range(GT):
                        mm = pe.matmul(U_ps[:, t, :], alT[b][:, t, :], hk[b][:, t, :], start=True, stop=True)
                    mm.then_inc(s_U, 1)

            pipeline(pe, G, 4, body)


def mamba_block(nc, x, w_in, conv_w, conv_b, dt_bias, a_log, d_skip, norm_w, w_out, w_lin, b_lin, x4):
    B = x.shape[0]
    G = B // GT
    H = dt_bias.shape[0]
    DI = norm_w.shape[0]
    C = DI // P
    HC = H // C
    HD = DI // H
    NS = (conv_b.shape[0] - DI) // 2
    TAPS = conv_w.shape[1]
    DT0 = DI + conv_b.shape[0]
    xg, x4g = gather_view(x), gather_view(x4)
    with ExitStack() as ctx:
        m = Space(nc, ctx, "mb")
        sb, bank, sem = m.sb, m.bank, m.sem
        ident, ones = sb("ident", [P, P]), sb("ones", [P, P])
        upto = sb("upto", [P, P])
        above = sb("above", [P, P])
        half, eps, zero = sb("half", [P, GT]), sb("eps", [P, GT]), sb("zero", [P, GT])
        tick, ptick = sb("tick", [P, 8]), sb("ptick", [P, 1])
        win = sb("win", [P, w_in.shape[1]])
        cw, cb = sb("cw", [P, C + 1, TAPS]), sb("cb", [P, C + 1])
        dtb, alog, nega = sb("dtb", [P, H]), sb("alog", [P, H]), sb("nega", [P, H])
        dcol, nw = sb("dcol", [P, C]), sb("nw", [P, C])
        wout, woutT, wlin = sb("wout", [P, C, D]), sb("woutT", [P, C, P]), sb("wlin", [P, D])
        wol = sb("wol", [P, C, D])
        brow = sb("brow", [P, D])

        def two(name, shape):
            return [sb(f"{name}{b}", shape) for b in range(2)]

        xt, xr, xb, xo, h = (two(n, [P, GT, D]) for n in ("x", "xr", "xb", "xo", "h"))
        st, ve = sb("st", [P, GT, 6]), sb("ve", [P, GT])
        mv, rstd = two("mv", [P, GT, 2]), two("rstd", [P, GT])
        hT = two("hT", [P, GT, P])
        cv = [two(f"cv{j}_", [P, GT, P]) for j in range(C + 1)]
        xs = [two(f"xs{j}_", [P, GT, P]) for j in range(C)]
        bs, cs = two("bs", [NS, GT, P]), two("cs", [NS, GT, P])
        sz = [two(f"sz{j}_", [P, GT, P]) for j in range(C)]
        dr, dn, dm, du, dd, dq, dz, dz2, dp, dp2 = (
            sb(n, [P, GT, H]) for n in ("dr", "dn", "dm", "du", "dd", "dq", "dz", "dz2", "dp", "dp2"))
        dt, da = two("dt", [P, GT, H]), two("da", [P, GT, H])
        sg = two("sg", [P, GT, H, P])
        ls = two("ls", [P, GT, H, P])
        gm = two("gm", [P, GT, P])
        xdt = two("xdt", [P, GT, H, HD])
        y1 = [sb(f"y1_{j}", [P, GT, P]) for j in range(C)]
        y2 = [two(f"y2_{j}_", [P, GT, P]) for j in range(C)]
        sq = [sb(f"sq{j}", [P, GT, P]) for j in range(C)]
        vs, rr = sb("vs", [P, GT]), sb("rr", [P, GT])

        T_ps = bank("T", [P, GT, P])
        X_ps = [bank(f"X{j}", [P, GT, P]) for j in range(C + 1)]
        Y_ps = [bank(f"Y{j}", [P, GT, P]) for j in range(C)]
        R_ps = [bank(f"R{j}", [P, GT, P]) for j in range(2)]
        dt_ps = R_ps[1][:, 0, 0:GT * H].rearrange("p (t h) -> p t h", t=GT)
        ss_ps = R_ps[1][:, 1, 0:GT]

        s_w, s_const, s_prep = sem("w"), sem("const"), sem("prep")
        s_x, s_xr, s_out = ([sem(f"{n}{b}") for b in range(2)] for n in ("x", "xr", "out"))
        s_st, s_mv, s_ve, s_rstd, s_h = sem("st"), sem("mv"), sem("ve"), sem("rstd"), sem("h")
        (s_T, s_hT, s_X, s_cv, s_tap, s_dt, s_dn, s_du, s_dtc, s_da, s_sg, s_Z, s_sz, s_xs, s_seg, s_ls,
         s_G, s_gm, s_xT, s_xdt, s_m, s_Y, s_y1, s_y2, s_sq, s_O, s_SS, s_vs, s_rr, s_xb, s_xo, s_ol, s_dtr) = (
            sem(n) for n in ("T", "hT", "X", "cv", "tap", "dt", "dn", "du", "dtc", "da", "sg", "Z", "sz", "xs",
                             "seg", "ls", "G", "gm", "xT", "xdt", "m", "Y", "y1", "y2", "sq", "O", "SS", "vs",
                             "rr", "xb", "xo", "ol", "dtr"))
        N_W = 5 + (C + 1) * 2 + 2 * C + H
        DTC = 13
        NT = (C + 1) * (TAPS - 1)
        block = ctx.enter_context(nc.Block())

        @block.sync
        def _(sp):
            def col(dst, src):
                sp.dma_start(dst, src.rearrange("(p z) -> p z", z=1)).then_inc(s_w, 16)

            sp.dma_start(win[:, :], w_in).then_inc(s_w, 16)
            for j in range(C + 1):
                sp.dma_start(cw[:, j, :], conv_w[j * P:(j + 1) * P, :]).then_inc(s_w, 16)
                col(cb[:, j:j + 1], conv_b[j * P:(j + 1) * P])
            sp.dma_start(dtb[:, :], dt_bias.partition_broadcast(P)).then_inc(s_w, 16)
            sp.dma_start(alog[:, :], a_log.partition_broadcast(P)).then_inc(s_w, 16)
            for k in range(H):
                sp.dma_start(dcol[k % HC * HD:(k % HC + 1) * HD, k // HC:k // HC + 1],
                             d_skip[k:k + 1].partition_broadcast(HD)).then_inc(s_w, 16)
            for j in range(C):
                col(nw[:, j:j + 1], norm_w[j * P:(j + 1) * P])
                sp.dma_start(wout[:, j, :], w_out[j * P:(j + 1) * P, :]).then_inc(s_w, 16)
            sp.dma_start(wlin[:, :], w_lin).then_inc(s_w, 16)
            sp.dma_start(brow[:, :], b_lin.partition_broadcast(P)).then_inc(s_w, 16)

            def body(s, b, live):
                if live(0):
                    passed(sp, s_h, s - 2, GT)
                    sp.dma_start(xt[b][:, :, :], xg[s]).then_inc(s_x[b], 16)
                if live(4):
                    passed(sp, s_xb, s - 6)
                    sp.dma_start(xr[b][:, :, :], xg[s - 4]).then_inc(s_xr[b], 16)
                if live(5):
                    passed(sp, s_xo, s - 5, GT)
                    sp.dma_start(x4g[s - 5], xo[1 - b][:, :, :]).then_inc(s_out[1 - b], 16)

            pipeline(sp, G, 5, body)
            for b in range(2):
                sp.wait_ge(s_out[b], 16 * (G // 2))

        @block.gpsimd
        def _(pool):
            make_identity(nc, pool, ident, s_const)
            pool.memset(half[:, :], -0.5).then_inc(s_const, 1)
            pool.memset(eps[:, :], EPS).then_inc(s_const, 1)
            pool.memset(ones[:, :], 1.0).then_inc(s_const, 1)
            pool.wait_ge(s_const, 5)
            pool.affine_select(out=upto[:, :], in_=ones[:, :], compare_op=ALU.is_ge, fill=0.0, base=0,
                               pattern=[[1, P]], channel_multiplier=-1).then_inc(s_const, 1)
            pool.affine_select(out=above[:, :], in_=ones[:, :], compare_op=ALU.is_gt, fill=0.0, base=0,
                               pattern=[[-1, P]], channel_multiplier=1).then_inc(s_const, 1)
            pool.wait_ge(s_const, 7)
            pool.wait_ge(s_w, 16 * N_W)

            def body(s, b, live):
                c = 1 - b
                if live(5):
                    passed(pool, s_O, s - 7)
                    passed(pool, s_sq, s - 7, C)
                    for j in range(C):
                        within(pool, s_y1, s - 5, C, j + 1)
                        pool.tensor_tensor(y2[j][c][:, :, :], y1[j][:, :, :], sz[j][c][:, :, :],
                                           ALU.mult).then_inc(s_y2, 1)
                    pool.wait_ge(s_xr[c], pair(s - 5, c))
                    passed(pool, s_xo, s - 7, GT)
                    pool.tensor_tensor(xb[c][:, :, :], xr[c][:, :, :],
                                       brow[:, :].unsqueeze(1).to_broadcast([P, GT, D]), ALU.add).then_inc(s_xb, 1)
                    passed(pool, s_vs, s - 5)
                    passed(pool, s_xo, s - 6, GT)
                    pool.tensor_tensor(rr[:, :], vs[:, :], half[:, :], ALU.pow).then_inc(s_rr, 1)
                if live(0):
                    norm_rstd(pool, mv[b], ve, rstd[b], eps, half, s, s_mv, s_ve, s_rstd, s_h)
                if live(2):
                    passed(pool, s_da, s - 2)
                    passed(pool, s_seg, s - 4, GT)
                    pool.tensor_tensor(sg[b][:, :, :, :].rearrange("p t h l -> p (t h) l"),
                                       da[b][:, :, :].rearrange("p t h -> p (t h)").unsqueeze(2)
                                       .to_broadcast([P, GT * H, P]),
                                       upto[:, :].unsqueeze(1).to_broadcast([P, GT * H, P]),
                                       ALU.mult).then_inc(s_sg, 1)

            pipeline(pool, G, 5, body)

        @block.scalar
        def _(act):
            act.wait_ge(s_w, 16 * N_W)
            act.activation(nega[:, :], alog[:, :], ACT.Exp).then_inc(s_prep, 1)

            def body(s, b, live):
                c = 1 - b
                if live(3):
                    passed(act, s_tap, s - 3, NT)
                    passed(act, s_G, s - 5)
                    act.activation(bs[c][:, :, :], cv[C][c][0:NS, :, :], ACT.Silu).then_inc(s_xs, 1)
                    act.activation(cs[c][:, :, :], cv[C][c][NS:2 * NS, :, :], ACT.Silu).then_inc(s_xs, 1)
                    for j in range(C):
                        passed_half(act, s_y1, s - 5, C, j + 1)
                        act.activation(xs[j][c][:, :, :], cv[j][c][:, :, :], ACT.Silu).then_inc(s_xs, 1)
                if live(2):
                    passed(act, s_xs, s - 4, C + 2)
                    for j in range(C + 1):
                        within(act, s_X, s - 2, C + 1, j + 1)
                        act.activation(cv[j][b][:, :, :], X_ps[j][:, :, :], ACT.Identity,
                                       bias=cb[:, j:j + 1], scale=cw[:, j, TAPS - 1:TAPS]).then_inc(s_cv, 1)
                if live(1):
                    passed(act, s_T, s - 1)
                    passed(act, s_Z, s - 3)
                    act.activation(hT[c][:, :, :], T_ps[:, :, :], ACT.Copy).then_inc(s_hT, 1)
                if live(3):
                    passed(act, s_Z, s - 3)
                    passed(act, s_y2, s - 5, C)
                    for j in range(C):
                        act.activation(sz[j][c][:, :, :], Y_ps[j][:, :, :], ACT.Silu).then_inc(s_sz, 1)
                if live(5):
                    passed(act, s_SS, s - 6)
                    for j in range(C):
                        within(act, s_y2, s - 5, C, j + 1)
                        act.activation(sq[j][:, :, :], y2[j][c][:, :, :], ACT.Square).then_inc(s_sq, 1)
                if live(2):
                    passed(act, s_dn, s - 2)
                    act.activation(du[:, :, :], dn[:, :, :], ACT.Exp).then_inc(s_du, 1)
                if live(3):
                    passed(act, s_Y, s - 5)
                    for t in range(GT):
                        within(act, s_seg, s - 3, GT, t + 1)
                        act.activation(ls[c][:, t, :, :], R_ps[t % 2][:, :, :], ACT.Exp).then_inc(s_ls, 1)

            pipeline(act, G, 5, body)

        @block.vector
        def _(dve):
            dve.wait_ge(s_w, 16 * N_W)
            dve.wait_ge(s_prep, 1)
            dve.tensor_scalar(nega[:, :], nega[:, :], -1.0, None, ALU.mult).then_inc(s_prep, 1)
            dve.wait_ge(s_ol, 1)
            dve.tensor_copy(woutT[:, :, :], T_ps[:, 0:C, :]).then_inc(s_prep, 1)
            dve.wait_ge(s_ol, 2)
            for j in range(C):
                dve.tensor_scalar(wol[:, j, :], R_ps[0][:, j, :], nw[:, j:j + 1], None, ALU.mult).then_inc(s_prep, 1)
            dve.wait_ge(s_prep, 3 + C)
            dve.wait_ge(s_const, 7)

            def body(s, b, live):
                c = 1 - b

                def taps(k):
                    for j in range(C + 1):
                        if k == 1:
                            within(dve, s_cv, s - 2, C + 1, j + 1)
                        else:
                            within(dve, s_tap, s - 2, NT, (k - 2) * (C + 1) + j + 1)
                        dve.scalar_tensor_tensor(out=cv[j][b][:, :, k:P], in0=X_ps[j][:, :, 0:P - k],
                                                 scalar=cw[:, j, TAPS - 1 - k:TAPS - k],
                                                 in1=cv[j][b][:, :, k:P], op0=ALU.mult,
                                                 op1=ALU.add).then_inc(s_tap, 1)

                def times_dt(j):
                    within(dve, s_xT, s - 3, C, j + 1)
                    dve.tensor_tensor(xdt[c][:, :, j * HC:(j + 1) * HC, :],
                                      R_ps[1 - j][:, :, :].rearrange("p t (h d) -> p t h d", h=HC),
                                      dt[c][:, :, j * HC:(j + 1) * HC].unsqueeze(3)
                                      .to_broadcast([P, GT, HC, HD]), ALU.mult).then_inc(s_xdt, 1)

                if live(5):
                    passed(dve, s_Y, s - 5)
                    passed(dve, s_y2, s - 6, C)
                    for j in range(C):
                        dve.scalar_tensor_tensor(out=y1[j][:, :, :], in0=xs[j][c][:, :, :], scalar=dcol[:, j:j + 1],
                                                 in1=Y_ps[j][:, :, :], op0=ALU.mult, op1=ALU.add).then_inc(s_y1, 1)
                if live(1):
                    passed(dve, s_T, s - 3)
                    norm_apply(dve, xt[c], mv[c], rstd[c], h[c], s - 1, s_rstd, s_h)
                if live(4):
                    passed(dve, s_gm, s - 4)
                    passed(dve, s_ls, s - 4, GT)
                    dve.tensor_tensor(ls[b][:, :, :, :], ls[b][:, :, :, :],
                                      gm[b][:, :, :].unsqueeze(2).to_broadcast([P, GT, H, P]),
                                      ALU.mult).then_inc(s_m, 1)
                if live(2):
                    taps(1)
                if live(3):
                    passed(dve, s_G, s - 3)
                    passed(dve, s_m, s - 5)
                    dve.tensor_tensor(gm[c][:, :, :], R_ps[0][:, :, :],
                                      upto[:, :].unsqueeze(1).to_broadcast([P, GT, P]), ALU.mult).then_inc(s_gm, 1)
                if live(3):
                    passed(dve, s_Y, s - 5)
                    times_dt(0)
                if live(2):
                    taps(2)
                if live(3):
                    for j in range(1, C):
                        times_dt(j)
                if live(2):
                    taps(3)
                if live(5):
                    passed(dve, s_SS, s - 5)
                    if live(2):
                        passed(dve, s_dt, s - 2)
                    passed(dve, s_rr, s - 6)
                    dve.tensor_scalar(vs[:, :], ss_ps, 1.0 / DI, EPS, ALU.mult, ALU.add).then_inc(s_vs, 1)
                if live(2):
                    passed(dve, s_dt, s - 2)
                    dve.tensor_tensor(dr[:, :, :], dt_ps, dtb[:, :].unsqueeze(1).to_broadcast([P, GT, H]),
                                      ALU.add).then_inc(s_dtc, 1)
                    within(dve, s_dtc, s - 2, DTC, 1)
                    dve.scalar_tensor_tensor(out=dn[:, :, :], in0=dr[:, :, :], scalar=-1.0, in1=dr[:, :, :],
                                             op0=ALU.mult, op1=ALU.min).then_inc(s_dn, 1)
                    dve.tensor_scalar(dm[:, :, :], dr[:, :, :], 0.0, None, ALU.max).then_inc(s_dtc, 1)
                if live(0):
                    dve.wait_ge(s_x[b], pair(s, b))
                    passed(dve, s_mv, s - 1, GT)
                    norm_stats(dve, xt[b], st, mv[b], tick, s, s_st, s_mv)
                if live(5):
                    passed(dve, s_rr, s - 5)
                    passed(dve, s_O, s - 5)
                    passed(dve, s_xb, s - 5)
                    if not (isinstance(s, int) and s < 7):
                        dve.wait_ge(s_out[c], pair(s - 7, c))
                    for t in range(GT):
                        dve.scalar_tensor_tensor(out=xo[c][:, t, :], in0=T_ps[:, t, :], scalar=rr[:, t:t + 1],
                                                 in1=xb[c][:, t, :], op0=ALU.mult, op1=ALU.add).then_inc(s_xo, 1)
                if live(2):
                    passed(dve, s_du, s - 2)
                    dve.tensor_scalar(dd[:, :, :], du[:, :, :], 2.0, None, ALU.add).then_inc(s_dtc, 1)
                    within(dve, s_dtc, s - 2, DTC, 3)
                    dve.reciprocal(dq[:, :, :], dd[:, :, :]).then_inc(s_dtc, 1)
                    within(dve, s_dtc, s - 2, DTC, 4)
                    dve.tensor_tensor(dz[:, :, :], du[:, :, :], dq[:, :, :], ALU.mult).then_inc(s_dtc, 1)
                    within(dve, s_dtc, s - 2, DTC, 5)
                    dve.tensor_tensor(dz2[:, :, :], dz[:, :, :], dz[:, :, :], ALU.mult).then_inc(s_dtc, 1)
                    within(dve, s_dtc, s - 2, DTC, 6)
                    dve.tensor_scalar(dp[:, :, :], dz2[:, :, :], 1.0 / 13, None, ALU.mult).then_inc(s_dtc, 1)
                    for n, k in enumerate((11, 9, 7, 5, 3)):
                        src, dst = (dp, dp2) if n % 2 == 0 else (dp2, dp)
                        within(dve, s_dtc, s - 2, DTC, 7 + n)
                        dve.scalar_tensor_tensor(out=dst[:, :, :], in0=src[:, :, :], scalar=1.0 / k,
                                                 in1=dz2[:, :, :], op0=ALU.add, op1=ALU.mult).then_inc(s_dtc, 1)
                    within(dve, s_dtc, s - 2, DTC, 12)
                    dve.scalar_tensor_tensor(out=dp[:, :, :], in0=dp2[:, :, :], scalar=1.0, in1=dz[:, :, :],
                                             op0=ALU.add, op1=ALU.mult).then_inc(s_dtc, 1)
                    passed(dve, s_dtc, s - 2, DTC)
                    passed(dve, s_xdt, s - 4, C)
                    dve.scalar_tensor_tensor(out=dt[b][:, :, :], in0=dp[:, :, :], scalar=2.0, in1=dm[:, :, :],
                                             op0=ALU.mult, op1=ALU.add).then_inc(s_dtr, 1)
                    passed(dve, s_dtr, s - 2)
                    passed(dve, s_sg, s - 4)
                    dve.tensor_tensor(da[b][:, :, :], dt[b][:, :, :],
                                      nega[:, :].unsqueeze(1).to_broadcast([P, GT, H]), ALU.mult).then_inc(s_da, 1)

            pipeline(dve, G, 5, body)

        @block.tensor
        def _(pe):
            pe.wait_ge(s_w, 16 * N_W)
            pe.wait_ge(s_const, 7)
            for j in range(C):
                mm = pe.transpose(T_ps[:, j, :], wout[:, j, :], ident[:, :])
            mm.then_inc(s_ol, 1)
            pe.wait_ge(s_prep, 3)
            for j in range(C):
                mm = pe.matmul(R_ps[0][:, j, :], woutT[:, j, :], wlin[:, :], start=True, stop=True)
            mm.then_inc(s_ol, 1)
            pe.wait_ge(s_prep, 3 + C)

            def body(s, b, live):
                c = 1 - b

                def turned(j):
                    for t in range(GT):
                        mm = pe.transpose(R_ps[1 - j][:, t, :], xs[j][c][:, t, :], ident[:, :])
                    mm.then_inc(s_xT, 1)

                if live(2):
                    passed(pe, s_hT, s - 2)
                    passed(pe, s_tap, s - 3, NT)
                    for j in range(C + 1):
                        pe.matmul(X_ps[j][:, :, :], win[:, DI + j * P:DI + (j + 1) * P], hT[b][:, :, :],
                                  start=True, stop=True).then_inc(s_X, 1)
                if live(3):
                    passed(pe, s_hT, s - 3)
                    passed(pe, s_y1, s - 5, C)
                    for j in range(C):
                        mm = pe.matmul(Y_ps[j][:, :, :], win[:, j * P:(j + 1) * P], hT[c][:, :, :],
                                       start=True, stop=True)
                    mm.then_inc(s_Z, 1)
                if live(1):
                    passed(pe, s_h, s - 1, GT)
                    passed(pe, s_xo, s - 6, GT)
                    for t in range(GT):
                        mm = pe.transpose(T_ps[:, t, :], h[c][:, t, :], ident[:, :])
                    mm.then_inc(s_T, 1)
                if live(3):
                    passed(pe, s_xs, s - 3, C + 2)
                    passed(pe, s_ls, s - 4, GT)
                    for t in range(GT):
                        mm = pe.matmul(R_ps[0][:, t, :], bs[c][:, t, :], cs[c][:, t, :], start=True, stop=True)
                    mm.then_inc(s_G, 1)
                    turned(0)
                if live(5):
                    passed(pe, s_y2, s - 5, C)
                    if live(1):
                        passed(pe, s_hT, s - 1)
                    for t in range(GT):
                        for j in range(C):
                            mm = pe.matmul(T_ps[:, t, :], y2[j][c][:, t, :], wol[:, j, :],
                                           start=(j == 0), stop=(j == C - 1))
                    mm.then_inc(s_O, 1)
                if live(3):
                    passed(pe, s_gm, s - 3)
                    for j in range(1, C):
                        turned(j)
                if live(5):
                    passed(pe, s_sq, s - 5, C)
                    passed(pe, s_vs, s - 6)
                    if live(3):
                        within(pe, s_xdt, s - 3, C, 1)
                    elif live(4):
                        passed(pe, s_ls, s - 4, GT)
                    for t in range(GT):
                        for j in range(C):
                            mm = pe.matmul(ss_ps[:, t:t + 1], sq[j][:, t, :], ones[:, 0:1],
                                           start=(j == 0), stop=(j == C - 1))
                    mm.then_inc(s_SS, 1)
                if live(2):
                    passed(pe, s_hT, s - 2)
                    passed(pe, s_dn, s - 3)
                    if live(3):
                        within(pe, s_xdt, s - 3, C, 1)
                    for t in range(GT):
                        mm = pe.matmul(dt_ps[:, t, :], hT[b][:, t, :], win[:, DT0:DT0 + H], start=True, stop=True)
                    mm.then_inc(s_dt, 1)
                if live(3):
                    passed(pe, s_sg, s - 3)
                    for t in range(GT):
                        if t == 0:
                            passed(pe, s_xdt, s - 3, C)
                        elif t == 1:
                            if live(2):
                                passed(pe, s_dn, s - 2)
                            if live(5):
                                passed(pe, s_vs, s - 5)
                        else:
                            within(pe, s_ls, s - 3, GT, t - 1)
                        pe.matmul(R_ps[t % 2][:, :, :], above[:, :], sg[c][:, t, :, :],
                                  start=True, stop=True).then_inc(s_seg, 1)
                if live(4):
                    passed(pe, s_m, s - 4)
                    passed(pe, s_xdt, s - 4, C)
                    passed(pe, s_y1, s - 5, C)
                    if live(3):
                        passed(pe, s_sz, s - 3, C)
                    for t in range(GT):
                        for k in range(H):
                            mm = pe.matmul(Y_ps[k // HC][k % HC * HD:(k % HC + 1) * HD, t, :], xdt[b][:, t, k, :],
                                           ls[b][:, t, k, :], start=True, stop=True)
                    mm.then_inc(s_Y, 1)

            pipeline(pe, G, 5, body)


_INS = ['x', 'adj', 'L0_gnn_W', 'L0_gnn_a', 'L0_ffn_W1', 'L0_ffn_b1', 'L0_ffn_Wg', 'L0_ffn_bg', 'L0_ffn_Wd', 'L0_ffn_bd',
        'L1_gnn_a0', 'L1_gnn_a1', 'L1_gnn_a2', 'L1_gnn_a3', 'L1_gnn_bias', 'L1_ffn_W_in', 'L1_ffn_conv_w',
        'L1_ffn_conv_b', 'L1_ffn_dt_bias', 'L1_ffn_A_log', 'L1_ffn_D', 'L1_ffn_norm_w', 'L1_ffn_W_out',
        'L1_ffn_W_lin', 'L1_ffn_b_lin']
_OUT = ((64, 128, 128), 'float32')


def build(nc, i, out):
    graphs, n_experts = i['x'].shape[0], i['L0_ffn_bd'].shape[0]

    def scratch(name, shape):
        return nc.dram_tensor(name, list(shape), F32, kind="Internal").ap()

    x1, x3, h_rows = (scratch(n, (graphs * P, D)) for n in ("x1", "x3", "h_rows"))
    by_graph = [v.rearrange("(g p) d -> g p d", p=P) for v in (x1, x3)]
    additive_attention(nc, i['x'], i['adj'], i['L0_gnn_W'], i['L0_gnn_a'], by_graph[0])
    with ExitStack() as ctx:
        rt = Routing(nc, ctx, graphs, n_experts)
        y_rows = scratch("y_rows", (rt.tiles * P, D))
        gates(nc, by_graph[0], i['L0_ffn_W1'], i['L0_ffn_b1'], i['L0_ffn_Wg'], i['L0_ffn_bg'], rt, h_rows)
        experts(nc, i['L0_ffn_W1'], i['L0_ffn_b1'], i['L0_ffn_Wd'], i['L0_ffn_bd'], rt, h_rows, y_rows)
        typed_attention(nc, by_graph[0], rt, y_rows, i['adj'], [i[f'L1_gnn_a{k}'] for k in range(4)],
                        i['L1_gnn_bias'], by_graph[1])
    mamba_block(nc, by_graph[1], *(i[f'L1_ffn_{n}'] for n in ('W_in', 'conv_w', 'conv_b', 'dt_bias', 'A_log', 'D',
                                                              'norm_w', 'W_out', 'W_lin', 'b_lin')), out)


def kernel(**inputs):
    import numpy as _np
    import concourse.bacc as _bacc
    from concourse import mybir as _mybir
    from concourse.bass_utils import run_bass_kernel_spmd as _run

    nc = _bacc.Bacc("TRN2", target_bir_lowering=False, num_devices=1)
    arrays, args = {}, {}
    for name in _INS:
        a = _np.ascontiguousarray(inputs[name])
        arrays[f"in_{name}_dram"] = a
        args[name] = nc.dram_tensor(f"in_{name}_dram", a.shape, _mybir.dt.from_np(a.dtype), kind="ExternalInput").ap()
    shape, dtype = _OUT
    out = nc.dram_tensor("out_0_dram", shape, _mybir.dt.from_np(_np.dtype(dtype)), kind="ExternalOutput").ap()
    build(nc, args, out)
    r = _run(nc, [arrays], core_ids=[0])
    return r.results[0]["out_0_dram"]
```

```python
from contextlib import ExitStack

import concourse.bass as bass
from concourse import mybir

F32 = mybir.dt.float32
I32 = mybir.dt.int32
BF16 = mybir.dt.bfloat16
ALU = mybir.AluOpType
ACT = mybir.ActivationFunctionType
AX = mybir.AxisListType.X

P = 128
D = 128
GT = 4
EPS = 1e-5
NEG = -9e15
BIG = 3e38


F32R = mybir.dt.float32r
PARTS = ((0, 0), (0, 1), (1, 0))


class Space:

    def __init__(self, nc, ctx, tag):
        self.nc, self.ctx, self.tag, self.sems = nc, ctx, tag, []
        ctx.callback(self.end)

    def end(self):
        if self.sems:
            self.nc.clear_and_free_semaphores(self.sems)
            self.nc.all_engine_barrier()

    def sb(self, name, shape, dt=F32):
        return self.ctx.enter_context(self.nc.sbuf_tensor(f"{self.tag}_{name}", list(shape), dt))

    def bank(self, name, shape):
        return self.ctx.enter_context(self.nc.psum_tensor(f"{self.tag}_{name}", list(shape), F32))

    def sem(self, name):
        self.sems.append(self.nc.alloc_semaphore(name=f"{self.tag}_{name}"))
        return self.sems[-1]


def passed(eng, sem, q, n=1):
    if isinstance(q, int) and q < 0:
        return
    eng.wait_ge(sem, q * n + n)


def within(eng, sem, q, n, k):
    eng.wait_ge(sem, q * n + k)


def passed_half(eng, sem, q, n, k):
    if not (isinstance(q, int) and q < 0):
        within(eng, sem, q, n, k)


def pair(q, b):
    return (q - b) * 8 + 16


def pair_gt(q, b):
    return ((q - b) * 8 + 16) * GT


def pipeline(eng, groups, lags, body):
    head = (lags + 3) // 2 * 2
    tail = groups // 2 * 2

    def peeled(s):
        body(s, s % 2, lambda lag: 0 <= s - lag < groups)

    for s in range(head):
        peeled(s)
    with eng.Fori(head // 2, tail // 2) as i:
        for u in range(2):
            body(i * 2 + u, u, lambda lag: True)
    for s in range(tail, groups + lags):
        peeled(s)


def gate(pool, tick, zero, s, sem_gate):
    passed(pool, sem_gate, s - 1)
    pool.tensor_tensor(tick[:, :], zero[:, 0:1], zero[:, 0:1], ALU.add).then_inc(sem_gate, 1)


def gather_view(dram):
    return dram.rearrange("(g t) p d -> g p t d", t=GT)


def norm_stats(dve, x, st, mv, tick, s, sem_st, sem_mv):
    norm_halves(dve, x, st, sem_st)
    for t in range(GT):
        norm_both(dve, t, st, mv, tick, s, sem_st, sem_mv)


def norm_halves(dve, x, st, sem_st):
    for t in range(GT):
        dve.bn_stats(st[:, t, :], x[:, t, :]).then_inc(sem_st, 1)


def norm_both(dve, t, st, mv, tick, s, sem_st, sem_mv):
    if t == 0:
        passed(dve, sem_st, s, GT)
        dve.memset(tick[:, 0:1], 0.0)
    dve.bn_aggr(mv[:, t, :], st[:, t, :]).then_inc(sem_mv, 1)


def norm_rstd(pool, mv, ve, rstd, eps, half, s, sem_mv, sem_ve, sem_rstd, sem_h):
    passed(pool, sem_rstd, s - 1)
    passed(pool, sem_mv, s, GT)
    pool.tensor_tensor(ve[:, :], mv[:, :, 1], eps[:, :], ALU.add).then_inc(sem_ve, 1)
    passed(pool, sem_ve, s)
    passed(pool, sem_h, s - 2, GT)
    pool.tensor_tensor(rstd[:, :], ve[:, :], half[:, :], ALU.pow).then_inc(sem_rstd, 1)


def norm_apply(dve, x, mv, rstd, h, s, sem_rstd, sem_h):
    passed(dve, sem_rstd, s)
    for t in range(GT):
        dve.tensor_scalar(h[:, t, :], x[:, t, :], mv[:, t, 0:1], rstd[:, t:t + 1],
                          ALU.subtract, ALU.mult).then_inc(sem_h, 1)


def make_identity(nc, pool, ident, sem, n=0):
    pool.memset(ident[:, :], 0.0).then_inc(sem, 1)
    pool.wait_ge(sem, n + 1)
    pool.affine_select(out=ident[:, :], in_=ident[:, :], compare_op=ALU.not_equal, fill=1.0, base=0,
                       pattern=[[-1, P]], channel_multiplier=1).then_inc(sem, 1)


def additive_attention(nc, x, adj, w, a, x1):
    B = x.shape[0]
    G = B // GT
    xg, adjg, x1g = gather_view(x), gather_view(adj), gather_view(x1)
    with ExitStack() as ctx:
        m = Space(nc, ctx, "aa")
        sb, bank, sem = m.sb, m.bank, m.sem
        ident = sb("ident", [P, P])
        ones = sb("ones", [P, P])
        half, eps, zero = sb("half", [P, GT]), sb("eps", [P, GT]), sb("zero", [P, GT])
        tick, ptick = sb("tick", [P, 8]), sb("ptick", [P, 1])
        wn = sb("wn", [P, D])
        wt = sb("wt", [P, D])
        ab = sb("ab", [P, 2, P])
        acol = sb("acol", [P, 2])
        wab = sb("wab", [P, 2, P])
        xt = [sb(f"x{b}", [P, GT, D]) for b in range(2)]
        xr = [sb(f"xr{b}", [P, GT, D]) for b in range(2)]
        aj = [sb(f"adj{b}", [P, GT, P], I32) for b in range(2)]
        st = sb("st", [P, GT, 6])
        mv = [sb(f"mv{b}", [P, GT, 2]) for b in range(2)]
        ve = sb("ve", [P, GT])
        rstd = [sb(f"rstd{b}", [P, GT]) for b in range(2)]
        h = [sb(f"h{b}", [P, GT, D]) for b in range(2)]
        hT = [sb(f"hT{b}", [P, GT, P]) for b in range(2)]
        wh = [sb(f"wh{b}", [P, GT, D]) for b in range(2)]
        msk = [sb(f"msk{b}", [P, GT, P]) for b in range(2)]
        e = sb("e", [P, GT, P])
        em = [sb(f"em{b}", [P, GT, P]) for b in range(2)]
        mx = sb("mx", [P, GT])
        nmx = [sb(f"nmx{b}", [P, GT]) for b in range(2)]
        prob = [sb(f"prob{b}", [P, GT, P]) for b in range(2)]
        probT = [sb(f"probT{b}", [P, GT, P]) for b in range(2)]
        rden = [sb(f"rden{b}", [P, GT]) for b in range(2)]
        xo = [sb(f"xo{b}", [P, GT, D]) for b in range(2)]
        T_ps, PT_ps, E_ps, Wh_ps, U_ps = (bank(n, [P, GT, P]) for n in ("T", "PT", "E", "Wh", "U"))
        den_ps = bank("den", [P, 512])

        s_gate = sem("gate")
        s_w, s_const, s_wt, s_wtc, s_ab = sem("w"), sem("const"), sem("wt"), sem("wtc"), sem("ab")
        s_x = [sem(f"x{b}") for b in range(2)]
        s_xr = [sem(f"xr{b}") for b in range(2)]
        s_adj = [sem(f"adj{b}") for b in range(2)]
        s_out = [sem(f"out{b}") for b in range(2)]
        s_st, s_mv, s_ve, s_rstd, s_h = sem("st"), sem("mv"), sem("ve"), sem("rstd"), sem("h")
        s_T, s_hT, s_E, s_e, s_msk, s_em, s_mx, s_nmx, s_prob = (
            sem(n) for n in ("T", "hT", "E", "e", "msk", "em", "mx", "nmx", "prob"))
        s_Wh, s_wh, s_PT, s_probT, s_den, s_U, s_rden, s_xo = (
            sem(n) for n in ("Wh", "wh", "PT", "probT", "den", "U", "rden", "xo"))
        block = ctx.enter_context(nc.Block())

        @block.sync
        def _(sp):
            sp.dma_start(wn[:, :], w).then_inc(s_w, 16)
            sp.dma_start(acol[:, :], a.rearrange("(k p) z -> p (k z)", p=P),
                         allow_slow_non_contiguous=True).then_inc(s_w, 16)

            def body(s, b, live):
                if live(0):
                    passed(sp, s_h, s - 2, GT)
                    sp.dma_start(xt[b][:, :, :], xg[s]).then_inc(s_x[b], 16)
                    passed(sp, s_msk, s - 2)
                    sp.dma_start(aj[b][:, :, :], adjg[s]).then_inc(s_adj[b], 16)
                if live(2):
                    passed(sp, s_xo, s - 4, GT)
                    sp.dma_start(xr[b][:, :, :], xg[s - 2]).then_inc(s_xr[b], 16)
                if live(4):
                    passed(sp, s_xo, s - 4, GT)
                    sp.dma_start(x1g[s - 4], xo[b][:, :, :]).then_inc(s_out[b], 16)

            pipeline(sp, G, 4, body)
            for b in range(2):
                sp.wait_ge(s_out[b], 16 * (G // 2))

        @block.gpsimd
        def _(pool):
            make_identity(nc, pool, ident, s_const)
            pool.memset(ones[:, :], 1.0).then_inc(s_const, 1)
            pool.memset(half[:, :], -0.5).then_inc(s_const, 1)
            pool.memset(eps[:, :], EPS).then_inc(s_const, 1)
            pool.memset(zero[:, :], 0.0).then_inc(s_const, 1)
            pool.wait_ge(s_const, 6)

            def body(s, b, live):
                c = 1 - b
                if live(1):
                    pool.wait_ge(s_adj[c], pair(s - 1, c))
                    passed(pool, s_e, s - 3)
                    gate(pool, ptick, zero, s - 1, s_gate)
                    pool.tensor_scalar(msk[c][:, :, :], aj[c][:, :, :], 0.0, None, ALU.is_le).then_inc(s_msk, 1)
                if live(0):
                    norm_rstd(pool, mv[b], ve, rstd[b], eps, half, s, s_mv, s_ve, s_rstd, s_h)

            pipeline(pool, G, 3, body)

        @block.scalar
        def _(act):
            def body(s, b, live):
                c = 1 - b
                if live(3):
                    passed(act, s_PT, s - 3)
                    passed(act, s_U, s - 5)
                    act.activation(probT[c][:, :, :], PT_ps[:, :, :], ACT.Copy).then_inc(s_probT, 1)
                if live(1):
                    passed(act, s_T, s - 1)
                    passed(act, s_Wh, s - 3)
                    act.activation(hT[c][:, :, :], T_ps[:, :, :], ACT.Copy).then_inc(s_hT, 1)
                if live(2):
                    passed(act, s_Wh, s - 2)
                    passed(act, s_U, s - 4)
                    act.activation(wh[b][:, :, :], Wh_ps[:, :, :], ACT.Copy).then_inc(s_wh, 1)
                    passed(act, s_nmx, s - 2)
                    passed(act, s_PT, s - 4)
                    for t in range(GT):
                        act.activation(prob[b][:, t, :], em[b][:, t, :], ACT.Exp,
                                       bias=nmx[b][:, t:t + 1]).then_inc(s_prob, 1)

            pipeline(act, G, 3, body)

        @block.vector
        def _(dve):
            dve.wait_ge(s_w, 32)
            dve.wait_ge(s_const, 3)
            for k in range(2):
                dve.tensor_scalar(ab[:, k, :], ones[:, :], acol[:, k:k + 1], None, ALU.mult).then_inc(s_ab, 1)
            dve.wait_ge(s_wt, 1)
            dve.tensor_copy(wt[:, :], T_ps[:, 0, :]).then_inc(s_wtc, 1)
            dve.wait_ge(s_wt, 2)
            dve.tensor_copy(wab[:, :, :], E_ps[:, 0:2, :]).then_inc(s_wtc, 1)

            def body(s, b, live):
                c = 1 - b
                if live(1):
                    passed(dve, s_T, s - 3)
                    norm_apply(dve, xt[c], mv[c], rstd[c], h[c], s - 1, s_rstd, s_h)
                if live(2):
                    passed(dve, s_E, s - 2)
                    passed(dve, s_msk, s - 2)
                    dve.scalar_tensor_tensor(out=e[:, :, :], in0=msk[b][:, :, :], scalar=NEG,
                                             in1=E_ps[:, :, :], op0=ALU.mult, op1=ALU.add).then_inc(s_e, 1)
                    passed(dve, s_e, s - 2)
                    passed(dve, s_prob, s - 4, GT)
                    dve.scalar_tensor_tensor(out=em[b][:, :, :], in0=e[:, :, :], scalar=0.2,
                                             in1=e[:, :, :], op0=ALU.mult, op1=ALU.max).then_inc(s_em, 1)
                    passed(dve, s_em, s - 2)
                    dve.tensor_reduce(mx[:, :], em[b][:, :, :], AX, ALU.max).then_inc(s_mx, 1)
                    passed(dve, s_mx, s - 2)
                    dve.tensor_scalar(nmx[b][:, :], mx[:, :], -1.0, None, ALU.mult).then_inc(s_nmx, 1)
                if live(0):
                    dve.wait_ge(s_x[b], pair(s, b))
                    passed(dve, s_mv, s - 1, GT)
                    norm_stats(dve, xt[b], st, mv[b], tick, s, s_st, s_mv)
                if live(3):
                    passed(dve, s_den, s - 3)
                    dve.reciprocal(rden[c][:, :], den_ps[:, 0:GT]).then_inc(s_rden, 1)
                    passed(dve, s_rden, s - 3)
                    passed(dve, s_U, s - 3)
                    dve.wait_ge(s_xr[c], pair(s - 3, c))
                    if not (isinstance(s, int) and s < 5):
                        dve.wait_ge(s_out[c], pair(s - 5, c))
                    for t in range(GT):
                        dve.scalar_tensor_tensor(out=xo[c][:, t, :], in0=U_ps[:, t, :],
                                                 scalar=rden[c][:, t:t + 1], in1=xr[c][:, t, :],
                                                 op0=ALU.mult, op1=ALU.add).then_inc(s_xo, 1)

            pipeline(dve, G, 3, body)

        @block.tensor
        def _(pe):
            pe.wait_ge(s_w, 32)
            pe.wait_ge(s_const, 2)
            pe.transpose(T_ps[:, 0, :], wn[:, :], ident[:, :]).then_inc(s_wt, 1)
            pe.wait_ge(s_ab, 2)
            pe.matmul(E_ps[:, 0:2, :], wn[:, :], ab[:, :, :], start=True, stop=True).then_inc(s_wt, 1)
            pe.wait_ge(s_wtc, 2)

            def body(s, b, live):
                c = 1 - b
                if live(3):
                    passed(pe, s_prob, s - 3, GT)
                    passed(pe, s_probT, s - 4)
                    for t in range(GT):
                        mm = pe.transpose(PT_ps[:, t, :], prob[c][:, t, :], ident[:, :])
                    mm.then_inc(s_PT, 1)
                if live(2):
                    passed(pe, s_hT, s - 2)
                    passed(pe, s_e, s - 3)
                    pe.matmul(E_ps[:, :, :], wab[:, 1, :], hT[b][:, :, :], start=True, stop=False)
                    for t in range(GT):
                        mm = pe.matmul(E_ps[:, t, :], hT[b][:, t, :], wab[:, 0, :], start=False, stop=(t == GT - 1))
                    mm.then_inc(s_E, 1)
                if live(1):
                    passed(pe, s_h, s - 1, GT)
                    passed(pe, s_hT, s - 2)
                    for t in range(GT):
                        mm = pe.transpose(T_ps[:, t, :], h[c][:, t, :], ident[:, :])
                    mm.then_inc(s_T, 1)
                if live(2):
                    passed(pe, s_hT, s - 2)
                    passed(pe, s_wh, s - 3)
                    for t in range(GT):
                        mm = pe.matmul(Wh_ps[:, t, :], hT[b][:, t, :], wt[:, :], start=True, stop=True)
                    mm.then_inc(s_Wh, 1)
                if live(3):
                    passed(pe, s_probT, s - 3)
                    passed(pe, s_rden, s - 4)
                    for t in range(GT):
                        mm = pe.matmul(den_ps[:, t:t + 1], probT[c][:, t, :], ones[:, 0:1], start=True, stop=True)
                    mm.then_inc(s_den, 1)
                    passed(pe, s_wh, s - 3)
                    passed(pe, s_xo, s - 4, GT)
                    for t in range(GT):
                        mm = pe.matmul(U_ps[:, t, :], probT[c][:, t, :], wh[c][:, t, :], start=True, stop=True)
                    mm.then_inc(s_U, 1)

            pipeline(pe, G, 3, body)


class Routing:

    def __init__(self, nc, ctx, graphs, experts, chunks):
        m = Space(nc, ctx, "rt")
        self.tiles = graphs + experts
        self.tiles += -self.tiles % (2 * GT)
        self.ptop = m.sb("ptop", [P, graphs])
        self.row = m.sb("row", [P, graphs], I32)
        self.expert = m.sb("expert", [P, self.tiles], I32)
        self.node = m.sb("node", [P, self.tiles], I32)
        self.w1p = [m.sb(f"w1p{n}", [P, chunks * P], F32R) for n in range(2)]
        self.b1s = m.sb("b1s", [P, chunks])
        self.wds, self.bds = m.sb("wds", [P, chunks, experts * D]), m.sb("bds", [1, experts * D])


def gates(nc, x1, w1, b1, wg, bg, wd, bd, rt, h_rows):
    B = x1.shape[0]
    G = B // GT
    E = bg.shape[0]
    C = w1.shape[1] // P
    xg, hg = gather_view(x1), h_rows.rearrange("(g t p) d -> g p t d", t=GT, p=P)
    with ExitStack() as ctx:
        m = Space(nc, ctx, "ga")
        sb, bank, sem = m.sb, m.bank, m.sem
        ident, ones = sb("ident", [P, P]), sb("ones", [P, P])
        before = sb("before", [P, P])
        half, eps = sb("half", [P, GT]), sb("eps", [P, GT])
        tick = sb("tick", [P, 8])
        w1s, b1s, w1p = sb("w1s", [P, C * P]), rt.b1s, rt.w1p
        wgs, bgs = sb("wgs", [P, C, E]), sb("bgs", [E, 1])
        xt = [sb(f"x{b}", [P, GT, D]) for b in range(2)]
        st, ve = sb("st", [P, GT, 6]), sb("ve", [P, GT])
        mv = [sb(f"mv{b}", [P, GT, 2]) for b in range(2)]
        rstd = [sb(f"rstd{b}", [P, GT]) for b in range(2)]
        h = [sb(f"h{b}", [P, GT, D]) for b in range(2)]
        hT = [[sb(f"hT{b}{n}", [P, GT, P], F32R) for n in range(2)] for b in range(2)]
        HT = [sb(f"HT{b}", [P, C, GT, P]) for b in range(2)]
        HTp = [[sb(f"HT{b}{n}", [P, C, GT, P], F32R) for n in range(2)] for b in range(2)]
        wgp = [sb(f"wgp{n}", [P, C, E], F32R) for n in range(2)]
        lg, lgT = sb("lg", [P, B, E]), sb("lgT", [E, GT, P])
        iota_e, iota_j = sb("iota_e", [P, B, E]), sb("iota_j", [P, rt.tiles, E])
        top, ex, first, oh = (sb(n, [P, B, E]) for n in ("top", "ex", "first", "oh"))
        mx, den, idx, pos = (sb(n, [P, B]) for n in ("mx", "den", "idx", "pos"))
        inc, off = sb("inc", [P, B, E]), sb("off", [P, B, E])
        cnt_i, pad_i = sb("cnt_i", [P, E], I32), sb("pad_i", [P, E], I32)
        pad, end, start = sb("pad", [P, E]), sb("end", [P, E]), sb("start", [P, E])
        full, tex = sb("full", [P, rt.tiles, E]), sb("tex", [P, rt.tiles])
        hi_i, lo_i = sb("hi_i", [P, B], I32), sb("lo_i", [P, B], I32)
        hi, lo, graph = sb("hi", [P, B]), sb("lo", [P, B]), sb("graph", [P, B], BF16)
        iota_p, iota_t = sb("iota_p", [P, P]), sb("iota_t", [P, rt.tiles])
        at_row, at_tile = sb("at_row", [P, B, P], BF16), sb("at_tile", [P, B, rt.tiles], BF16)
        at_num = sb("at_num", [P, B, 2, rt.tiles], BF16)
        iota_q, place = sb("iota_q", [P, 1]), sb("place", [P, rt.tiles])
        T_ps = bank("T", [P, GT, P])
        G_ps = [bank(f"G{c}", [P, GT, P]) for c in range(C)]
        L_ps, N_ps = bank("L", [P, GT, P]), bank("N", [P, GT, E])

        s_w, s_wd, s_const = sem("w"), sem("wd"), sem("const")
        s_x, s_hd = [sem(f"x{b}") for b in range(2)], [sem(f"hd{b}") for b in range(2)]
        s_st, s_mv, s_ve, s_rstd, s_h = sem("st"), sem("mv"), sem("ve"), sem("rstd"), sem("h")
        s_T, s_hT, s_G, s_HT, s_L, s_lgT, s_N, s_lg = (
            sem(n) for n in ("T", "hT", "G", "HT", "L", "lgT", "N", "lg"))
        s_hTl, s_HTh, s_HTl, s_whi, s_wlo = (sem(n) for n in ("hTl", "HTh", "HTl", "whi", "wlo"))
        s_r, s_max, s_ex, s_cnt, s_oh = sem("r"), sem("max"), sem("ex"), sem("cnt"), sem("oh")
        s_hilo, s_atr, s_att, s_place, s_graph, s_inv = (
            sem(n) for n in ("hilo", "atr", "att", "place", "graph", "inv"))
        CH = 8
        block = ctx.enter_context(nc.Block())

        @block.sync
        def _(sp):
            def body(s, b, live):
                if live(0):
                    passed(sp, s_h, s - 2, GT)
                    sp.dma_start(xt[b][:, :, :], xg[s]).then_inc(s_x[b], 16)
                if live(2):
                    passed(sp, s_h, s - 2, GT)
                    sp.dma_start(hg[s - 2], h[b][:, :, :]).then_inc(s_hd[b], 16)

            pipeline(sp, G, 4, body)
            for c in range(C):
                sp.dma_start(rt.wds[:, c, :].rearrange("p (e d) -> p e d", e=E),
                             wd[:, c * P:(c + 1) * P, :].rearrange("e p d -> p e d")).then_inc(s_wd, 16)
            sp.dma_start(rt.bds[:, :], bd.rearrange("(z e) d -> z (e d)", z=1)).then_inc(s_wd, 16)
            for b in range(2):
                sp.wait_ge(s_hd[b], 16 * (G // 2))
            sp.wait_ge(s_wd, 16 * (C + 1))

        @block.gpsimd
        def _(pool):
            make_identity(nc, pool, ident, s_const)
            pool.memset(half[:, :], -0.5).then_inc(s_const, 1)
            pool.memset(eps[:, :], EPS).then_inc(s_const, 1)
            pool.memset(ones[:, :], 1.0).then_inc(s_const, 1)
            pool.wait_ge(s_const, 5)
            pool.affine_select(out=before[:, :], in_=ones[:, :], compare_op=ALU.is_gt, fill=0.0, base=0,
                               pattern=[[1, P]], channel_multiplier=-1).then_inc(s_const, 1)
            pool.iota(iota_e[:, :, :], pattern=[[0, B], [1, E]], base=0, channel_multiplier=0,
                      allow_small_or_imprecise_dtypes=True).then_inc(s_const, 1)
            pool.iota(iota_j[:, :, :], pattern=[[P, rt.tiles], [0, E]], base=0, channel_multiplier=0,
                      allow_small_or_imprecise_dtypes=True).then_inc(s_const, 1)
            pool.iota(iota_p[:, :], pattern=[[1, P]], base=0, channel_multiplier=0,
                      allow_small_or_imprecise_dtypes=True).then_inc(s_const, 1)
            pool.iota(iota_t[:, :], pattern=[[1, rt.tiles]], base=0, channel_multiplier=0,
                      allow_small_or_imprecise_dtypes=True).then_inc(s_const, 1)
            pool.iota(graph[:, :], pattern=[[1, B]], base=0, channel_multiplier=0,
                      allow_small_or_imprecise_dtypes=True).then_inc(s_const, 1)
            pool.iota(iota_q[:, :], pattern=[[0, 1]], base=0, channel_multiplier=1,
                      allow_small_or_imprecise_dtypes=True).then_inc(s_const, 1)
            pool.wait_ge(s_const, 12)

            def body(s, b, live):
                if live(0):
                    norm_rstd(pool, mv[b], ve, rstd[b], eps, half, s, s_mv, s_ve, s_rstd, s_h)

            pipeline(pool, G, 4, body)
            for c in range(B // CH):
                g = slice(c * CH, (c + 1) * CH)
                pool.wait_ge(s_att, c + 1)
                pool.tensor_tensor(at_num[:, g, 1, :], at_tile[:, g, :],
                                   graph[:, g].unsqueeze(2).to_broadcast([P, CH, rt.tiles]),
                                   ALU.mult).then_inc(s_graph, 1)

        @block.scalar
        def _(act):
            act.dma_start(w1s[:, :], w1).then_inc(s_w, 16)
            for c in range(C):
                act.dma_start(b1s[:, c:c + 1], b1[c * P:(c + 1) * P].rearrange("(p z) -> p z", z=1)).then_inc(s_w, 16)
            act.dma_start(wgs[:, :, :], wg.rearrange("(c p) e -> p c e", p=P)).then_inc(s_w, 16)
            act.dma_start(bgs[:, :], bg.rearrange("(p z) -> p z", z=1)).then_inc(s_w, 16)
            act.wait_ge(s_w, 16 * (C + 3))
            act.activation(w1p[0][:, :], w1s[:, :], ACT.Copy).then_inc(s_whi, 1)
            act.activation(wgp[0][:, :, :], wgs[:, :, :], ACT.Copy).then_inc(s_whi, 1)

            def body(s, b, live):
                c = 1 - b
                if live(1):
                    passed(act, s_T, s - 1)
                    passed(act, s_G, s - 3, C)
                    act.activation(hT[c][0][:, :, :], T_ps[:, :, :], ACT.Copy).then_inc(s_hT, 1)
                if live(2):
                    def high(k):
                        within(act, s_HT, s - 2, C, k + 1)
                        act.activation(HTp[b][0][:, k, :, :], HT[b][:, k, :, :], ACT.Copy).then_inc(s_HTh, 1)

                    passed(act, s_HTl, s - 4, C)
                    passed(act, s_L, s - 4)
                    for k in range(C):
                        within(act, s_G, s - 2, C, k + 1)
                        act.activation(HT[b][:, k, :, :], G_ps[k][:, :, :], ACT.Gelu,
                                       bias=b1s[:, k:k + 1]).then_inc(s_HT, 1)
                        if k:
                            high(k - 1)
                    high(C - 1)

            pipeline(act, G, 4, body)
            act.wait_ge(s_max, 1)
            act.activation(ex[:, :, :], top[:, :, :], ACT.Exp).then_inc(s_ex, 1)
            for c in range(B // CH):
                g = slice(c * CH, (c + 1) * CH)
                act.wait_ge(s_att, c + 1)
                act.activation(at_num[:, g, 0, :], at_tile[:, g, :], ACT.Copy, scale=iota_q[:, 0:1]).then_inc(s_place, 1)

        @block.vector
        def _(dve):
            dve.wait_ge(s_w, 16 * (C + 3))
            dve.wait_ge(s_const, 12)
            dve.wait_ge(s_whi, 2)
            dve.tensor_tensor(w1p[1][:, :], w1s[:, :], w1p[0][:, :].bitcast(F32), ALU.subtract).then_inc(s_wlo, 1)
            dve.tensor_tensor(wgp[1][:, :, :], wgs[:, :, :], wgp[0][:, :, :].bitcast(F32),
                              ALU.subtract).then_inc(s_wlo, 1)

            def body(s, b, live):
                c = 1 - b
                if live(1):
                    passed(dve, s_T, s - 3)
                    if not (isinstance(s, int) and s < 3):
                        dve.wait_ge(s_hd[c], pair(s - 3, c))
                    norm_apply(dve, xt[c], mv[c], rstd[c], h[c], s - 1, s_rstd, s_h)
                if live(0):
                    dve.wait_ge(s_x[b], pair(s, b))
                    passed(dve, s_mv, s - 1, GT)
                    norm_stats(dve, xt[b], st, mv[b], tick, s, s_st, s_mv)
                if live(4):
                    passed(dve, s_L, s - 4)
                    passed(dve, s_N, s - 5)
                    dve.tensor_tensor(lgT[:, :, :], L_ps[0:E, :, :],
                                      bgs[:, 0:1].unsqueeze(2).to_broadcast([E, GT, P]), ALU.add).then_inc(s_lgT, 1)
                if live(3):
                    passed(dve, s_L, s - 5)
                    for k in range(C):
                        within(dve, s_HTh, s - 3, C, k + 1)
                        dve.tensor_tensor(HTp[c][1][:, k, :, :], HT[c][:, k, :, :],
                                          HTp[c][0][:, k, :, :].bitcast(F32), ALU.subtract).then_inc(s_HTl, 1)
                if live(1):
                    passed(dve, s_hT, s - 1)
                    dve.tensor_tensor(hT[c][1][:, :, :], T_ps[:, :, :], hT[c][0][:, :, :].bitcast(F32),
                                      ALU.subtract).then_inc(s_hTl, 1)
                if live(4):
                    passed(dve, s_N, s - 4)
                    dve.tensor_copy(lg[:, bass.ts(s - 4, GT), :], N_ps[:, :, :]).then_inc(s_lg, 1)

            pipeline(dve, G, 4, body)

            n = [0]

            def then(ins):
                n[0] += 1
                ins.then_inc(s_r, 1)
                dve.wait_ge(s_r, n[0])

            dve.wait_ge(s_lg, G)
            then(dve.tensor_reduce(mx[:, :], lg[:, :, :], AX, ALU.max))
            mx_e = mx[:, :].unsqueeze(2).to_broadcast([P, B, E])
            dve.tensor_tensor(top[:, :, :], lg[:, :, :], mx_e, ALU.subtract).then_inc(s_max, 1)
            then(dve.tensor_tensor(oh[:, :, :], lg[:, :, :], mx_e, ALU.is_equal))
            then(dve.scalar_tensor_tensor(out=first[:, :, :], in0=oh[:, :, :], scalar=-float(E),
                                          in1=iota_e[:, :, :], op0=ALU.mult, op1=ALU.add))
            then(dve.tensor_reduce(idx[:, :], first[:, :, :], AX, ALU.min))
            dve.tensor_tensor(oh[:, :, :], first[:, :, :], idx[:, :].unsqueeze(2).to_broadcast([P, B, E]),
                              ALU.is_equal).then_inc(s_oh, 1)
            dve.wait_ge(s_ex, 1)
            then(dve.tensor_reduce(den[:, :], ex[:, :, :], AX, ALU.add))
            then(dve.reciprocal(rt.ptop[:, :], den[:, :]))
            dve.wait_ge(s_cnt, 2)
            for k in range(E):
                sc = dve.tensor_tensor_scan(inc[:, :, k], ones[:, 0:B], G_ps[0][:, :, :].rearrange(
                    "p t (u e) -> p (t u) e", e=E)[:, :, k], 0.0, ALU.mult, ALU.add)
            then(sc)
            then(dve.tensor_tensor(off[:, :, :], inc[:, :, :], G_ps[0][:, :, :].rearrange(
                "p t (u e) -> p (t u) e", e=E), ALU.subtract))
            then(dve.tensor_tensor(off[:, :, :], off[:, :, :], G_ps[1][:, :, :].rearrange(
                "p t (u e) -> p (t u) e", e=E), ALU.add))
            then(dve.tensor_scalar(cnt_i[:, :], inc[:, B - 1, :], float(P - 1), None, ALU.add))
            shift = P.bit_length() - 1
            then(dve.tensor_scalar(pad_i[:, :], cnt_i[:, :], shift, shift, ALU.arith_shift_right,
                                   ALU.arith_shift_left))
            then(dve.tensor_copy(pad[:, :], pad_i[:, :]))
            then(dve.tensor_tensor_scan(end[:, :], ones[:, 0:E], pad[:, :], 0.0, ALU.mult, ALU.add))
            then(dve.tensor_tensor(start[:, :], end[:, :], pad[:, :], ALU.subtract))
            then(dve.tensor_tensor(off[:, :, :], off[:, :, :], start[:, :].unsqueeze(1).to_broadcast([P, B, E]),
                                   ALU.add))
            then(dve.tensor_tensor(off[:, :, :], off[:, :, :], oh[:, :, :], ALU.mult))
            then(dve.tensor_reduce(pos[:, :], off[:, :, :], AX, ALU.add))
            then(dve.tensor_copy(rt.row[:, :], pos[:, :]))
            then(dve.tensor_scalar(hi_i[:, :], rt.row[:, :], shift, None, ALU.arith_shift_right))
            dve.tensor_copy(hi[:, :], hi_i[:, :]).then_inc(s_hilo, 1)
            then(dve.tensor_scalar(lo_i[:, :], rt.row[:, :], P - 1, None, ALU.bitwise_and))
            dve.tensor_copy(lo[:, :], lo_i[:, :]).then_inc(s_hilo, 1)
            dve.wait_ge(s_hilo, 2)
            for c in range(B // CH):
                g = slice(c * CH, (c + 1) * CH)
                dve.tensor_tensor(at_tile[:, g, :], iota_t[:, :].unsqueeze(1).to_broadcast([P, CH, rt.tiles]),
                                  hi[:, g].unsqueeze(2).to_broadcast([P, CH, rt.tiles]),
                                  ALU.is_equal).then_inc(s_att, 1)
                dve.tensor_tensor(at_row[:, g, :], iota_p[:, :].unsqueeze(1).to_broadcast([P, CH, P]),
                                  lo[:, g].unsqueeze(2).to_broadcast([P, CH, P]), ALU.is_equal).then_inc(s_atr, 1)
            then(dve.tensor_tensor(full[:, :, :], end[:, :].unsqueeze(1).to_broadcast([P, rt.tiles, E]),
                                   iota_j[:, :, :], ALU.is_le))
            then(dve.tensor_reduce(tex[:, :], full[:, :, :], AX, ALU.add))
            then(dve.tensor_scalar(rt.expert[:, :], tex[:, :], float(E - 1), None, ALU.min))
            dve.wait_ge(s_inv, 1)
            dve.tensor_copy(place[:, :], L_ps[:, 0, 0:rt.tiles]).then_inc(s_place, 1)
            dve.wait_ge(s_place, B // CH + 1)
            dve.scalar_tensor_tensor(out=rt.node[:, :], in0=L_ps[:, 1, 0:rt.tiles], scalar=float(P),
                                     in1=place[:, :], op0=ALU.mult, op1=ALU.add)

        @block.tensor
        def _(pe):
            pe.wait_ge(s_w, 16 * (C + 3))
            pe.wait_ge(s_const, 6)
            pe.wait_ge(s_wlo, 2)

            def body(s, b, live):
                c = 1 - b
                if live(1):
                    passed(pe, s_h, s - 1, GT)
                    passed(pe, s_hTl, s - 2)
                    for t in range(GT):
                        mm = pe.transpose(T_ps[:, t, :], h[c][:, t, :], ident[:, :])
                    mm.then_inc(s_T, 1)
                if live(2):
                    passed(pe, s_hTl, s - 2)
                    for k in range(C):
                        passed_half(pe, s_HT, s - 3, C, k + 1)
                        for n, (u, v) in enumerate(PARTS):
                            mm = pe.matmul(G_ps[k][:, :, :], w1p[u][:, k * P:(k + 1) * P], hT[b][v][:, :, :],
                                           start=(n == 0), stop=(n == len(PARTS) - 1))
                        mm.then_inc(s_G, 1)
                if live(4):
                    passed(pe, s_lgT, s - 4)
                    passed(pe, s_lg, s - 5)
                    for t in range(GT):
                        mm = pe.matmul(N_ps[:, t, :], lgT[:, t, :], ident[0:E, 0:E], start=True, stop=True)
                    mm.then_inc(s_N, 1)
                if live(3):
                    passed(pe, s_HTl, s - 3, C)
                    passed(pe, s_lgT, s - 4)
                    for k in range(C):
                        for n, (u, v) in enumerate(PARTS):
                            mm = pe.matmul(L_ps[0:E, :, :], wgp[u][:, k, :], HTp[c][v][:, k, :, :],
                                           start=(k == n == 0), stop=(k == C - 1 and n == len(PARTS) - 1))
                    mm.then_inc(s_L, 1)

            pipeline(pe, G, 4, body)
            pe.wait_ge(s_oh, 1)
            oh2 = oh[:, :, :].rearrange("p t e -> p (t e)")
            flat = [g[:, :, :].rearrange("p t d -> p (t d)") for g in G_ps]
            pe.matmul(flat[0], ones[:, :], oh2, start=True, stop=True).then_inc(s_cnt, 1)
            pe.matmul(flat[1], before[:, :], oh2, start=True, stop=True).then_inc(s_cnt, 1)
            for c in range(B // CH):
                pe.wait_ge(s_atr, c + 1)
                pe.wait_ge(s_place, c + 1)
                pe.wait_ge(s_graph, c + 1)
                for t in range(c * CH, (c + 1) * CH):
                    mm = pe.matmul(L_ps[:, 0:2, 0:rt.tiles], at_row[:, t, :], at_num[:, t, :, :],
                                   start=(t == 0), stop=(t == B - 1))
            mm.then_inc(s_inv, 1)


def experts(nc, rt, h_rows, y_rows, E, next_weights):
    G = rt.tiles // GT
    C = rt.b1s.shape[1]
    yg = y_rows.rearrange("(g t p) d -> g p t d", t=GT, p=P)
    with ExitStack() as ctx:
        m = Space(nc, ctx, "ex")
        sb, bank, sem = m.sb, m.bank, m.sem
        ident, ones = sb("ident", [P, P]), sb("ones", [1, P])
        w1p, b1s, wds, bds = rt.w1p, rt.b1s, rt.wds, rt.bds
        h = [sb(f"h{b}", [P, GT, D]) for b in range(2)]
        hT = [[sb(f"hT{b}{n}", [P, GT, P], F32R) for n in range(2)] for b in range(2)]
        HT = [sb(f"HT{b}", [P, C, GT, P]) for b in range(2)]
        y = [sb(f"y{b}", [P, GT, D]) for b in range(2)]
        T_ps, Y_ps = bank("T", [P, GT, P]), bank("Y", [P, GT, D])
        G_ps = [bank(f"G{c}", [P, GT, P]) for c in range(C)]
        node = [sb(f"node{b}", [P, GT], I32) for b in range(2)]
        zero, ptick = sb("zero", [P, 1]), sb("ptick", [P, 1])
        s_const, s_gate, s_node = sem("const"), sem("gate"), sem("node")
        s_hl, s_out = [sem(f"hl{b}") for b in range(2)], [sem(f"out{b}") for b in range(2)]
        s_T, s_hT, s_hTl, s_G, s_HT, s_Y, s_y = (
            sem(n) for n in ("T", "hT", "hTl", "G", "HT", "Y", "y"))
        block = ctx.enter_context(nc.Block())

        @block.sync
        def _(sp):
            next_weights.load(sp)

            def body(s, b, live):
                if live(3):
                    passed(sp, s_y, s - 3)
                    sp.dma_start(yg[s - 3], y[1 - b][:, :, :]).then_inc(s_out[1 - b], 16)

            pipeline(sp, G, 3, body)
            for b in range(2):
                sp.wait_ge(s_out[b], 16 * (G // 2))

        @block.gpsimd
        def _(pool):
            make_identity(nc, pool, ident, s_const)
            pool.memset(ones[:, :], 1.0).then_inc(s_const, 1)
            pool.memset(zero[:, :], 0.0).then_inc(s_const, 1)
            pool.wait_ge(s_const, 4)

            def body(s, b, live):
                if live(0):
                    passed(pool, s_node, s)
                    passed(pool, s_T, s - 2)
                    gate(pool, ptick, zero, s, s_gate)
                    for t in range(GT):
                        pool.indirect_dma_start(h[b][:, t, :], None, h_rows,
                                                bass.IndirectOffsetOnAxis(node[b][:, t:t + 1], 0)).then_inc(s_hl[b], 16)

            pipeline(pool, G, 3, body)

        @block.scalar
        def _(act):
            def body(s, b, live):
                c = 1 - b
                if live(1):
                    passed(act, s_T, s - 1)
                    passed(act, s_G, s - 3, C)
                    act.activation(hT[c][0][:, :, :], T_ps[:, :, :], ACT.Copy).then_inc(s_hT, 1)
                if live(2):
                    passed(act, s_Y, s - 4)
                    for k in range(C):
                        within(act, s_G, s - 2, C, k + 1)
                        act.activation(HT[b][:, k, :, :], G_ps[k][:, :, :], ACT.Gelu,
                                       bias=b1s[:, k:k + 1]).then_inc(s_HT, 1)

            pipeline(act, G, 3, body)

        @block.vector
        def _(dve):
            dve.tensor_copy(node[0][:, :], rt.node[:, 0:GT]).then_inc(s_node, 1)
            dve.tensor_copy(node[1][:, :], rt.node[:, GT:2 * GT]).then_inc(s_node, 1)

            def body(s, b, live):
                c = 1 - b
                if live(0) and not (isinstance(s, int) and s < 2):
                    dve.wait_ge(s_hl[b], pair_gt(s - 2, b))
                    dve.tensor_copy(node[b][:, :], rt.node[:, bass.ts(s, GT)]).then_inc(s_node, 1)
                if live(1):
                    passed(dve, s_hT, s - 1)
                    passed(dve, s_G, s - 3, C)
                    dve.tensor_tensor(hT[c][1][:, :, :], T_ps[:, :, :], hT[c][0][:, :, :].bitcast(F32),
                                      ALU.subtract).then_inc(s_hTl, 1)
                if live(3):
                    passed(dve, s_Y, s - 3)
                    if not (isinstance(s, int) and s < 5):
                        dve.wait_ge(s_out[c], pair(s - 5, c))
                    dve.tensor_copy(y[c][:, :, :], Y_ps[:, :, :]).then_inc(s_y, 1)

            pipeline(dve, G, 3, body)

        @block.tensor
        def _(pe):
            pe.wait_ge(s_const, 3)

            def body(s, b, live):
                c = 1 - b
                if live(3):
                    own = [pe.value_load(rt.expert[0:1, bass.ts((s - 3) * GT + t, 1)], min_val=0, max_val=E - 1)
                           for t in range(GT)]
                if live(1):
                    pe.wait_ge(s_hl[c], pair_gt(s - 1, c))
                    passed(pe, s_hTl, s - 2)
                    for t in range(GT):
                        mm = pe.transpose(T_ps[:, t, :], h[c][:, t, :], ident[:, :])
                    mm.then_inc(s_T, 1)
                if live(3):
                    passed(pe, s_HT, s - 3, C)
                    passed(pe, s_y, s - 4)
                    for t in range(GT):
                        for k in range(C):
                            pe.matmul(Y_ps[:, t, :], HT[c][:, k, t, :], wds[:, k, bass.ts(own[t], D)],
                                      start=(k == 0), stop=False)
                        mm = pe.matmul(Y_ps[:, t, :], ones[:, :], bds[:, bass.ts(own[t], D)], start=False, stop=True)
                    mm.then_inc(s_Y, 1)
                if live(2):
                    passed(pe, s_hTl, s - 2)
                    for k in range(C):
                        passed_half(pe, s_HT, s - 3, C, k + 1)
                        for n, (u, v) in enumerate(PARTS):
                            mm = pe.matmul(G_ps[k][:, :, :], w1p[u][:, k * P:(k + 1) * P], hT[b][v][:, :, :],
                                           start=(n == 0), stop=(n == len(PARTS) - 1))
                        mm.then_inc(s_G, 1)

            pipeline(pe, G, 3, body)


def typed_attention(nc, x1, rt, y_rows, adj, a_all, bias, x3):
    B = x1.shape[0]
    G = B // GT
    K = len(a_all)
    HG = GT // 2
    xg, adjg, x3g = gather_view(x1), gather_view(adj), gather_view(x3)
    with ExitStack() as ctx:
        m = Space(nc, ctx, "ta")
        sb, bank, sem = m.sb, m.bank, m.sem

        def two(name, shape, dt=F32):
            return [sb(f"{name}{b}", shape, dt) for b in range(2)]

        ident = sb("ident", [P, P])
        half, eps, zero = sb("half", [P, GT]), sb("eps", [P, GT]), sb("zero", [P, GT])
        tick, ptick, ptick2 = sb("tick", [P, 1 + 2 * K]), sb("ptick", [P, 1]), sb("ptick2", [P, 1])
        acol, brow, ones = sb("acol", [P, K]), sb("brow", [1, D]), sb("ones", [1, P])
        row, pt = two("row", [P, GT], I32), two("pt", [P, GT])
        xt, yt, x2, xb, xo = (two(n, [P, GT, D]) for n in ("x", "y", "x2", "xb", "xo"))
        aj = two("adj", [P, GT, P], I32)
        st, ve = sb("st", [P, GT, 6]), sb("ve", [P, GT])
        mv, rstd = two("mv", [P, GT, 2]), two("rstd", [P, GT])
        h, hk = two("h", [P, GT, D]), two("hk", [P, GT, D])
        hT, hTa = two("hT", [P, GT, P]), two("hTa", [P, K, GT, P])
        is_k = two("is_k", [P, K, GT, P], I32)
        sel, lk, al, alT = (two(n, [P, GT, P]) for n in ("sel", "lk", "al", "alT"))
        T_ps, AT_ps, U_ps = (bank(n, [P, GT, P]) for n in ("T", "AT", "U"))
        E_ps = [bank(f"E{i}", [P, HG, K, P]) for i in range(2)]

        s_w, s_const, s_gate, s_gate2, s_isk_pool = (sem(n) for n in ("w", "const", "gate", "gate2", "isk_pool"))
        KV = K // 2
        s_x, s_y, s_adj, s_hk, s_out = ([sem(f"{n}{b}") for b in range(2)] for n in ("x", "y", "adj", "hk", "out"))
        s_st, s_mv, s_ve, s_rstd, s_h = sem("st"), sem("mv"), sem("ve"), sem("rstd"), sem("h")
        (s_row, s_x2, s_T, s_hT, s_hTa, s_isk, s_fill, s_E, s_sel, s_lk, s_al, s_AT, s_alT, s_U, s_xb, s_xo) = (
            sem(n) for n in ("row", "x2", "T", "hT", "hTa", "isk", "fill", "E", "sel", "lk", "al", "AT", "alT",
                             "U", "xb", "xo"))
        block = ctx.enter_context(nc.Block())

        @block.sync
        def _(sp):
            for k in range(K):
                sp.dma_start(acol[:, k:k + 1], a_all[k]).then_inc(s_w, 16)
            sp.dma_start(brow[:, :], bias.rearrange("(z d) -> z d", z=1)).then_inc(s_w, 16)

            def body(s, b, live):
                c = 1 - b
                if live(0):
                    passed(sp, s_x2, s - 2, GT)
                    sp.dma_start(xt[b][:, :, :], xg[s]).then_inc(s_x[b], 16)
                if live(1):
                    passed(sp, s_isk, s - 3, KV)
                    passed(sp, s_isk_pool, s - 3, K - KV)
                    sp.dma_start(aj[c][:, :, :], adjg[s - 1]).then_inc(s_adj[c], 16)
                if live(2):
                    passed(sp, s_h, s - 2, GT)
                    passed(sp, s_U, s - 4)
                    sp.dma_start(hk[b][:, :, :], h[b][:, :, :]).then_inc(s_hk[b], 16)
                if live(5):
                    passed(sp, s_xo, s - 5)
                    sp.dma_start(x3g[s - 5], xo[c][:, :, :]).then_inc(s_out[c], 16)

            pipeline(sp, G, 5, body)
            for b in range(2):
                sp.wait_ge(s_out[b], 16 * (G // 2))

        @block.gpsimd
        def _(pool):
            pool.memset(zero[:, :], 0.0).then_inc(s_const, 1)
            pool.memset(half[:, :], -0.5).then_inc(s_const, 1)
            pool.memset(eps[:, :], EPS).then_inc(s_const, 1)
            make_identity(nc, pool, ident, s_const, 3)
            pool.memset(ones[:, :], 1.0).then_inc(s_const, 1)
            pool.wait_ge(s_const, 6)
            pool.wait_ge(s_w, 16 * (K + 1))

            def body(s, b, live):
                c = 1 - b
                if live(0):
                    passed(pool, s_row, s, 2)
                    passed(pool, s_x2, s - 2, GT)
                    gate(pool, ptick, zero, s, s_gate)
                    for t in range(GT):
                        pool.indirect_dma_start(yt[b][:, t, :], None, y_rows,
                                                bass.IndirectOffsetOnAxis(row[b][:, t:t + 1], 0)).then_inc(s_y[b], 16)
                if live(1):
                    norm_rstd(pool, mv[c], ve, rstd[c], eps, half, s - 1, s_mv, s_ve, s_rstd, s_h)
                if live(2):
                    passed(pool, s_lk, s - 4)
                    pool.wait_ge(s_adj[b], pair(s - 2, b))
                    passed(pool, s_sel, s - 4, 2 * K)
                    gate(pool, ptick2, zero, s - 2, s_gate2)
                    pool.memset(sel[b][:, :, :], -BIG).then_inc(s_fill, 1)
                    for k in range(KV, K):
                        pool.tensor_scalar(is_k[b][:, k, :, :], aj[b][:, :, :], float(k + 1), None,
                                           ALU.is_equal).then_inc(s_isk_pool, 1)

            pipeline(pool, G, 4, body)

        @block.scalar
        def _(act):
            act.wait_ge(s_w, 16 * (K + 1))

            def body(s, b, live):
                c = 1 - b
                if live(2):
                    passed(act, s_T, s - 2)
                    passed(act, s_E, s - 4, 2)
                    act.activation(hT[b][:, :, :], T_ps[:, :, :], ACT.Copy).then_inc(s_hT, 1)
                if live(2):
                    passed(act, s_hT, s - 2)
                    for k in range(K):
                        act.activation(hTa[b][:, k, :, :], hT[b][:, :, :], ACT.Copy,
                                       scale=acol[:, k:k + 1]).then_inc(s_hTa, 1)
                if live(4):
                    passed(act, s_AT, s - 4)
                    act.activation(alT[b][:, :, :], AT_ps[:, :, :], ACT.Copy).then_inc(s_alT, 1)
                if live(3):
                    passed(act, s_lk, s - 3)
                    passed(act, s_AT, s - 5)
                    act.activation(al[c][:, :, :], lk[c][:, :, :], ACT.Sigmoid).then_inc(s_al, 1)
                if live(2):
                    passed(act, s_x2, s - 2, GT)
                    passed(act, s_xo, s - 4)
                    act.activation(xb[b][:, :, :], x2[b][:, :, :], ACT.Copy).then_inc(s_xb, 1)

            pipeline(act, G, 4, body)

        @block.vector
        def _(dve):
            def take_routing(s, b):
                if not (isinstance(s, int) and s < 2):
                    dve.wait_ge(s_y[b], pair_gt(s - 2, b))
                passed(dve, s_x2, s - 2, GT)
                dve.tensor_copy(row[b][:, :], rt.row[:, bass.ts(s, GT)]).then_inc(s_row, 1)
                dve.tensor_copy(pt[b][:, :], rt.ptop[:, bass.ts(s, GT)]).then_inc(s_row, 1)

            def body(s, b, live):
                c = 1 - b

                def select(k, i):
                    n = 2 * k + i
                    if k:
                        within(dve, s_sel, s - 3, 2 * K, n - 1)
                    dve.memset(tick[:, 1 + n:2 + n], 0.0)
                    dve.copy_predicated(sel[c][:, i * HG:(i + 1) * HG, :],
                                        is_k[c][:, k, i * HG:(i + 1) * HG, :],
                                        E_ps[i][:, :, k, :]).then_inc(s_sel, 1)

                if live(0):
                    take_routing(s, b)
                if live(2):
                    if not (isinstance(s, int) and s < 4):
                        dve.wait_ge(s_hk[b], pair(s - 4, b))
                    passed(dve, s_T, s - 4)
                    norm_apply(dve, x2[b], mv[b], rstd[b], h[b], s - 2, s_rstd, s_h)
                if live(1):
                    passed(dve, s_row, s - 1, 2)
                    dve.wait_ge(s_x[c], pair(s - 1, c))
                    dve.wait_ge(s_y[c], pair_gt(s - 1, c))
                    passed(dve, s_xb, s - 3)
                    passed(dve, s_h, s - 3, GT)
                    for t in range(GT):
                        dve.scalar_tensor_tensor(out=x2[c][:, t, :], in0=yt[c][:, t, :], scalar=pt[c][:, t:t + 1],
                                                 in1=xt[c][:, t, :], op0=ALU.mult, op1=ALU.add).then_inc(s_x2, 1)
                    passed(dve, s_mv, s - 2, GT)
                    passed(dve, s_x2, s - 1, GT)
                    norm_stats(dve, x2[c], st, mv[c], tick, s - 1, s_st, s_mv)
                if live(2):
                    dve.wait_ge(s_adj[b], pair(s - 2, b))
                    passed(dve, s_sel, s - 4, 2 * K)
                    for k in range(KV):
                        dve.tensor_scalar(is_k[b][:, k, :, :], aj[b][:, :, :], float(k + 1), None,
                                          ALU.is_equal).then_inc(s_isk, 1)
                if live(3):
                    passed(dve, s_isk, s - 3, KV)
                    passed(dve, s_isk_pool, s - 3, K - KV)
                    passed(dve, s_fill, s - 3)
                    passed(dve, s_E, s - 3, 2)
                    for k in range(K):
                        for i in range(2):
                            select(k, i)
                    passed(dve, s_sel, s - 3, 2 * K)
                    passed(dve, s_al, s - 5)
                    dve.scalar_tensor_tensor(out=lk[c][:, :, :], in0=sel[c][:, :, :], scalar=0.2,
                                             in1=sel[c][:, :, :], op0=ALU.mult, op1=ALU.max).then_inc(s_lk, 1)
                if live(4):
                    passed(dve, s_U, s - 4)
                    passed(dve, s_xb, s - 4)
                    if not (isinstance(s, int) and s < 6):
                        dve.wait_ge(s_out[b], pair(s - 6, b))
                    dve.tensor_tensor(xo[b][:, :, :], U_ps[:, :, :], xb[b][:, :, :], ALU.add).then_inc(s_xo, 1)

            pipeline(dve, G, 4, body)

        @block.tensor
        def _(pe):
            pe.wait_ge(s_const, 6)
            pe.wait_ge(s_w, 16 * (K + 1))

            def body(s, b, live):
                c = 1 - b

                def scores(i):
                    passed_half(pe, s_sel, s - 4, 2 * K, 2 * K - 1 + i)
                    for t in range(i * HG, (i + 1) * HG):
                        mm = pe.matmul(E_ps[i][:, t - i * HG, :, :], hT[c][:, t, :], hTa[c][:, :, t, :],
                                       start=True, stop=True)
                    mm.then_inc(s_E, 1)

                if live(3):
                    passed(pe, s_hTa, s - 3, K)
                    scores(0)
                if live(2):
                    passed(pe, s_h, s - 2, GT)
                    passed(pe, s_hT, s - 3)
                    for t in range(GT):
                        mm = pe.transpose(T_ps[:, t, :], h[b][:, t, :], ident[:, :])
                    mm.then_inc(s_T, 1)
                if live(3):
                    scores(1)
                if live(4):
                    passed(pe, s_al, s - 4)
                    passed(pe, s_alT, s - 5)
                    for t in range(GT):
                        mm = pe.transpose(AT_ps[:, t, :], al[b][:, t, :], ident[:, :])
                    mm.then_inc(s_AT, 1)
                    passed(pe, s_alT, s - 4)
                    pe.wait_ge(s_hk[b], pair(s - 4, b))
                    passed(pe, s_xo, s - 5)
                    for t in range(GT):
                        pe.matmul(U_ps[:, t, :], alT[b][:, t, :], hk[b][:, t, :], start=True, stop=False)
                        mm = pe.matmul(U_ps[:, t, :], ones[:, :], brow[:, :], start=False, stop=True)
                    mm.then_inc(s_U, 1)

            pipeline(pe, G, 4, body)


class MambaWeights:

    def __init__(self, nc, ctx, w_in, conv_w, conv_b, dt_bias, a_log, d_skip, norm_w, w_out, w_lin, b_lin):
        m = Space(nc, ctx, "mw")
        self.dram = (w_in, conv_w, conv_b, dt_bias, a_log, d_skip, norm_w, w_out, w_lin, b_lin)
        self.heads, self.inner = dt_bias.shape[0], norm_w.shape[0]
        self.conv, self.taps = conv_w.shape
        H, C, CC = self.heads, self.inner // P, self.conv // P
        self.win = m.sb("win", [P, w_in.shape[1]])
        self.cw, self.cb = m.sb("cw", [P, CC, self.taps]), m.sb("cb", [P, CC])
        self.dtb, self.alog = m.sb("dtb", [P, H]), m.sb("alog", [P, H])
        self.dcol, self.nw = m.sb("dcol", [P, C]), m.sb("nw", [P, C])
        self.wout, self.wlin, self.brow = m.sb("wout", [P, C, D]), m.sb("wlin", [P, D]), m.sb("brow", [P, D])
        self.s_w = m.sem("w")
        self.loads = 5 + CC * 2 + 2 * C + H

    def load(self, sp):
        w_in, conv_w, conv_b, dt_bias, a_log, d_skip, norm_w, w_out, w_lin, b_lin = self.dram
        s_w, C, CC, H = self.s_w, self.inner // P, self.conv // P, self.heads
        HC, HD = H // C, self.inner // H

        def col(dst, src):
            sp.dma_start(dst, src.rearrange("(p z) -> p z", z=1)).then_inc(s_w, 16)

        sp.dma_start(self.win[:, :], w_in).then_inc(s_w, 16)
        for j in range(CC):
            sp.dma_start(self.cw[:, j, :], conv_w[j * P:(j + 1) * P, :]).then_inc(s_w, 16)
            col(self.cb[:, j:j + 1], conv_b[j * P:(j + 1) * P])
        sp.dma_start(self.dtb[:, :], dt_bias.partition_broadcast(P)).then_inc(s_w, 16)
        sp.dma_start(self.alog[:, :], a_log.partition_broadcast(P)).then_inc(s_w, 16)
        for k in range(H):
            sp.dma_start(self.dcol[k % HC * HD:(k % HC + 1) * HD, k // HC:k // HC + 1],
                         d_skip[k:k + 1].partition_broadcast(HD)).then_inc(s_w, 16)
        for j in range(C):
            col(self.nw[:, j:j + 1], norm_w[j * P:(j + 1) * P])
            sp.dma_start(self.wout[:, j, :], w_out[j * P:(j + 1) * P, :]).then_inc(s_w, 16)
        sp.dma_start(self.wlin[:, :], w_lin).then_inc(s_w, 16)
        sp.dma_start(self.brow[:, :], b_lin.partition_broadcast(P)).then_inc(s_w, 16)


def mamba_block(nc, x, w, x4):
    B = x.shape[0]
    G = B // GT
    H = w.heads
    DI = w.inner
    C = DI // P
    HC = H // C
    HD = DI // H
    NS = (w.conv - DI) // 2
    TAPS = w.taps
    DT0 = DI + w.conv
    xg, x4g = gather_view(x), gather_view(x4)
    with ExitStack() as ctx:
        m = Space(nc, ctx, "mb")
        sb, bank, sem = m.sb, m.bank, m.sem
        ident, ones = sb("ident", [P, P]), sb("ones", [P, P])
        upto = sb("upto", [P, P])
        above = sb("above", [P, P], F32R)
        half, eps, zero = sb("half", [P, GT]), sb("eps", [P, GT]), sb("zero", [P, GT])
        tick, ptick = sb("tick", [P, 8]), sb("ptick", [P, 1])
        win, cw, cb, dtb, alog, dcol, nw, wout, wlin, brow, s_w = (
            w.win, w.cw, w.cb, w.dtb, w.alog, w.dcol, w.nw, w.wout, w.wlin, w.brow, w.s_w)
        nega, woutT = sb("nega", [P, H]), sb("woutT", [P, C, P])
        wol = sb("wol", [P, C, D])

        def two(name, shape, dt=F32):
            return [sb(f"{name}{b}", shape, dt) for b in range(2)]

        xt, xr, xb, xo, h = (two(n, [P, GT, D]) for n in ("x", "xr", "xb", "xo", "h"))
        st, ve = sb("st", [P, GT, 6]), sb("ve", [P, GT])
        mv, rstd = two("mv", [P, GT, 2]), two("rstd", [P, GT])
        mr, nmr = sb("mr", [P, GT]), two("nmr", [P, GT])
        hT = two("hT", [P, GT, P])
        cv = [two(f"cv{j}_", [P, GT, P]) for j in range(C + 1)]
        xs = [two(f"xs{j}_", [P, GT, P]) for j in range(C)]
        bs, cs = two("bs", [NS, GT, P]), two("cs", [NS, GT, P])
        sz = [two(f"sz{j}_", [P, GT, P]) for j in range(C)]
        dr, dn, dm, du, dd, dq, dz, dz2, dp, dp2 = (
            sb(n, [P, GT, H]) for n in ("dr", "dn", "dm", "du", "dd", "dq", "dz", "dz2", "dp", "dp2"))
        dt, da = two("dt", [P, GT, H]), two("da", [P, GT, H])
        dap = [two(f"da{n}_", [P, GT, H], F32R) for n in range(2)]
        sg = [two(f"sg{n}_", [P, GT, H, P], F32R) for n in range(2)]
        ls = two("ls", [P, GT, H, P])
        gm = two("gm", [P, GT, P])
        xdt = two("xdt", [P, GT, H, HD])
        y1 = [sb(f"y1_{j}", [P, GT, P]) for j in range(C)]
        y2 = [two(f"y2_{j}_", [P, GT, P]) for j in range(C)]
        sq = [sb(f"sq{j}", [P, GT, P]) for j in range(C)]
        vs, rr = sb("vs", [P, GT]), sb("rr", [P, GT])

        T_ps = bank("T", [P, GT, P])
        X_ps = [bank(f"X{j}", [P, GT, P]) for j in range(C + 1)]
        Y_ps = [bank(f"Y{j}", [P, GT, P]) for j in range(C)]
        R_ps = [bank(f"R{j}", [P, GT, P]) for j in range(2)]
        dt_ps = R_ps[1][:, 0, 0:GT * H].rearrange("p (t h) -> p t h", t=GT)
        ss_ps = R_ps[1][:, 1, 0:GT]

        s_const, s_prep = sem("const"), sem("prep")
        s_x, s_xr, s_out = ([sem(f"{n}{b}") for b in range(2)] for n in ("x", "xr", "out"))
        s_st, s_mv, s_ve, s_rstd, s_h = sem("st"), sem("mv"), sem("ve"), sem("rstd"), sem("h")
        (s_T, s_hT, s_X, s_cv, s_tap, s_dt, s_dn, s_du, s_dtc, s_da, s_sg, s_Z, s_sz, s_xs, s_seg, s_ls,
         s_G, s_gm, s_xT, s_xdt, s_m, s_Y, s_y1, s_y2, s_sq, s_O, s_SS, s_vs, s_rr, s_xb, s_xo, s_ol, s_dtr) = (
            sem(n) for n in ("T", "hT", "X", "cv", "tap", "dt", "dn", "du", "dtc", "da", "sg", "Z", "sz", "xs",
                             "seg", "ls", "G", "gm", "xT", "xdt", "m", "Y", "y1", "y2", "sq", "O", "SS", "vs",
                             "rr", "xb", "xo", "ol", "dtr"))
        s_mr, s_nmr = sem("mr"), sem("nmr")
        N_W = w.loads
        DTC = 13
        NT = (C + 1) * (TAPS - 1)
        block = ctx.enter_context(nc.Block())

        @block.sync
        def _(sp):
            def body(s, b, live):
                if live(0):
                    passed(sp, s_h, s - 2, GT)
                    sp.dma_start(xt[b][:, :, :], xg[s]).then_inc(s_x[b], 16)
                if live(4):
                    passed(sp, s_xb, s - 6)
                    sp.dma_start(xr[b][:, :, :], xg[s - 4]).then_inc(s_xr[b], 16)
                if live(5):
                    passed(sp, s_xo, s - 5, GT)
                    sp.dma_start(x4g[s - 5], xo[1 - b][:, :, :]).then_inc(s_out[1 - b], 16)

            pipeline(sp, G, 5, body)
            for b in range(2):
                sp.wait_ge(s_out[b], 16 * (G // 2))

        @block.gpsimd
        def _(pool):
            make_identity(nc, pool, ident, s_const)
            pool.memset(half[:, :], -0.5).then_inc(s_const, 1)
            pool.memset(eps[:, :], EPS).then_inc(s_const, 1)
            pool.memset(ones[:, :], 1.0).then_inc(s_const, 1)
            pool.memset(zero[:, :], 0.0).then_inc(s_const, 1)
            pool.wait_ge(s_const, 6)
            pool.affine_select(out=upto[:, :], in_=ones[:, :], compare_op=ALU.is_ge, fill=0.0, base=0,
                               pattern=[[1, P]], channel_multiplier=-1).then_inc(s_const, 1)
            pool.affine_select(out=above[:, :], in_=ones[:, :], compare_op=ALU.is_gt, fill=0.0, base=0,
                               pattern=[[-1, P]], channel_multiplier=1).then_inc(s_const, 1)
            pool.wait_ge(s_const, 8)
            pool.wait_ge(s_w, 16 * N_W)

            def body(s, b, live):
                c = 1 - b
                if live(5):
                    passed(pool, s_O, s - 7)
                    passed(pool, s_sq, s - 7, C)
                    for j in range(C):
                        within(pool, s_y1, s - 5, C, j + 1)
                        pool.tensor_tensor(y2[j][c][:, :, :], y1[j][:, :, :], sz[j][c][:, :, :],
                                           ALU.mult).then_inc(s_y2, 1)
                if live(3):
                    passed(pool, s_da, s - 3, 3)
                    passed(pool, s_seg, s - 5, GT)
                    for n in range(2):
                        pool.tensor_tensor(sg[n][c][:, :, :, :].rearrange("p t h l -> p (t h) l"),
                                           dap[n][c][:, :, :].bitcast(F32).rearrange("p t h -> p (t h)").unsqueeze(2)
                                           .to_broadcast([P, GT * H, P]),
                                           upto[:, :].unsqueeze(1).to_broadcast([P, GT * H, P]),
                                           ALU.mult).then_inc(s_sg, 1)
                if live(5):
                    pool.wait_ge(s_xr[c], pair(s - 5, c))
                    passed(pool, s_xo, s - 7, GT)
                    pool.tensor_tensor(xb[c][:, :, :], xr[c][:, :, :],
                                       brow[:, :].unsqueeze(1).to_broadcast([P, GT, D]), ALU.add).then_inc(s_xb, 1)
                    passed(pool, s_vs, s - 5)
                    passed(pool, s_xo, s - 6, GT)
                    pool.tensor_tensor(rr[:, :], vs[:, :], half[:, :], ALU.pow).then_inc(s_rr, 1)
                if live(0):
                    norm_rstd(pool, mv[b], ve, rstd[b], eps, half, s, s_mv, s_ve, s_rstd, s_h)
                    passed(pool, s_rstd, s)
                    passed(pool, s_nmr, s - 1)
                    pool.tensor_tensor(mr[:, :], mv[b][:, :, 0], rstd[b][:, :], ALU.mult).then_inc(s_mr, 1)
                    passed(pool, s_mr, s)
                    pool.tensor_tensor(nmr[b][:, :], zero[:, :], mr[:, :], ALU.subtract).then_inc(s_nmr, 1)

            pipeline(pool, G, 5, body)

        @block.scalar
        def _(act):
            act.wait_ge(s_w, 16 * N_W)
            act.activation(nega[:, :], alog[:, :], ACT.Exp).then_inc(s_prep, 1)

            def body(s, b, live):
                c = 1 - b
                if live(3):
                    passed(act, s_tap, s - 3, NT)
                    passed(act, s_G, s - 5)
                    act.activation(bs[c][:, :, :], cv[C][c][0:NS, :, :], ACT.Silu).then_inc(s_xs, 1)
                    act.activation(cs[c][:, :, :], cv[C][c][NS:2 * NS, :, :], ACT.Silu).then_inc(s_xs, 1)
                    for j in range(C):
                        passed_half(act, s_y1, s - 5, C, j + 1)
                        act.activation(xs[j][c][:, :, :], cv[j][c][:, :, :], ACT.Silu).then_inc(s_xs, 1)
                if live(2):
                    passed(act, s_xs, s - 4, C + 2)
                    for j in range(C + 1):
                        within(act, s_X, s - 2, C + 1, j + 1)
                        act.activation(cv[j][b][:, :, :], X_ps[j][:, :, :], ACT.Identity,
                                       bias=cb[:, j:j + 1], scale=cw[:, j, TAPS - 1:TAPS]).then_inc(s_cv, 1)
                if live(1):
                    passed(act, s_T, s - 1)
                    passed(act, s_Z, s - 3)
                    act.activation(hT[c][:, :, :], T_ps[:, :, :], ACT.Copy).then_inc(s_hT, 1)
                if live(3):
                    passed(act, s_Z, s - 3)
                    passed(act, s_y2, s - 5, C)
                    for j in range(C):
                        act.activation(sz[j][c][:, :, :], Y_ps[j][:, :, :], ACT.Silu).then_inc(s_sz, 1)
                if live(5):
                    passed(act, s_SS, s - 6)
                    for j in range(C):
                        within(act, s_y2, s - 5, C, j + 1)
                        act.activation(sq[j][:, :, :], y2[j][c][:, :, :], ACT.Square).then_inc(s_sq, 1)
                if live(2):
                    passed(act, s_dn, s - 2)
                    act.activation(du[:, :, :], dn[:, :, :], ACT.Exp).then_inc(s_du, 1)
                if live(3):
                    passed(act, s_Y, s - 5)
                    for t in range(GT):
                        within(act, s_seg, s - 3, GT, t + 1)
                        act.activation(ls[c][:, t, :, :], R_ps[t % 2][:, :, :], ACT.Exp).then_inc(s_ls, 1)
                if live(0):
                    passed(act, s_nmr, s)
                    passed(act, s_T, s - 2)
                    for t in range(GT):
                        act.activation(h[b][:, t, :], xt[b][:, t, :], ACT.Identity, scale=rstd[b][:, t:t + 1],
                                       bias=nmr[b][:, t:t + 1]).then_inc(s_h, 1)

            pipeline(act, G, 5, body)

        @block.vector
        def _(dve):
            dve.wait_ge(s_w, 16 * N_W)
            dve.wait_ge(s_prep, 1)
            dve.tensor_scalar(nega[:, :], nega[:, :], -1.0, None, ALU.mult).then_inc(s_prep, 1)
            dve.wait_ge(s_ol, 1)
            dve.tensor_copy(woutT[:, :, :], T_ps[:, 0:C, :]).then_inc(s_prep, 1)
            dve.wait_ge(s_ol, 2)
            for j in range(C):
                dve.tensor_scalar(wol[:, j, :], R_ps[0][:, j, :], nw[:, j:j + 1], None, ALU.mult).then_inc(s_prep, 1)
            dve.wait_ge(s_prep, 3 + C)
            dve.wait_ge(s_const, 8)

            def body(s, b, live):
                c = 1 - b

                def taps(k, first=0, last=C + 1):
                    for j in range(first, last):
                        if k == 1:
                            within(dve, s_cv, s - 2, C + 1, j + 1)
                        else:
                            within(dve, s_tap, s - 2, NT, (k - 2) * (C + 1) + j + 1)
                        dve.scalar_tensor_tensor(out=cv[j][b][:, :, k:P], in0=X_ps[j][:, :, 0:P - k],
                                                 scalar=cw[:, j, TAPS - 1 - k:TAPS - k],
                                                 in1=cv[j][b][:, :, k:P], op0=ALU.mult,
                                                 op1=ALU.add).then_inc(s_tap, 1)

                def times_dt(j):
                    within(dve, s_xT, s - 3, C, j + 1)
                    dve.tensor_tensor(xdt[c][:, :, j * HC:(j + 1) * HC, :],
                                      R_ps[1 - j][:, :, :].rearrange("p t (h d) -> p t h d", h=HC),
                                      dt[c][:, :, j * HC:(j + 1) * HC].unsqueeze(3)
                                      .to_broadcast([P, GT, HC, HD]), ALU.mult).then_inc(s_xdt, 1)

                def atanh(n):
                    if n == 0:
                        passed(dve, s_du, s - 2)
                    else:
                        within(dve, s_dtc, s - 2, DTC, 2 + n)
                    if n == 0:
                        op = dve.tensor_scalar(dd[:, :, :], du[:, :, :], 2.0, None, ALU.add)
                    elif n == 1:
                        op = dve.reciprocal(dq[:, :, :], dd[:, :, :])
                    elif n == 2:
                        op = dve.tensor_tensor(dz[:, :, :], du[:, :, :], dq[:, :, :], ALU.mult)
                    elif n == 3:
                        op = dve.tensor_tensor(dz2[:, :, :], dz[:, :, :], dz[:, :, :], ALU.mult)
                    elif n == 4:
                        op = dve.tensor_scalar(dp[:, :, :], dz2[:, :, :], 1.0 / 13, None, ALU.mult)
                    else:
                        src, dst = (dp, dp2) if n % 2 else (dp2, dp)
                        op = dve.scalar_tensor_tensor(out=dst[:, :, :], in0=src[:, :, :], scalar=1.0 / (21 - 2 * n),
                                                      in1=dz2[:, :, :], op0=ALU.add, op1=ALU.mult)
                    op.then_inc(s_dtc, 1)

                if live(5):
                    passed(dve, s_Y, s - 5)
                    passed(dve, s_y2, s - 6, C)
                    for j in range(C):
                        dve.scalar_tensor_tensor(out=y1[j][:, :, :], in0=xs[j][c][:, :, :], scalar=dcol[:, j:j + 1],
                                                 in1=Y_ps[j][:, :, :], op0=ALU.mult, op1=ALU.add).then_inc(s_y1, 1)
                if live(4):
                    passed(dve, s_gm, s - 4)
                    passed(dve, s_ls, s - 4, GT)
                    dve.tensor_tensor(ls[b][:, :, :, :], ls[b][:, :, :, :],
                                      gm[b][:, :, :].unsqueeze(2).to_broadcast([P, GT, H, P]),
                                      ALU.mult).then_inc(s_m, 1)
                if live(2):
                    taps(1)
                if live(3):
                    passed(dve, s_G, s - 3)
                    passed(dve, s_m, s - 5)
                    dve.tensor_tensor(gm[c][:, :, :], R_ps[0][:, :, :],
                                      upto[:, :].unsqueeze(1).to_broadcast([P, GT, P]), ALU.mult).then_inc(s_gm, 1)
                if live(3):
                    passed(dve, s_Y, s - 5)
                    times_dt(0)
                if live(2):
                    taps(2)
                if live(3):
                    for j in range(1, C):
                        times_dt(j)
                if live(2):
                    taps(3, 0, 2)
                if live(5):
                    passed(dve, s_SS, s - 5)
                    if live(2):
                        passed(dve, s_dt, s - 2)
                    passed(dve, s_rr, s - 6)
                    dve.tensor_scalar(vs[:, :], ss_ps, 1.0 / DI, EPS, ALU.mult, ALU.add).then_inc(s_vs, 1)
                if live(2):
                    passed(dve, s_dt, s - 2)
                    dve.tensor_tensor(dr[:, :, :], dt_ps, dtb[:, :].unsqueeze(1).to_broadcast([P, GT, H]),
                                      ALU.add).then_inc(s_dtc, 1)
                    within(dve, s_dtc, s - 2, DTC, 1)
                    dve.scalar_tensor_tensor(out=dn[:, :, :], in0=dr[:, :, :], scalar=-1.0, in1=dr[:, :, :],
                                             op0=ALU.mult, op1=ALU.min).then_inc(s_dn, 1)
                    dve.tensor_scalar(dm[:, :, :], dr[:, :, :], 0.0, None, ALU.max).then_inc(s_dtc, 1)
                if live(2):
                    taps(3, 2, C + 1)
                if live(0):
                    dve.wait_ge(s_x[b], pair(s, b))
                    passed(dve, s_mv, s - 1, GT)
                    norm_halves(dve, xt[b], st, s_st)
                for t in range(GT):
                    if live(2):
                        atanh(t)
                    if live(0):
                        norm_both(dve, t, st, mv[b], tick, s, s_st, s_mv)
                if live(2):
                    atanh(4)
                    atanh(5)
                if live(5):
                    passed(dve, s_rr, s - 5)
                    passed(dve, s_O, s - 5)
                    passed(dve, s_xb, s - 5)
                    if not (isinstance(s, int) and s < 7):
                        dve.wait_ge(s_out[c], pair(s - 7, c))
                for t in range(GT):
                    if live(5):
                        dve.scalar_tensor_tensor(out=xo[c][:, t, :], in0=T_ps[:, t, :], scalar=rr[:, t:t + 1],
                                                 in1=xb[c][:, t, :], op0=ALU.mult, op1=ALU.add).then_inc(s_xo, 1)
                    if live(2):
                        atanh(6 + t)
                if live(2):
                    within(dve, s_dtc, s - 2, DTC, 12)
                    dve.scalar_tensor_tensor(out=dp[:, :, :], in0=dp2[:, :, :], scalar=1.0, in1=dz[:, :, :],
                                             op0=ALU.add, op1=ALU.mult).then_inc(s_dtc, 1)
                    passed(dve, s_dtc, s - 2, DTC)
                    passed(dve, s_xdt, s - 4, C)
                    dve.scalar_tensor_tensor(out=dt[b][:, :, :], in0=dp[:, :, :], scalar=2.0, in1=dm[:, :, :],
                                             op0=ALU.mult, op1=ALU.add).then_inc(s_dtr, 1)
                    passed(dve, s_dtr, s - 2)
                    passed(dve, s_sg, s - 4, 2)
                    dve.tensor_tensor(da[b][:, :, :], dt[b][:, :, :],
                                      nega[:, :].unsqueeze(1).to_broadcast([P, GT, H]), ALU.mult).then_inc(s_da, 1)
                    within(dve, s_da, s - 2, 3, 1)
                    dve.tensor_copy(dap[0][b][:, :, :], da[b][:, :, :]).then_inc(s_da, 1)
                    within(dve, s_da, s - 2, 3, 2)
                    dve.tensor_tensor(dap[1][b][:, :, :], da[b][:, :, :], dap[0][b][:, :, :].bitcast(F32),
                                      ALU.subtract).then_inc(s_da, 1)

            pipeline(dve, G, 5, body)

        @block.tensor
        def _(pe):
            pe.wait_ge(s_w, 16 * N_W)
            pe.wait_ge(s_const, 8)
            for j in range(C):
                mm = pe.transpose(T_ps[:, j, :], wout[:, j, :], ident[:, :])
            mm.then_inc(s_ol, 1)
            pe.wait_ge(s_prep, 3)
            for j in range(C):
                mm = pe.matmul(R_ps[0][:, j, :], woutT[:, j, :], wlin[:, :], start=True, stop=True)
            mm.then_inc(s_ol, 1)
            pe.wait_ge(s_prep, 3 + C)

            def body(s, b, live):
                c = 1 - b

                def turned(j):
                    for t in range(GT):
                        mm = pe.transpose(R_ps[1 - j][:, t, :], xs[j][c][:, t, :], ident[:, :])
                    mm.then_inc(s_xT, 1)

                if live(2):
                    passed(pe, s_hT, s - 2)
                    passed(pe, s_tap, s - 3, NT)
                    for j in range(C + 1):
                        pe.matmul(X_ps[j][:, :, :], win[:, DI + j * P:DI + (j + 1) * P], hT[b][:, :, :],
                                  start=True, stop=True).then_inc(s_X, 1)
                if live(3):
                    passed(pe, s_hT, s - 3)
                    passed(pe, s_y1, s - 5, C)
                    for j in range(C):
                        mm = pe.matmul(Y_ps[j][:, :, :], win[:, j * P:(j + 1) * P], hT[c][:, :, :],
                                       start=True, stop=True)
                    mm.then_inc(s_Z, 1)
                if live(1):
                    passed(pe, s_h, s - 1, GT)
                    passed(pe, s_xo, s - 6, GT)
                    for t in range(GT):
                        mm = pe.transpose(T_ps[:, t, :], h[c][:, t, :], ident[:, :])
                    mm.then_inc(s_T, 1)
                if live(3):
                    passed(pe, s_xs, s - 3, C + 2)
                    passed(pe, s_ls, s - 4, GT)
                    for t in range(GT):
                        mm = pe.matmul(R_ps[0][:, t, :], bs[c][:, t, :], cs[c][:, t, :], start=True, stop=True)
                    mm.then_inc(s_G, 1)
                    turned(0)
                if live(5):
                    passed(pe, s_y2, s - 5, C)
                    if live(1):
                        passed(pe, s_hT, s - 1)
                    for t in range(GT):
                        for j in range(C):
                            mm = pe.matmul(T_ps[:, t, :], y2[j][c][:, t, :], wol[:, j, :],
                                           start=(j == 0), stop=(j == C - 1))
                    mm.then_inc(s_O, 1)
                if live(3):
                    passed(pe, s_gm, s - 3)
                    for j in range(1, C):
                        turned(j)
                if live(5):
                    passed(pe, s_sq, s - 5, C)
                    passed(pe, s_vs, s - 6)
                    if live(3):
                        within(pe, s_xdt, s - 3, C, 1)
                    elif live(4):
                        passed(pe, s_ls, s - 4, GT)
                    for t in range(GT):
                        for j in range(C):
                            mm = pe.matmul(ss_ps[:, t:t + 1], sq[j][:, t, :], ones[:, 0:1],
                                           start=(j == 0), stop=(j == C - 1))
                    mm.then_inc(s_SS, 1)
                if live(2):
                    passed(pe, s_hT, s - 2)
                    passed(pe, s_dn, s - 3)
                    if live(3):
                        within(pe, s_xdt, s - 3, C, 1)
                    for t in range(GT):
                        mm = pe.matmul(dt_ps[:, t, :], hT[b][:, t, :], win[:, DT0:DT0 + H], start=True, stop=True)
                    mm.then_inc(s_dt, 1)
                if live(3):
                    passed(pe, s_sg, s - 3, 2)
                    for t in range(GT):
                        if t == 0:
                            passed(pe, s_xdt, s - 3, C)
                        elif t == 1:
                            if live(2):
                                passed(pe, s_dn, s - 2)
                            if live(5):
                                passed(pe, s_vs, s - 5)
                        else:
                            within(pe, s_ls, s - 3, GT, t - 1)
                        for n in range(2):
                            mm = pe.matmul(R_ps[t % 2][:, :, :], above[:, :], sg[n][c][:, t, :, :],
                                           start=(n == 0), stop=(n == 1))
                        mm.then_inc(s_seg, 1)
                if live(4):
                    passed(pe, s_m, s - 4)
                    passed(pe, s_xdt, s - 4, C)
                    passed(pe, s_y1, s - 5, C)
                    if live(3):
                        passed(pe, s_sz, s - 3, C)
                    for t in range(GT):
                        for k in range(H):
                            mm = pe.matmul(Y_ps[k // HC][k % HC * HD:(k % HC + 1) * HD, t, :], xdt[b][:, t, k, :],
                                           ls[b][:, t, k, :], start=True, stop=True)
                    mm.then_inc(s_Y, 1)

            pipeline(pe, G, 5, body)


_INS = ['x', 'adj', 'L0_gnn_W', 'L0_gnn_a', 'L0_ffn_W1', 'L0_ffn_b1', 'L0_ffn_Wg', 'L0_ffn_bg', 'L0_ffn_Wd', 'L0_ffn_bd',
        'L1_gnn_a0', 'L1_gnn_a1', 'L1_gnn_a2', 'L1_gnn_a3', 'L1_gnn_bias', 'L1_ffn_W_in', 'L1_ffn_conv_w',
        'L1_ffn_conv_b', 'L1_ffn_dt_bias', 'L1_ffn_A_log', 'L1_ffn_D', 'L1_ffn_norm_w', 'L1_ffn_W_out',
        'L1_ffn_W_lin', 'L1_ffn_b_lin']
_OUT = ((64, 128, 128), 'float32')


def build(nc, i, out):
    graphs, n_experts = i['x'].shape[0], i['L0_ffn_bd'].shape[0]

    def scratch(name, shape):
        return nc.dram_tensor(name, list(shape), F32, kind="Internal").ap()

    x1, x3, h_rows = (scratch(n, (graphs * P, D)) for n in ("x1", "x3", "h_rows"))
    by_graph = [v.rearrange("(g p) d -> g p d", p=P) for v in (x1, x3)]
    additive_attention(nc, i['x'], i['adj'], i['L0_gnn_W'], i['L0_gnn_a'], by_graph[0])
    with ExitStack() as outer:
        mw = MambaWeights(nc, outer, *(i[f'L1_ffn_{n}'] for n in ('W_in', 'conv_w', 'conv_b', 'dt_bias', 'A_log', 'D',
                                                                  'norm_w', 'W_out', 'W_lin', 'b_lin')))
        feed_forward_and_attention(nc, i, graphs, n_experts, scratch, by_graph, h_rows, mw)
        mamba_block(nc, by_graph[1], mw, out)


def feed_forward_and_attention(nc, i, graphs, n_experts, scratch, by_graph, h_rows, next_weights):
    with ExitStack() as ctx:
        rt = Routing(nc, ctx, graphs, n_experts, i['L0_ffn_W1'].shape[1] // P)
        y_rows = scratch("y_rows", (rt.tiles * P, D))
        gates(nc, by_graph[0], i['L0_ffn_W1'], i['L0_ffn_b1'], i['L0_ffn_Wg'], i['L0_ffn_bg'], i['L0_ffn_Wd'],
              i['L0_ffn_bd'], rt, h_rows)
        experts(nc, rt, h_rows, y_rows, n_experts, next_weights)
        typed_attention(nc, by_graph[0], rt, y_rows, i['adj'], [i[f'L1_gnn_a{k}'] for k in range(4)],
                        i['L1_gnn_bias'], by_graph[1])


def kernel(**inputs):
    import numpy as _np
    import concourse.bacc as _bacc
    from concourse import mybir as _mybir
    from concourse.bass_utils import run_bass_kernel_spmd as _run

    nc = _bacc.Bacc("TRN2", target_bir_lowering=False, num_devices=1)
    arrays, args = {}, {}
    for name in _INS:
        a = _np.ascontiguousarray(inputs[name])
        arrays[f"in_{name}_dram"] = a
        args[name] = nc.dram_tensor(f"in_{name}_dram", a.shape, _mybir.dt.from_np(a.dtype), kind="ExternalInput").ap()
    shape, dtype = _OUT
    out = nc.dram_tensor("out_0_dram", shape, _mybir.dt.from_np(_np.dtype(dtype)), kind="ExternalOutput").ap()
    build(nc, args, out)
    r = _run(nc, [arrays], core_ids=[0])
    return r.results[0]["out_0_dram"]
```
